# Optimizing a Trainium2 kernel written in Bass

```python
import numpy as np
import jax
import jax.numpy as jnp

def _softmax(x, axis=-1):
    return jax.nn.softmax(x, axis=axis)

def _gelu(x):
    return jax.nn.gelu(x, approximate=True)

def _silu(x):
    return jax.nn.silu(x)

def _sigmoid(x):
    return jax.nn.sigmoid(x)

def _layernorm(x, axis=-1, eps=1e-05):
    m = jnp.mean(x, axis=axis, keepdims=True)
    v = jnp.var(x, axis=axis, keepdims=True)
    return (x - m) / jnp.sqrt(v + eps)

def _scatter_add(tgt, idx, src, axis=0):
    return tgt.at[idx].add(src)

def _segment_sum(src, seg, n):
    return jax.ops.segment_sum(src, seg, n)
kernel_name = 'mk_adaln_ffn_d2_seqx_r8_a4c9dd'

def setup_inputs(seed: int=0):
    np.random.seed(seed)
    _w = jnp.asarray

    def _rec_inputs():
        import jax
        import jax.numpy as jnp
        _rk = jax.random.key(seed)
        x = -0.0003929 + 0.9999 * jax.random.normal(jax.random.fold_in(_rk, 1), (128, 32, 512), jnp.float32)
        _lenS = 32 - jax.random.randint(jax.random.fold_in(_rk, 7), (128,), 0, max(1, 32 // 4) + 1, jnp.int32)
        _lenS2 = 32 - jax.random.randint(jax.random.fold_in(_rk, 8), (128,), 0, max(1, 32 // 4) + 1, jnp.int32)
        itok_B_78_3631 = jax.random.randint(jax.random.fold_in(_rk, 11), (128,), 78, 454, jnp.int32)
        itok_B_3_7 = jax.random.randint(jax.random.fold_in(_rk, 12), (128,), 3, 8, jnp.int32)
        return (x, itok_B_78_3631, itok_B_3_7)
    x, itok_B_78_3631, itok_B_3_7 = _rec_inputs()

    def _L0_cond_setup():
        import math
        import jax, jax.numpy as jnp
        import numpy as np
        B, H, N, L = (16, 32, 64, 512)
        DT_MIN, DT_MAX = (0.001, 0.1)

        def _get_kernel(log_dt, C, log_A_real, A_imag, length):
            dt = jnp.exp(log_dt)
            Cc = C[..., 0] + 1j * C[..., 1]
            A = -jnp.exp(log_A_real) + 1j * A_imag
            dtA = A * dt[:, None]
            Ct = Cc * (jnp.exp(dtA) - 1.0) / A
            P = dtA[:, :, None] * jnp.arange(length, dtype=jnp.float32)
            K = 2.0 * jnp.einsum('hn,hnl->hl', Ct, jnp.exp(P)).real
            return K
        key = jax.random.key(seed)
        ks = jax.random.split(key, 5)
        u = jax.random.normal(ks[0], (B, H, L), dtype=jnp.float32)
        log_dt = jax.random.uniform(ks[1], (H,), dtype=jnp.float32) * (math.log(DT_MAX) - math.log(DT_MIN)) + math.log(DT_MIN)
        C = jax.random.normal(ks[2], (H, N, 2), dtype=jnp.float32)
        log_A_real = jnp.log(0.5 * jnp.ones((H, N), dtype=jnp.float32))
        A_imag = math.pi * jnp.broadcast_to(jnp.arange(N, dtype=jnp.float32), (H, N))
        D = jax.random.normal(ks[3], (H,), dtype=jnp.float32)
        length = jax.random.randint(ks[4], (B,), 1, L + 1, dtype=jnp.int32)
        return {'u': u, 'log_dt': log_dt, 'C': C, 'log_A_real': log_A_real, 'A_imag': A_imag, 'D': D, 'length': length}
    _L0_cond_all = _L0_cond_setup()
    _L0_cond_in = {k: v for k, v in _L0_cond_all.items() if k in ('log_dt', 'C', 'log_A_real', 'A_imag', 'D')}
    del _L0_cond_all

    def _L0_ffn_setup():
        import jax, jax.numpy as jnp
        import numpy as np
        TOP_K = 2
        SCALING = 32.0 / 64.0
        key = jax.random.key(seed)
        ks = jax.random.split(key, 6)
        Bsz, S, Din, Dout, R, E = (4, 256, 512, 512, 64, 16)
        x = jax.random.normal(ks[0], (Bsz, S, Din), dtype=jnp.float32)
        base_w = jax.random.normal(ks[1], (Dout, Din), dtype=jnp.float32) * 0.02
        base_b = jax.random.normal(ks[2], (Dout,), dtype=jnp.float32) * 0.02
        A = jax.random.normal(ks[3], (R, Din), dtype=jnp.float32) * (1.0 / np.sqrt(Din))
        B = jax.random.normal(ks[4], (E, Dout, R), dtype=jnp.float32) * 0.02
        router_w = jax.random.normal(ks[5], (E, Din), dtype=jnp.float32) * 0.02
        return {'x': x, 'base_w': base_w, 'base_b': base_b, 'A': A, 'B': B, 'router_w': router_w}
    _L0_ffn_all = _L0_ffn_setup()
    _L0_ffn_in = {k: v for k, v in _L0_ffn_all.items() if k in ('base_w', 'base_b', 'A', 'B', 'router_w')}
    del _L0_ffn_all

    def _L1_cond_setup():
        import jax, jax.numpy as jnp
        import numpy as np
        MAX_LORAS, OUT, IN = (8, 512, 512)
        B, S = (4, 256)
        key = jax.random.key(seed)
        k1, k2, k3 = jax.random.split(key, 3)
        x = jax.random.normal(k1, (B, S, IN), dtype=jnp.float32)
        weight = jax.random.normal(k2, (MAX_LORAS, OUT, IN), dtype=jnp.float32) * 0.02
        adapter_ids = jax.random.randint(k3, (B,), 0, MAX_LORAS, dtype=jnp.int32)
        return {'x': x, 'weight': weight, 'adapter_ids': adapter_ids}
    _L1_cond_all = _L1_cond_setup()
    _L1_cond_in = {k: v for k, v in _L1_cond_all.items() if k in ('weight',)}
    del _L1_cond_all

    def _L1_ffn_setup():
        import jax, jax.numpy as jnp
        import numpy as np
        IN_F = 512
        OUT_F = 512
        N_CLUSTERS = 64
        THRESHOLD = 0.01
        TEMPERATURE = 0.1
        BATCH, SEQ = (4, 256)
        key = jax.random.key(seed)
        k1, k2, k3, k4, k5 = jax.random.split(key, 5)
        s = 1.0 / np.sqrt(IN_F)
        return {'input': jax.random.normal(k1, (BATCH, SEQ, IN_F), dtype=jnp.float32), 'weight': jax.random.normal(k2, (OUT_F, IN_F), dtype=jnp.float32) * s, 'bias': jax.random.uniform(k3, (OUT_F,), dtype=jnp.float32, minval=-s, maxval=s), 'centroids': jax.random.normal(k4, (N_CLUSTERS, IN_F), dtype=jnp.float32) * s, 'assignments': jax.random.randint(k5, (OUT_F,), 0, N_CLUSTERS, dtype=jnp.int32)}
    _L1_ffn_all = _L1_ffn_setup()
    _L1_ffn_in = {k: v for k, v in _L1_ffn_all.items() if k in ('weight', 'bias', 'centroids', 'assignments')}
    del _L1_ffn_all
    return {'x': x, 'itok_B_78_3631': itok_B_78_3631, 'itok_B_3_7': itok_B_3_7, 'L0_cond_log_dt': _L0_cond_in['log_dt'], 'L0_cond_C': _L0_cond_in['C'], 'L0_cond_log_A_real': _L0_cond_in['log_A_real'], 'L0_cond_A_imag': _L0_cond_in['A_imag'], 'L0_cond_D': _L0_cond_in['D'], 'L0_ffn_base_w': _L0_ffn_in['base_w'], 'L0_ffn_base_b': _L0_ffn_in['base_b'], 'L0_ffn_A': _L0_ffn_in['A'], 'L0_ffn_B': _L0_ffn_in['B'], 'L0_ffn_router_w': _L0_ffn_in['router_w'], 'L1_cond_weight': _L1_cond_in['weight'], 'L1_ffn_weight': _L1_ffn_in['weight'], 'L1_ffn_bias': _L1_ffn_in['bias'], 'L1_ffn_centroids': _L1_ffn_in['centroids'], 'L1_ffn_assignments': _L1_ffn_in['assignments']}

def reference(x, itok_B_78_3631, itok_B_3_7, L0_cond_log_dt, L0_cond_C, L0_cond_log_A_real, L0_cond_A_imag, L0_cond_D, L0_ffn_base_w, L0_ffn_base_b, L0_ffn_A, L0_ffn_B, L0_ffn_router_w, L1_cond_weight, L1_ffn_weight, L1_ffn_bias, L1_ffn_centroids, L1_ffn_assignments):
    import jax
    import jax.numpy as jnp

    def _L0_cond_ref(u, log_dt, C, log_A_real, A_imag, D, length):
        import math
        import jax, jax.numpy as jnp
        import numpy as np
        B, H, N, L = (16, 32, 64, 512)
        DT_MIN, DT_MAX = (0.001, 0.1)

        def _get_kernel(log_dt, C, log_A_real, A_imag, length):
            dt = jnp.exp(log_dt)
            Cc = C[..., 0] + 1j * C[..., 1]
            A = -jnp.exp(log_A_real) + 1j * A_imag
            dtA = A * dt[:, None]
            Ct = Cc * (jnp.exp(dtA) - 1.0) / A
            P = dtA[:, :, None] * jnp.arange(length, dtype=jnp.float32)
            K = 2.0 * jnp.einsum('hn,hnl->hl', Ct, jnp.exp(P)).real
            return K
        Bq, Hq, Lq = u.shape
        K = _get_kernel(log_dt, C, log_A_real, A_imag, Lq)
        n = 2 * Lq
        kf = jnp.fft.rfft(K, n=n)
        uf = jnp.fft.rfft(u, n=n)
        y = jnp.fft.irfft(uf * kf[None], n=n)[..., :Lq]
        y = y + u * D[:, None]
        mask = (jnp.arange(Lq)[None, :] < length[:, None]).astype(u.dtype)
        return y * mask[:, None, :]

    def _L0_ffn_ref(x, base_w, base_b, A, B, router_w):
        import jax, jax.numpy as jnp
        import numpy as np
        TOP_K = 2
        SCALING = 32.0 / 64.0
        base_out = jnp.einsum('bsi,oi->bso', x, base_w) + base_b
        res_hidden = jnp.einsum('bsi,ri->bsr', x, A)
        logits = jnp.einsum('bsi,ei->bse', x, router_w)
        probs = jax.nn.softmax(logits, axis=-1)
        topw, topi = jax.lax.top_k(probs, TOP_K)
        topw = topw / (jnp.sum(topw, axis=-1, keepdims=True) + 1e-06)
        num_experts = B.shape[0]
        combine = jnp.sum(jax.nn.one_hot(topi, num_experts, dtype=x.dtype) * topw[..., None], axis=-2)
        delta = jnp.einsum('bse,bsr,eor->bso', combine, res_hidden, B)
        return base_out + delta * SCALING

    def _L1_cond_ref(x, weight, adapter_ids):
        import jax, jax.numpy as jnp
        import numpy as np
        MAX_LORAS, OUT, IN = (8, 512, 512)
        B, S = (4, 256)
        w = weight[adapter_ids]
        return jnp.einsum('bsi,boi->bso', x, w)

    def _L1_ffn_ref(input, weight, bias, centroids, assignments):
        import jax, jax.numpy as jnp
        import numpy as np
        IN_F = 512
        OUT_F = 512
        N_CLUSTERS = 64
        THRESHOLD = 0.01
        TEMPERATURE = 0.1
        BATCH, SEQ = (4, 256)
        shape = input.shape
        x = input.reshape(-1, shape[-1])
        dots = jax.nn.softmax(x @ centroids.T / TEMPERATURE, axis=-1)
        hits = dots > THRESHOLD
        query_sel = jnp.any(hits, axis=1)
        cluster_sel = jnp.any(hits, axis=0)
        row_sel = cluster_sel[assignments]
        dense = x @ weight.T + bias
        out = jnp.where(query_sel[:, None] & row_sel[None, :], dense, jnp.zeros((), dense.dtype))
        return out.reshape(*shape[:-1], -1)
    x = x + _L0_ffn_ref(_L0_cond_ref(x, L0_cond_log_dt, L0_cond_C, L0_cond_log_A_real, L0_cond_A_imag, L0_cond_D, itok_B_78_3631), L0_ffn_base_w, L0_ffn_base_b, L0_ffn_A, L0_ffn_B, L0_ffn_router_w)
    x = x + _L1_ffn_ref(_L1_cond_ref(x, L1_cond_weight, itok_B_3_7), L1_ffn_weight, L1_ffn_bias, L1_ffn_centroids, L1_ffn_assignments)
    return x

_drawn_inputs = setup_inputs


def setup_inputs(seed=0):
    import zlib

    import numpy as np

    out = dict(_drawn_inputs(seed))
    spreads = {'L0_cond_log_A_real': (-0.6931471824645996, 0.594)}
    factors = {'L0_ffn_base_b': 3.262, 'L1_ffn_bias': 2.863}
    for name, (base, spread) in spreads.items():
        noise = np.random.default_rng([zlib.crc32(name.encode()), seed]).standard_normal(out[name].shape)
        drawn = base * np.exp(spread * noise) if base else spread * noise
        out[name] = jnp.asarray(drawn.astype(out[name].dtype))
    for name, factor in factors.items():
        out[name] = (out[name] * factor).astype(out[name].dtype)
    return out
```

```python
import math
from contextlib import ExitStack

import concourse.bass as bass
from concourse import mybir

P = 128
B, H, L = 128, 32, 512
LB = L // P
NM = 64
E, R = 16, 64
NP = E * R // P
AR = R + E
IDS = 8
C = 64
GH = 4
NG = H // GH
TB = 4
NT = (B + IDS * (TB - 1)) // TB
TD = 8
NTD = -(-NT // TD) * TD
RB = 4
FA, FB = 16, 32
KPITCH = L + P
SCALING = 0.5
MAGIC = 1.5 * 2.0 ** 23
TURN = 6.283185
ROUTE = 24
DOTS = 9
NWT = LB + 1 + NP

F32 = mybir.dt.float32
F32R = mybir.dt.float32r
I32 = mybir.dt.int32
U32 = mybir.dt.uint32
ALU = mybir.AluOpType
ACT = mybir.ActivationFunctionType
AX = mybir.AxisListType.X


def build(nc, x, lengths, adapter_ids, log_dt, ssm_c, log_a_real, a_imag, ssm_d, base_w, base_b,
          lora_a, lora_b, router_w, cond_w, ffn_w, ffn_bias, centroids, assignments, out):
    ctx = ExitStack()

    def sem(name):
        return ctx.enter_context(nc.semaphore(name))

    def alloc(stack, name, shape, dt=F32):
        return stack.enter_context(nc.sbuf_tensor(name, shape, dt))

    k_dram = nc.dram_tensor("k_rev", (2, H, KPITCH), F32, kind="Internal").ap()
    x1_dram = nc.dram_tensor("x1_scratch", (B, H, L), F32, kind="Internal").ap()

    with ctx:
        ident = alloc(ctx, "ident", [P, P])
        tile_id = alloc(ctx, "tile_adapter", [1, NTD], I32)
        slot_b = alloc(ctx, "slot_batch", [1, TB, NTD], I32)
        slot_ok = alloc(ctx, "slot_filled", [P, NTD])
        slot_row = alloc(ctx, "slot_out_row", [P, NTD], U32)
        w_id = [alloc(ctx, f"cond_w_{n}", [P, LB, L]) for n in range(2)]
        f_raw = w_id[0]
        cent_raw = alloc(ctx, "centroids_raw", [C, L])

        l0 = ExitStack()
        bw = [alloc(l0, f"lora_b_{n}", [P, NP, L], F32R) for n in ("hi", "lo")]
        w0 = [alloc(l0, f"base_w_{n}", [P, LB, L], F32R) for n in ("hi", "lo")]
        arw = [alloc(l0, f"a_router_{n}", [P, LB, AR], F32R) for n in ("hi", "lo")]
        xg = [alloc(l0, f"x_group_{n}", [P, GH, L]) for n in range(2)]
        sk = [alloc(l0, f"hankel_{n}", [P, 2, L], F32R) for n in range(2)]
        uT = [[alloc(l0, f"uT_{m}_{n}", [P, LB, B], F32R) for m in ("hi", "lo")] for n in range(2)]
        y32 = [alloc(l0, f"y_masked_{n}", [P, LB, B]) for n in range(2)]
        yT = [alloc(l0, f"yT_{n}", [P, LB, GH, B], F32R) for n in ("hi", "lo")]
        mask = alloc(l0, "length_mask", [P, LB, B])
        b0_bc = alloc(l0, "base_b_bc", [P, L])
        sel = alloc(l0, "expert_selection", [2 * E, NP, P], F32R)
        res = alloc(l0, "res_hidden", [P, GH * B])
        lgT = alloc(l0, "logitsT", [E, GH * B])
        cst = alloc(l0, "combine_split", [P, GH, 2 * E])
        cTs = alloc(l0, "combineT", [2 * E, GH * B], F32R)
        g32 = [alloc(l0, f"gated_{n}", [P, GH * B]) for n in range(2)]
        gT = [[alloc(l0, f"gatedT_{m}_{n}", [P, GH * B], F32R) for m in ("hi", "lo")] for n in range(2)]
        iota_e = alloc(l0, "expert_marks", [P, E])
        rmax = alloc(l0, "r_max", [P, GH])
        rex = alloc(l0, "r_exp", [P, GH, E])
        rsum = alloc(l0, "r_sum", [P, GH])
        rinv = alloc(l0, "r_inv", [P, GH])
        rprob = alloc(l0, "r_prob", [P, GH, E])
        rtop = alloc(l0, "r_top", [P, 2, GH])
        rmark = alloc(l0, "r_mark", [P, GH])
        rden = alloc(l0, "r_den", [P, GH])
        rw = alloc(l0, "r_weight", [P, 2, GH])
        roh = alloc(l0, "r_onehot", [P, GH, 2, E])
        rcomb = alloc(l0, "r_combine", [P, GH, E])
        w_raw = w_id[0]
        w_rev = w_id[1]
        flat = alloc(l0, "setup", [P, 12 * 1024])
        spaces, off = [flat[:, :]], [0]

        def carve(cols, parts=P):
            if off[0] + cols > spaces[0].shape[1]:
                spaces.pop(0)
                off[0] = 0
            off[0] += cols
            return spaces[0][0:parts, off[0] - cols:off[0]]

        ar_raw = carve(L, AR)
        ar_rev = carve(L, AR)
        b_raw = carve(4 * E * R).rearrange("p (a e r) -> p a e r", a=4, e=E)
        modes = carve(4 * P, H).rearrange("p (q n) -> p q n", q=4)
        c_raw = carve(2 * NM, H).rearrange("p (n c) -> p n c", c=2)
        par = carve(4 * H).rearrange("p (q h) -> p q h", q=4)
        dt_bc = carve(H)
        small = carve(32 * H).rearrange("p (q h) -> p q h", q=32)
        phase_off = carve(2)
        bval = carve(FB)
        aval = carve(FA)
        v_ph = carve(H * FB).rearrange("p (h b) -> p h b", h=H)
        tmp = carve(H * FB)
        sel32 = tmp[0:2 * E, :].rearrange("p (j q) -> p j q", j=NP)
        a_tmp = tmp.rearrange("p (q h b) -> p q h b", q=2, h=H)
        v_tmp = tmp.rearrange("p (h b) -> p h b", h=H)
        k32 = tmp[0:FA, :].rearrange("p (h b) -> p h b", h=H)
        v_mag = carve(H * FB).rearrange("p (h b) -> p h b", h=H)
        a_ph = carve(2 * H * FA).rearrange("p (q h b) -> p q h b", q=2, h=H)
        a_mag = carve(H * FA).rearrange("p (h b) -> p h b", h=H)
        d_add = carve(H, FA)
        k_zero = carve(P, H)
        len_i = carve(B).bitcast(I32)
        len_f = carve(B)
        pos = carve(LB)
        spaces += [t[:, :] for t in (res, *g32)] + [t[:, :, :].rearrange("p k b -> p (k b)") for t in y32]
        quad = carve(TB * P).rearrange("p (q r h) -> p q r h", q=TB, r=TB)
        ids_ri = carve(B).bitcast(I32)
        ids_ci = carve(1).bitcast(I32)
        ids_r = carve(B)
        ids_c = carve(2)
        low = carve(B)
        one_s = carve(P)
        same = carve(B)
        rank = carve(2)
        iota8 = carve(IDS)
        oh8 = carve(IDS)
        tri8 = carve(IDS * IDS).rearrange("p (e f) -> p e f", e=IDS)
        prod88 = carve(IDS * IDS).rearrange("p (e f) -> p e f", e=IDS)
        n_tiles = carve(IDS)
        n_tiles_i = carve(IDS).bitcast(I32)
        first_tile = carve(IDS)
        place = carve(4)
        slot_v = carve(TB * NTD).rearrange("p (q t) -> p q t", q=TB)
        match = carve(TB * NTD).rearrange("p (q t) -> p q t", q=TB)
        b_col = carve(2)
        h_less = carve(1)
        pad_add = carve(1)
        row_f = carve(NTD)
        row_pad = carve(NTD)
        l0.close()

        l1 = ExitStack()
        mw = [alloc(l1, f"merged_w_{n}", [P, IDS, LB, L], F32R) for n in ("hi", "lo")]
        mc = alloc(l1, "merged_c", [P, IDS, LB, C])
        l1b = ExitStack()
        w_sp = [[alloc(l1b, f"cond_w_{m}_{n}", [P, LB, L], F32R) for m in ("hi", "lo")] for n in range(2)]
        f_w = [alloc(l1b, f"ffn_wT_{n}", [P, LB, L], F32R) for n in ("hi", "lo")]
        f_c = [alloc(l1b, f"centroidsT_{n}", [P, LB, C], F32R) for n in ("hi", "lo")]
        l1b.close()
        rows = [w_id[0][:, n, :] for n in range(RB)]
        outt = [w_id[1][:, n, :] for n in range(RB)]
        xtf = [alloc(l1, f"x1T_{n}", [P, LB, P]) for n in range(2)]
        xts = [[alloc(l1, f"x1T_{m}_{n}", [P, LB, P], F32R) for m in ("hi", "lo")] for n in range(2)]
        dshift = alloc(l1, "dots_shifted", [P, TD, C])
        dexp = alloc(l1, "dots_exp", [P, TD, C])
        hits = alloc(l1, "hits", [P, TD, C])
        row_now = [alloc(l1, f"out_row_of_tile_{n}", [P, 1], U32) for n in range(RB)]
        hitmax = alloc(l1, "hit_any", [P, C])
        hit8 = alloc(l1, "hit_any_of_eight", [P, C])
        dmax = alloc(l1, "dots_max", [P, TD])
        dsum = alloc(l1, "dots_sum", [P, TD])
        dinv = alloc(l1, "dots_inv", [P, TD])
        query = alloc(l1, "query_sel", [P, NTD])
        csel = alloc(l1, "cluster_sel", [C, P])
        onehot = alloc(l1, "assign_onehot", [C, L])
        assign_i = alloc(l1, "assign_i", [C, L], I32)
        assign_f = alloc(l1, "assign_f", [C, L])
        cidx = alloc(l1, "cluster_index", [C, 1])
        ones = alloc(l1, "ones", [P, P])
        rowsel = alloc(l1, "row_sel", [P, L])
        b1_bc = alloc(l1, "ffn_bias_bc", [P, L])
        dense = [alloc(l1, f"dense_{n}", [P, L]) for n in range(2)]
        dsel = [alloc(l1, f"dense_sel_{n}", [P, L]) for n in range(RB)]
        l1.close()

        k_split = [yT[n][0:FA, :, :, :].rearrange("a k i b -> a (k i b)")[:, 0:H * FB]
                   .rearrange("a (h b) -> a h b", h=H) for n in range(2)]

        def bank(name):
            return ctx.enter_context(nc.psum_tensor(name, [P, 512], F32))

        acc = [bank(f"acc{i}") for i in range(GH)]
        wb = [bank(f"work{i}") for i in range(2)]
        bb = [bank(f"bcast{i}") for i in range(2)]

        s_par = sem("params_loaded")
        s_w0l = sem("base_w_loaded")
        s_arl = sem("a_router_loaded")
        s_bl = sem("lora_b_loaded")
        s_cst = sem("pool_constants_ready")
        s_id = sem("ident_ready")
        s_pool = sem("pool_chain")
        s_dve = sem("dve_setup_chain")
        s_rt = sem("dve_routing_chain")
        s_dn = sem("dve_layer1_chain")
        s_stk = sem("mode_stack_ready")
        s_kps_par = sem("params_in_psum")
        s_parT = sem("params_transposed")
        s_sort = sem("sort_inputs_ready")
        t_cnt = sem("adapter_counts_in_psum")
        t_mat = sem("slots_matched")
        t_tab = sem("slot_tables_in_psum")
        t_rdy = sem("slot_tables_ready")
        s_dt = sem("dt_and_decay_ready")
        s_t0 = sem("turns_ready")
        s_mag = sem("decay_exponents_ready")
        s_mags = sem("decays_ready")
        s_fr = sem("phases_ready")
        s_sin = sem("sines_ready")
        s_uv = sem("mode_factors_ready")
        s_kps = sem("kernels_in_psum")
        s_khi = sem("kernels_hi")
        s_klo = sem("kernels_lo")
        s_kst = sem("kernels_stored")
        s_rev = sem("weights_reversed")
        s_wps = sem("weights_in_psum")
        s_whi = sem("weights_hi")
        s_wlo = sem("weights_lo")
        s_x = [[sem(f"x_loaded_{n}_{i}") for i in range(GH)] for n in range(2)]
        s_sk = [sem(f"hankel_loaded_{n}") for n in range(2)]
        u_ps = sem("u_in_psum")
        u_hi = sem("u_hi")
        u_lo = sem("u_lo")
        y_ps = sem("y_in_psum")
        y_ms = sem("y_masked")
        y_hi = sem("y_hi")
        y_lo = sem("y_lo")
        ar_ps = sem("ar_in_psum")
        ar_ev = sem("ar_evacuated")
        lt_ps = sem("logits_in_psum")
        r_sub = sem("logits_shifted")
        r_exp = sem("logits_exp")
        c_rdy = sem("combine_ready")
        ct_ps = sem("combineT_in_psum")
        ct_sb = sem("combineT_ready")
        bc_ps = sem("gates_in_psum")
        g_mul = sem("gated_ready")
        g_hi = sem("gated_hi")
        g_lo = sem("gated_lo")
        d_done = sem("experts_added")
        b_done = sem("base_added")
        a_done = sem("head_accumulated")
        xb_rdy = sem("x_plus_bias")
        x1_rdy = sem("x1_ready")
        x1_st = [sem(f"x1_stored_{n}") for n in range(2)]
        s_fwl = sem("ffn_w_loaded")
        s_cwl = [sem(f"cond_w_loaded_{n}") for n in range(2)]
        cw_hi = sem("cond_w_hi")
        cw_lo = sem("cond_w_lo")
        m_ps = sem("merged_in_psum")
        m_hi = sem("merged_hi")
        m_lo = sem("merged_lo")
        mc_ps = sem("merged_c_in_psum")
        mc_ev = sem("merged_c_ready")
        s_l1l = sem("layer1_rows_loaded")
        s_l1c = sem("layer1_consts")
        s_rd = [sem(f"dots_rows_loaded_{n}") for n in range(RB)]
        xd_ps = sem("dots_x1T_in_psum")
        xd_ev = sem("dots_x1T_ready")
        dm_ps = sem("dots_in_psum")
        dt_sh = sem("dots_shifted_ready")
        dt_exp = sem("dots_exp_ready")
        cnt_ps = sem("hit_counts_in_psum")
        cs_rdy = sem("cluster_sel_ready")
        rs_ps = sem("row_sel_in_psum")
        s_rl = [sem(f"rows_loaded_{n}") for n in range(RB)]
        xe_ps = sem("x1T_in_psum")
        xe_hi = sem("x1T_hi")
        xe_lo = sem("x1T_lo")
        ft_ps = sem("dense_in_psum")
        ft_ev = sem("dense_evacuated")
        ft_sel = sem("dense_selected")
        o_rdy = sem("out_tile_ready")
        row_rdy = sem("out_rows_of_tile_ready")
        s_out = [sem(f"out_stored_{n}") for n in range(RB)]

        block = ctx.enter_context(nc.Block())

        def weight_out(k, part):
            if k < LB:
                return w0[part][:, k, :]
            if k == LB:
                return arw[part][:, :, :]
            if k < NWT:
                return bw[part][:, k - LB - 1, :]
            if k < NWT + LB:
                return f_w[part][:, k - NWT, :]
            return f_c[part][:, :, :]

        def weight_in_psum(k, cols):
            src = acc[k % GH][:, 0:cols]
            return src.rearrange("p (k c) -> p k c", k=LB) if k in (LB, NWT + LB) else src

        class Chain:

            def __init__(self, eng, s, base=0):
                self.eng, self.s, self.base, self.n = eng, s, base, 0
                self.others = {}

            def after(self, ins, other=None):
                if other is not None:
                    self.others[other.name] = self.others.get(other.name, 0) + 1
                    ins.then_inc(other, 1)
                    self.eng.wait_ge(other, self.others[other.name])
                    return
                self.n += 1
                ins.then_inc(self.s, 1)
                self.eng.wait_ge(self.s, self.base + self.n)

        def load_x(sp, n, i, g):
            sp.dma_start(xg[n][:, i, :], x[:, bass.ds(GH * g + i, 1), :].rearrange("b h l -> b (h l)")
                         ).then_inc(s_x[n][i], 16)

        hankel = bass.AP(k_dram.tensor, 0, [[1, P], [H * KPITCH, 2], [KPITCH, H], [1, L]])

        def load_hankel(sp, g, i):
            sp.dma_start(sk[i % 2][:, :, :].bitcast(F32), hankel[:, :, bass.ds(GH * g + i, 1), :].rearrange("p s h l -> p s (h l)")
                         ).then_inc(s_sk[i % 2], 16)

        @block.sync
        def _(sp):
            sp.dma_start(modes[:, 0, 0:NM], log_a_real).then_inc(s_par, 16)
            sp.dma_start(modes[:, 0, NM:P], log_a_real).then_inc(s_par, 16)
            sp.dma_start(modes[:, 1, 0:NM], a_imag).then_inc(s_par, 16)
            sp.dma_start(modes[:, 1, NM:P], a_imag).then_inc(s_par, 16)
            sp.dma_start(c_raw, ssm_c).then_inc(s_par, 16)
            sp.dma_start(dt_bc, bass.AP(log_dt.tensor, 0, [[0, P], [1, H]])).then_inc(s_par, 16)
            sp.dma_start(len_i, bass.AP(lengths.tensor, 0, [[0, P], [1, B]])).then_inc(s_par, 16)
            sp.dma_start(ids_ri, bass.AP(adapter_ids.tensor, 0, [[0, P], [1, B]])).then_inc(s_par, 16)
            sp.dma_start(ids_ci, adapter_ids.rearrange("(b a) -> b a", a=1)).then_inc(s_par, 16)
            sp.dma_start(b0_bc[:, :], bass.AP(base_b.tensor, 0, [[0, P], [1, L]])).then_inc(s_par, 16)
            sp.wait_ge(s_cst, 1)
            sp.dma_start(d_add[FA - 1:FA, :], ssm_d.rearrange("(a h) -> a h", a=1)).then_inc(s_par, 16)
            sp.dma_start(w_raw[:, :, :], base_w.rearrange("(a p) l -> p a l", p=P)).then_inc(s_w0l, 16)
            sp.dma_start(ar_raw[0:R, :], lora_a).then_inc(s_arl, 16)
            sp.dma_start(ar_raw[R:AR, :], router_w).then_inc(s_arl, 16)
            for i in range(GH):
                load_x(sp, 0, i, 0)
            for a in range(4):
                sp.dma_start(b_raw[:, a, :, :], lora_b[:, P * a:P * a + P, :].rearrange("e p r -> p e r")
                             ).then_inc(s_bl, 16)
            for i in range(GH):
                load_x(sp, 1, i, 1)
            sp.wait_ge(s_klo, 1)
            for n in range(2):
                dst = bass.AP(k_dram.tensor, n * H * KPITCH, [[FB, FA], [KPITCH, H], [1, FB]])
                sp.dma_start(dst, k_split[n].bitcast(F32)).then_inc(s_kst, 16)
                dst0 = bass.AP(k_dram.tensor, n * H * KPITCH + L, [[KPITCH, H], [1, P]])
                sp.dma_start(dst0, k_zero).then_inc(s_kst, 16)
            sp.wait_ge(s_kst, 64)
            for i in range(GH):
                if i >= 2:
                    sp.wait_ge(y_ps, i - 1)
                load_hankel(sp, 0, i)

            cw = cond_w.rearrange("e (a p) k -> e p a k", p=P)
            sp.wait_ge(s_rev, 4)
            sp.wait_ge(s_wps, LB)
            sp.dma_start(f_raw[:, :, :], ffn_w.rearrange("(a p) o -> p a o", p=P)).then_inc(s_fwl, 16)
            sp.dma_start(cent_raw[:, :], centroids).then_inc(s_fwl, 16)
            sp.dma_start(w_id[1][:, :, :], cw[1, :, :, :]).then_inc(s_cwl[1], 16)

            def group(g, n, last):
                if not last:
                    for i in range(GH):
                        sp.wait_ge(y_ps, GH * g + GH + i - 1)
                        load_hankel(sp, g + 1, i)
                for i in range(GH):
                    sp.wait_ge(x1_rdy, GH * g + i + GH + 1)
                    sp.dma_start(x1_dram[:, bass.ds(GH * g + i, 1), :].rearrange("b h l -> b (h l)"),
                                 xg[n][:, i, :]).then_inc(x1_st[n], 16)

            with sp.Fori(0, NG // 2 - 1) as t:
                for n in range(2):
                    group(2 * t + n, n, False)
                    sp.wait_ge(x1_st[n], 64 * t + 64)
                    for i in range(GH):
                        load_x(sp, n, i, 2 * t + n + 2)
            group(NG - 2, 0, False)
            group(NG - 1, 1, True)
            sp.wait_ge(s_wps, NWT + LB)
            sp.dma_start(w_id[0][:, :, :], cw[0, :, :, :]).then_inc(s_cwl[0], 16)
            with sp.Fori(1, IDS // 2) as t:
                for n in range(2):
                    sp.wait_ge(cw_lo, 2 * t + n - 1)
                    sp.dma_start(w_id[n][:, :, :],
                                 cw[bass.ds(2 * t + n, 1), :, :, :].rearrange("e p a k -> p (e a) k")
                                 ).then_inc(s_cwl[n], 16)
            sp.wait_ge(mc_ps, IDS)
            sp.dma_start(b1_bc[:, :], bass.AP(ffn_bias.tensor, 0, [[0, P], [1, L]])).then_inc(s_l1l, 16)
            sp.dma_start(assign_i[:, :], bass.AP(assignments.tensor, 0, [[0, C], [1, L]])).then_inc(s_l1l, 16)
            for n in range(2):
                sp.wait_ge(x1_st[n], 16 * H // 2)
            sp.wait_ge(t_rdy, 4)

            def load_rows(t, n, s):
                for q in range(TB):
                    b = sp.value_load(slot_b[0:1, q, bass.ds(t, 1)], min_val=0, max_val=B - 1)
                    sp.dma_start(rows[n][H * q:H * q + H, :],
                                 x1_dram[bass.ds(b, 1), :, :].rearrange("b h l -> (b h) l")).then_inc(s[n], 16)

            for n in range(RB):
                load_rows(n, n, s_rd)
            with sp.Fori(1, NTD // RB) as c:
                for n in range(RB):
                    sp.wait_ge(xd_ps, RB * c + n - RB + 1)
                    load_rows(RB * c + n, n, s_rd)
            sp.wait_ge(xd_ps, NTD)
            for n in range(RB):
                load_rows(n, n, s_rl)
            with sp.Fori(1, NT // RB) as c:
                for n in range(RB):
                    sp.wait_ge(o_rdy, RB * c + n + 1)
                    load_rows(RB * c + n, n, s_rl)
            for t in range(NT // RB * RB, NT):
                sp.wait_ge(o_rdy, t + 1)
                load_rows(t, t % RB, s_rl)
            for n in range(RB):
                sp.wait_ge(s_out[n], 16 * len(range(n, NT, RB)))

        @block.gpsimd
        def _(pool):
            g = nc.gpsimd
            pool.sem_inc(o_rdy, RB)
            chain = Chain(pool, s_pool)
            imprecise = dict(allow_small_or_imprecise_dtypes=True)
            chain.after(g.memset(d_add, 0.0))
            chain.after(g.memset(k_zero, 0.0))
            chain.after(g.memset(phase_off[0:NM, :], 0.25), s_cst)
            chain.after(g.memset(phase_off[NM:P, :], 0.0), s_cst)
            chain.after(g.iota(bval, [[-1, FB]], base=FB - 1, channel_multiplier=0, **imprecise), s_cst)
            chain.after(g.iota(aval, [[-1, FA]], base=FA - 1, channel_multiplier=0, **imprecise), s_cst)
            chain.after(g.iota(pos, [[P, LB]], base=P - 1, channel_multiplier=-1, **imprecise), s_cst)
            chain.after(g.iota(iota_e[:, :], [[-1, E]], base=E, channel_multiplier=0, **imprecise), s_cst)
            chain.after(g.memset(ident[:, :], 0.0))
            chain.after(g.affine_select(out=ident[:, :], in_=ident[:, :], compare_op=ALU.not_equal, fill=1.0, base=0,
                            pattern=[[-1, P]], channel_multiplier=1), s_id)
            chain.after(g.memset(sel32, 0.0))
            sv = sel32.rearrange("k j (e r) -> k j e r", e=2)
            for part in range(2):
                chain.after(g.affine_select(out=sv, in_=sv, compare_op=ALU.not_equal, fill=1.0, base=-E * part,
                                            pattern=[[-2, NP], [-1, 2], [0, R]], channel_multiplier=1))
            chain.after(g.tensor_copy(sel[:, :, :], sel32), s_cst)
            chain.after(g.memset(low, 1.0))
            chain.after(g.affine_select(out=low, in_=low, compare_op=ALU.is_ge, fill=0.0, base=-1, pattern=[[-1, B]],
                            channel_multiplier=1), s_sort)
            chain.after(g.memset(tri8, 1.0))
            chain.after(g.affine_select(out=tri8, in_=tri8, compare_op=ALU.is_ge, fill=0.0, base=-1,
                            pattern=[[1, IDS], [-1, IDS]], channel_multiplier=0), s_sort)
            chain.after(g.memset(one_s, 1.0), s_sort)
            chain.after(g.iota(iota8, [[1, IDS]], base=0, channel_multiplier=0, **imprecise), s_sort)
            chain.after(g.iota(slot_v, [[1, TB], [TB, NTD]], base=0, channel_multiplier=0, **imprecise), s_sort)
            chain.after(g.iota(b_col[:, 0:1], [[0, 1]], base=0, channel_multiplier=1, **imprecise), s_sort)
            chain.after(g.iota(quad, [[0, TB], [0, TB], [0, H]], base=1, channel_multiplier=1, **imprecise))
            chain.after(g.affine_select(out=quad, in_=quad, compare_op=ALU.is_equal, fill=0.0, base=0,
                            pattern=[[1, TB], [-1, TB], [0, H]], channel_multiplier=0), s_sort)
            for q in range(TB):
                chain.after(g.iota(h_less[H * q:H * q + H, :], [[0, 1]], base=-H, channel_multiplier=1,
                       **imprecise), s_sort)
                chain.after(g.memset(pad_add[H * q:H * q + H, :], float((B + 1 + q) * H)), s_sort)
            pool.wait_ge(s_w0l, 16)
            for a in range(4):
                g.tensor_copy(w_rev[:, a, :].rearrange("p (k q) -> p k q", q=P),
                              w_raw[:, a, :].rearrange("p (k q) -> p k q", q=P)[:, :, ::-1]).then_inc(s_rev, 1)
            pool.wait_ge(s_arl, 32)
            g.tensor_copy(ar_rev.rearrange("p (k q) -> p k q", q=P),
                          ar_raw.rearrange("p (k q) -> p k q", q=P)[:, :, ::-1]).then_inc(s_rev, 1)

            def y_low(h, i):
                pool.wait_ge(y_hi, h + 1)
                g.tensor_tensor(yT[1][:, :, i, :], y32[i % 2][:, :, :], yT[0][:, :, i, :].bitcast(F32),
                                ALU.subtract).then_inc(y_lo, 1)

            def x_bias(h, n, i):
                pool.wait_ge(u_ps, h + 1)
                g.tensor_tensor(xg[n][:, i, :], xg[n][:, i, :], b0_bc[:, :], ALU.add).then_inc(xb_rdy, 1)

            def g_low(gr, j):
                pool.wait_ge(g_hi, NP * gr + j + 1)
                g.tensor_tensor(gT[j % 2][1][:, :], g32[j % 2][:, :], gT[j % 2][0][:, :].bitcast(F32),
                                ALU.subtract).then_inc(g_lo, 1)

            pool.wait_ge(s_par, 176)
            for i in range(GH):
                y_low(i, i)
                x_bias(i, 0, i)

            def group(gr, n, last):
                nxt = GH * gr + GH
                if not last:
                    y_low(nxt, 0)
                g_low(gr, 0)
                g_low(gr, 1)
                for i in range(1, GH):
                    if not last:
                        y_low(nxt + i, i)
                    g_low(gr, i + 1)
                for i in range(GH):
                    if not last:
                        x_bias(nxt + i, 1 - n, i)
                    if i < 3:
                        g_low(gr, i + 5)

            with pool.Fori(0, NG // 2 - 1) as t:
                for n in range(2):
                    group(2 * t + n, n, False)
            group(NG - 2, 0, False)
            group(NG - 1, 1, True)
            pool.wait_ge(mc_ps, IDS)
            g.memset(ones[:, :], 1.0).then_inc(s_l1c, 1)
            g.memset(hitmax[:, :], 0.0).then_inc(s_l1c, 1)
            g.iota(cidx[:, :], [[0, 1]], base=0, channel_multiplier=1, **imprecise).then_inc(s_l1c, 1)
            out_rows = out.rearrange("b h l -> (b h) l")
            last_row = pool.to_reg(B * H - 1)
            pool.wait_ge(t_rdy, 4)

            def next_row(t, n, stores):
                if not (isinstance(stores, int) and stores == 0):
                    pool.wait_ge(s_out[n], 16 * stores)
                g.tensor_copy(row_now[n][:, :], slot_row[:, bass.ds(t, 1)]).then_inc(row_rdy, 1)

            def finish(t, n, loads):
                pool.wait_ge(ft_sel, t + 1)
                pool.wait_ge(s_rl[n], TB * 16 * loads)
                pool.wait_ge(row_rdy, t + 1)
                g.tensor_tensor(outt[n], dsel[n][:, :], rows[n], ALU.add).then_inc(o_rdy, 1)
                pool.wait_ge(o_rdy, t + RB + 1)
                next_row(t + 1, (n + 1) % RB, loads - 1 + (n + 1) // RB)
                g.indirect_dma_start(out_rows, bass.IndirectOffsetOnAxis(ap=row_now[n][:, 0:1], axis=0),
                                     outt[n], None, bounds_check=last_row, oob_is_err=False
                                     ).then_inc(s_out[n], 16)

            next_row(0, 0, 0)
            for t in range(RB):
                finish(t, t, 1)
            with pool.Fori(1, NT // RB) as c:
                for n in range(RB):
                    finish(RB * c + n, n, c + 1)
            for t in range(NT // RB * RB, NT):
                finish(t, t % RB, t // RB + 1)

        S = {name: small[:, k, :] for k, name in enumerate(
            "dt ear th nal tu tr t0 ea tnh sn sh em1 t1 t2 t3 er1 ei den rden gr gi cr ci k1 k2 u32 r32 t32".split())}

        @block.scalar
        def _(act):
            a = nc.scalar
            act.sem_inc(xd_ev, 2)
            act.wait_ge(s_par, 176)
            a.activation(S["dt"], dt_bc, ACT.Exp).then_inc(s_dt, 1)
            act.wait_ge(s_parT, 1)
            a.activation(S["ear"], par[:, 0, :], ACT.Exp).then_inc(s_dt, 1)
            act.wait_ge(s_t0, 1)
            a.activation(S["ea"], S["nal"], ACT.Exp, scale=-1.0).then_inc(s_mags, 1)
            a.activation(S["tnh"], S["nal"], ACT.Tanh, scale=-0.5).then_inc(s_mags, 1)
            act.wait_ge(s_mag, 2)
            a.activation(v_mag, v_mag, ACT.Exp, scale=-1.0).then_inc(s_mags, 1)
            a.activation(a_mag, a_mag, ACT.Exp, scale=-float(FB)).then_inc(s_mags, 1)
            act.wait_ge(s_t0, 2)
            a.activation(S["sn"], S["t0"], ACT.Sin, scale=TURN).then_inc(s_sin, 1)
            a.activation(S["sh"], S["t0"], ACT.Sin, scale=TURN / 2).then_inc(s_sin, 1)
            act.wait_ge(s_fr, 1)
            a.activation(a_ph, a_ph, ACT.Sin, scale=TURN).then_inc(s_sin, 1)
            act.wait_ge(s_fr, 2)
            a.activation(v_ph, v_ph, ACT.Sin, scale=TURN).then_inc(s_sin, 1)

            for k in range(NWT):
                act.wait_ge(s_wps, k + 1)
                cols = LB * AR if k == LB else L
                a.activation(weight_out(k, 0), weight_in_psum(k, cols), ACT.Copy).then_inc(s_whi, 1)

            def u_high(h, i, first=False):
                act.wait_ge(u_ps, h + 1)
                if not (first and i < 2):
                    act.wait_ge(y_ps, h - 1)
                a.activation(uT[i % 2][0][:, :, :], wb[0][:, :], ACT.Copy).then_inc(u_hi, 1)

            def y_high(h, i, first=False):
                act.wait_ge(y_ms, h + 1)
                if not first:
                    act.wait_ge(b_done, h - GH + 1)
                a.activation(yT[0][:, :, i, :], y32[i % 2][:, :, :], ACT.Copy).then_inc(y_hi, 1)

            def ar_evac(gr):
                act.wait_ge(ar_ps, gr + 1)
                a.activation(lgT[:, :], wb[0][R:AR, :], ACT.Copy).then_inc(ar_ev, 1)
                a.activation(res[0:R, :], wb[0][0:R, :], ACT.Copy).then_inc(ar_ev, 1)

            def g_high(gr, j):
                act.wait_ge(g_mul, NP * gr + j + 1)
                if j >= 2:
                    act.wait_ge(d_done, (NP - 1) * gr + j - 1)
                a.activation(gT[j % 2][0][:, :], g32[j % 2][:, :], ACT.Copy).then_inc(g_hi, 1)

            u_high(0, 0, True)
            for i in range(GH):
                if i + 1 < GH:
                    u_high(i + 1, i + 1, True)
                y_high(i, i, True)
            ar_evac(0)

            def group(gr, n, last):
                nxt = GH * gr + GH
                act.wait_ge(r_sub, gr + 1)
                a.activation(rex[:, :, :], rex[:, :, :], ACT.Exp).then_inc(r_exp, 1)
                if not last:
                    u_high(nxt, 0)
                    y_high(nxt, 0)
                    u_high(nxt + 1, 1)
                act.wait_ge(ct_ps, gr + 1)
                a.activation(cTs[:, :], bb[1][0:2 * E, :], ACT.Copy).then_inc(ct_sb, 1)
                g_high(gr, 0)
                g_high(gr, 1)
                for i in range(1, GH):
                    if not last:
                        y_high(nxt + i, i)
                        if i + 1 < GH:
                            u_high(nxt + i + 1, i + 1)
                    g_high(gr, i + 1)
                for j in range(GH + 1, NP):
                    g_high(gr, j)
                if not last:
                    ar_evac(gr + 1)
            with act.Fori(0, NG // 2 - 1) as t:
                for n in range(2):
                    group(2 * t + n, n, False)
            group(NG - 2, 0, False)
            group(NG - 1, 1, True)
            for n in range(2):
                act.wait_ge(x1_st[n], 16 * H // 2)
            for k in range(NWT, NWT + LB + 1):
                act.wait_ge(s_wps, k + 1)
                cols = LB * C if k == NWT + LB else L
                a.activation(weight_out(k, 0), weight_in_psum(k, cols), ACT.Copy).then_inc(s_whi, 1)

            def split(e, n, first):
                act.wait_ge(s_cwl[n], 16 if first else (e - n) * 8 + 16)
                if not first:
                    act.wait_ge(mc_ps, e - 1)
                a.activation(w_sp[n][0][:, :, :], w_id[n][:, :, :], ACT.Copy).then_inc(cw_hi, 1)

            def merged(e):
                for k in range(LB):
                    act.wait_ge(m_ps, LB * e + k + 1)
                    a.activation(mw[0][:, bass.ds(e, 1), k, :].rearrange("p e f -> p (e f)"), acc[k][:, :],
                                 ACT.Copy).then_inc(m_hi, 1)

            split(0, 0, True)
            split(1, 1, True)
            with act.Fori(0, IDS // 2 - 1) as t:
                for n in range(2):
                    merged(2 * t + n)
                    split(2 * t + n + 2, n, False)
            merged(IDS - 2)
            merged(IDS - 1)

            def dots_x(t, n):
                act.wait_ge(xd_ps, t + 1)
                a.activation(xtf[n][:, :, :], wb[n][:, :], ACT.Copy).then_inc(xd_ev, 1)

            def dots_step(c, last):
                for w in range(TD - 1 if last else TD):
                    dots_x(c * TD + w + 1, (w + 1) % 2)
                act.wait_ge(dt_sh, c + 2)
                a.activation(dexp[:, :, :], dshift[:, :, :], ACT.Exp, scale=10.0).then_inc(dt_exp, 1)

            act.wait_ge(mc_ps, IDS)
            dots_x(0, 0)
            with act.Fori(0, NTD // TD - 1) as c:
                dots_step(c, False)
            dots_step(NTD // TD - 1, True)

            def dense_x(t, n):
                act.wait_ge(xe_ps, t + 1)
                a.activation(xts[n][0][:, :, :], wb[n][:, :], ACT.Copy).then_inc(xe_hi, 1)

            dense_x(0, 0)
            with act.Fori(0, NT // RB) as c:
                for n in range(RB):
                    dense_x(RB * c + n + 1, (n + 1) % 2)
            for t in range(NT // RB * RB + 1, NT):
                dense_x(t, t % 2)

        @block.vector
        def _(dve):
            v = nc.vector
            dve.sem_inc(x1_rdy, GH)
            dve.sem_inc(dt_sh, 1)
            dve.sem_inc(xe_lo, 2)
            dve.sem_inc(ft_ev, RB)
            chain = Chain(dve, s_dve)
            dve.wait_ge(s_par, 176)
            for q in range(2):
                for half in range(2):
                    v.tensor_copy(modes[:, 2 + q, NM * half:NM * half + NM], c_raw[:, :, q]).then_inc(s_stk, 1)
            chain.after(v.tensor_copy(len_f, len_i))
            dve.wait_ge(s_cst, 7)
            for k in range(LB):
                chain.after(v.tensor_scalar(mask[:, k, :], len_f, pos[:, k:k + 1], None, ALU.is_gt))
            dve.wait_ge(s_kps_par, 1)
            v.tensor_copy(par, bb[0][:, 0:4 * H].rearrange("p (q h) -> p q h", q=4)).then_inc(s_parT, 1)
            dve.wait_ge(s_parT, 1)
            dve.wait_ge(s_dt, 2)

            def tt(o, x0, x1, op):
                chain.after(v.tensor_tensor(S.get(o, o) if isinstance(o, str) else o,
                                            S[x0] if isinstance(x0, str) else x0,
                                            S[x1] if isinstance(x1, str) else x1, op))

            def ts(o, x0, s0, s1, op0, op1):
                chain.after(v.tensor_scalar(S[o] if isinstance(o, str) else o,
                                            S[x0] if isinstance(x0, str) else x0, s0, s1, op0, op1))

            aim = par[:, 1, :]
            v.tensor_tensor(S["nal"], S["ear"], S["dt"], ALU.mult).then_inc(s_t0, 1)
            dve.wait_ge(s_t0, 1)
            tt("th", aim, "dt", ALU.mult)
            ts("tu", "th", 1.0 / (2.0 * math.pi), None, ALU.mult, ALU.bypass)
            ts("tr", "tu", MAGIC, MAGIC, ALU.add, ALU.subtract)
            v.tensor_tensor(S["t0"], S["tu"], S["tr"], ALU.subtract).then_inc(s_t0, 1)
            dve.wait_ge(s_t0, 2)

            def bc(t, n):
                return t.rearrange("p (h o) -> p h o", o=1).broadcast_to([P, H, n])

            def row(t, n):
                return t.rearrange("p (o b) -> p o b", o=1).broadcast_to([P, H, n])

            v.tensor_tensor(v_mag, bc(S["nal"], FB), row(bval, FB), ALU.mult).then_inc(s_mag, 1)
            v.tensor_tensor(a_mag, bc(S["nal"], FA), row(aval, FA), ALU.mult).then_inc(s_mag, 1)
            ts("u32", "t0", float(FB), None, ALU.mult, ALU.bypass)
            ts("r32", "u32", MAGIC, MAGIC, ALU.add, ALU.subtract)
            tt("t32", "u32", "r32", ALU.subtract)
            chain.after(v.tensor_tensor(a_ph[:, 1, :, :], bc(S["t32"], FA), row(aval, FA), ALU.mult))
            chain.after(v.tensor_scalar(a_ph[:, 0, :, :], a_ph[:, 1, :, :], 0.25, None, ALU.add))
            chain.after(v.tensor_scalar(a_tmp, a_ph, MAGIC, MAGIC, ALU.add, ALU.subtract))
            v.tensor_tensor(a_ph, a_ph, a_tmp, ALU.subtract).then_inc(s_fr, 1)
            chain.after(v.tensor_tensor(v_ph, bc(S["t0"], FB), row(bval, FB), ALU.mult))
            chain.after(v.tensor_scalar(v_ph, v_ph, phase_off[:, 0:1], None, ALU.add))
            dve.wait_ge(s_fr, 1)
            chain.after(v.tensor_scalar(v_tmp, v_ph, MAGIC, MAGIC, ALU.add, ALU.subtract))
            v.tensor_tensor(v_ph, v_ph, v_tmp, ALU.subtract).then_inc(s_fr, 1)
            dve.wait_ge(s_mags, 2)
            chain.after(v.scalar_tensor_tensor(S["em1"], S["ea"], 1.0, S["tnh"], ALU.add, ALU.mult))
            dve.wait_ge(s_sin, 2)
            tt("t1", "sh", "sh", ALU.mult)
            tt("t2", "t1", "ea", ALU.mult)
            chain.after(v.scalar_tensor_tensor(S["er1"], S["t2"], -2.0, S["em1"], ALU.mult, ALU.add))
            tt("ei", "ea", "sn", ALU.mult)
            tt("t1", "ear", "ear", ALU.mult)
            tt("t2", aim, aim, ALU.mult)
            tt("den", "t1", "t2", ALU.add)
            chain.after(v.reciprocal(S["rden"], S["den"]))
            tt("t1", "ei", aim, ALU.mult)
            tt("t2", "er1", "ear", ALU.mult)
            tt("t3", "t1", "t2", ALU.subtract)
            tt("gr", "t3", "rden", ALU.mult)
            tt("t1", "ei", "ear", ALU.mult)
            tt("t2", "er1", aim, ALU.mult)
            tt("t3", "t1", "t2", ALU.add)
            chain.after(v.scalar_tensor_tensor(S["gi"], S["t3"], -1.0, S["rden"], ALU.mult, ALU.mult))
            tt("t1", par[:, 2, :], "gr", ALU.mult)
            tt("t2", par[:, 3, :], "gi", ALU.mult)
            tt("cr", "t1", "t2", ALU.subtract)
            tt("t1", par[:, 2, :], "gi", ALU.mult)
            tt("t2", par[:, 3, :], "gr", ALU.mult)
            tt("ci", "t1", "t2", ALU.add)
            for half, (f1, s1, f2, s2) in enumerate((("cr", 2.0, "ci", -2.0), ("ci", -2.0, "cr", -2.0))):
                rows = slice(NM * half, NM * half + NM)
                ts(S["k1"][rows, :], S[f1][rows, :], s1, None, ALU.mult, ALU.bypass)
                ts(S["k2"][rows, :], S[f2][rows, :], s2, None, ALU.mult, ALU.bypass)
            dve.wait_ge(s_mags, 4)
            dve.wait_ge(s_sin, 3)
            for q in range(2):
                chain.after(v.tensor_tensor(a_ph[:, q, :, :], a_ph[:, q, :, :], a_mag, ALU.mult))
                chain.after(v.tensor_tensor(a_ph[:, q, :, :], a_ph[:, q, :, :], bc(S["k1" if q == 0 else "k2"], FA),
                                            ALU.mult))
            v.tensor_tensor(a_ph[:, 0, :, :], a_ph[:, 0, :, :], a_ph[:, 1, :, :], ALU.add).then_inc(s_uv, 1)
            dve.wait_ge(s_sin, 4)
            v.tensor_tensor(v_ph, v_ph, v_mag, ALU.mult).then_inc(s_uv, 1)
            dve.wait_ge(s_kps, 1)
            for n in range(2):
                hs = slice(H // 2 * n, H // 2 * n + H // 2)
                chain.after(v.tensor_copy(k32[:, hs, :], bb[n][0:FA, :].rearrange("a (h b) -> a h b", b=FB)))
            chain.after(v.tensor_tensor(k32[:, :, FB - 1], k32[:, :, FB - 1], d_add, ALU.add))
            chain.after(v.tensor_copy(k_split[0], k32))
            v.tensor_tensor(k_split[1], k32, k_split[0].bitcast(F32), ALU.subtract).then_inc(s_klo, 1)
            for k in range(NWT):
                dve.wait_ge(s_whi, k + 1)
                cols = LB * AR if k == LB else L
                v.tensor_tensor(weight_out(k, 1), weight_in_psum(k, cols), weight_out(k, 0).bitcast(F32),
                                ALU.subtract).then_inc(s_wlo, 1)

            dve.wait_ge(s_sort, 7 + 2 * TB)
            chain.after(v.tensor_copy(ids_r, ids_ri))
            chain.after(v.tensor_copy(ids_c[:, 0:1], ids_ci))
            chain.after(v.tensor_scalar(same, ids_r, ids_c[:, 0:1], None, ALU.is_equal))
            chain.after(v.tensor_tensor(same, same, low, ALU.mult))
            chain.after(v.reduce_sum(rank[:, 0:1], same, AX))
            v.tensor_scalar(oh8, iota8, ids_c[:, 0:1], None, ALU.is_equal).then_inc(t_mat, 1)
            dve.wait_ge(t_cnt, 1)
            chain.after(v.tensor_scalar(n_tiles_i, wb[0][:, 0:IDS], float(TB - 1), None, ALU.add))
            chain.after(v.tensor_scalar(n_tiles_i, n_tiles_i, 2, None, ALU.arith_shift_right))
            chain.after(v.tensor_copy(n_tiles, n_tiles_i))
            chain.after(v.tensor_tensor(prod88, tri8, n_tiles.rearrange("p (o e) -> p o e", o=1)
                                        .broadcast_to([P, IDS, IDS]), ALU.mult))
            chain.after(v.reduce_sum(first_tile, prod88, AX))
            dve.wait_ge(t_mat, 1)
            chain.after(v.tensor_tensor(first_tile, first_tile, oh8, ALU.mult))
            chain.after(v.reduce_sum(place[:, 0:1], first_tile, AX))
            chain.after(v.scalar_tensor_tensor(place[:, 2:3], place[:, 0:1], float(TB), rank[:, 0:1], ALU.mult, ALU.add))
            v.tensor_scalar(match, slot_v, place[:, 2:3], None, ALU.is_equal).then_inc(t_mat, 1)
            dve.wait_ge(t_tab, 1)
            slot1 = wb[1][:, 0:NTD]
            v.tensor_scalar(slot_ok[:, :], slot1, 0.5, None, ALU.is_gt).then_inc(t_rdy, 1)
            chain.after(v.tensor_scalar(row_f, slot1, float(H), h_less, ALU.mult, ALU.add))
            chain.after(v.tensor_scalar(row_pad, slot1, 0.5, pad_add, ALU.is_lt, ALU.mult))
            v.tensor_tensor(slot_row[:, :], row_f, row_pad, ALU.add).then_inc(t_rdy, 1)
            v.tensor_copy(tile_id[:, :], wb[0][0:1, 64:64 + NTD]).then_inc(t_rdy, 1)
            v.tensor_copy(slot_b[:, :, :], wb[0][0:1, 128:128 + TB * NTD].rearrange("p (q t) -> p q t", q=TB)
                          ).then_inc(t_rdy, 1)

            def u_low(h, i):
                dve.wait_ge(u_hi, h + 1)
                v.tensor_tensor(uT[i % 2][1][:, :, :], wb[0][:, :].rearrange("p (k b) -> p k b", k=LB),
                                uT[i % 2][0][:, :, :].bitcast(F32), ALU.subtract).then_inc(u_lo, 1)

            def y_mask(h, i, first=False):
                dve.wait_ge(y_ps, h + 1)
                if not (first and i < 2):
                    dve.wait_ge(y_lo, h - 1)
                v.tensor_tensor(y32[i % 2][:, :, :], wb[1][:, :].rearrange("p (k b) -> p k b", k=LB),
                                mask[:, :, :], ALU.mult).then_inc(y_ms, 1)

            def gated(gr, j):
                dve.wait_ge(bc_ps, NP * gr + j + 1)
                if j >= 2:
                    dve.wait_ge(g_lo, NP * gr + j - 1)
                v.tensor_tensor(g32[j % 2][:, :], bb[j % 2][:, :], res[:, :], ALU.mult).then_inc(g_mul, 1)

            def routing(gr):
                ch = Chain(dve, s_rt, ROUTE * gr)
                dve.wait_ge(ar_ev, 2 * gr + 2)
                ch.after(v.tensor_copy(res[R:P, :], res[0:R, :]))
                dve.wait_ge(lt_ps, gr + 1)
                lg = bb[0][:, 0:GH * E].rearrange("p (i e) -> p i e", i=GH)

                def over(t, n=E):
                    return t.rearrange("p (i o) -> p i o", o=1).broadcast_to([P, GH, n])

                ch.after(v.reduce_max(rmax[:, :], lg, AX))
                v.tensor_tensor(rex[:, :, :], lg, over(rmax[:, :]), ALU.subtract).then_inc(r_sub, 1)
                dve.wait_ge(r_exp, gr + 1)
                ch.after(v.reduce_sum(rsum[:, :], rex[:, :, :], AX))
                ch.after(v.reciprocal(rinv[:, :], rsum[:, :]))
                ch.after(v.tensor_tensor(rprob[:, :, :], rex[:, :, :], over(rinv[:, :]), ALU.mult))
                marks = iota_e[:, :].rearrange("p (o e) -> p o e", o=1).broadcast_to([P, GH, E])
                for q in range(2):
                    ch.after(v.reduce_max(rtop[:, q, :], rprob[:, :, :], AX))
                    ch.after(v.tensor_tensor(roh[:, :, q, :], rprob[:, :, :], over(rtop[:, q, :]), ALU.is_equal))
                    ch.after(v.tensor_tensor(roh[:, :, q, :], roh[:, :, q, :], marks, ALU.mult))
                    ch.after(v.reduce_max(rmark[:, :], roh[:, :, q, :], AX))
                    ch.after(v.tensor_tensor(roh[:, :, q, :], marks, over(rmark[:, :]), ALU.is_equal))
                    if q == 0:
                        ch.after(v.scalar_tensor_tensor(rprob[:, :, :], roh[:, :, q, :], -2.0, rprob[:, :, :],
                                                        ALU.mult, ALU.add))
                ch.after(v.scalar_tensor_tensor(rden[:, :], rtop[:, 0, :], 1e-6, rtop[:, 1, :], ALU.add, ALU.add))
                ch.after(v.reciprocal(rinv[:, :], rden[:, :]))
                for q in range(2):
                    ch.after(v.scalar_tensor_tensor(rw[:, q, :], rtop[:, q, :], SCALING, rinv[:, :],
                                                    ALU.mult, ALU.mult))
                for q in range(2):
                    ch.after(v.tensor_tensor(roh[:, :, q, :], roh[:, :, q, :], over(rw[:, q, :]), ALU.mult))
                ch.after(v.tensor_tensor(rcomb[:, :, :], roh[:, :, 0, :], roh[:, :, 1, :], ALU.add))
                ch.after(v.tensor_copy(cst[:, :, 0:E].bitcast(F32R), rcomb[:, :, :]))
                v.tensor_tensor(cst[:, :, E:2 * E], rcomb[:, :, :], cst[:, :, 0:E], ALU.subtract).then_inc(c_rdy, 1)
                assert ch.n == ROUTE, ch.n

            u_low(0, 0)
            for i in range(GH):
                if i + 1 < GH:
                    u_low(i + 1, i + 1)
                y_mask(i, i, True)

            def group(gr, n, last):
                nxt = GH * gr + GH
                routing(gr)
                if not last:
                    u_low(nxt, 0)
                    y_mask(nxt, 0)
                    u_low(nxt + 1, 1)
                gated(gr, 0)
                gated(gr, 1)
                for i in range(1, GH):
                    if not last:
                        y_mask(nxt + i, i)
                        if i + 1 < GH:
                            u_low(nxt + i + 1, i + 1)
                    gated(gr, i + 1)
                for j in range(GH + 1, NP):
                    gated(gr, j)
                for i in range(GH):
                    dve.wait_ge(a_done, GH * gr + i + 1)
                    dve.wait_ge(xb_rdy, GH * gr + i + 1)
                    v.tensor_tensor(xg[n][:, i, :], acc[i][:, :], xg[n][:, i, :], ALU.add).then_inc(x1_rdy, 1)

            with dve.Fori(0, NG // 2 - 1) as t:
                for n in range(2):
                    group(2 * t + n, n, False)
            group(NG - 2, 0, False)
            group(NG - 1, 1, True)
            for k in range(NWT, NWT + LB + 1):
                dve.wait_ge(s_whi, k + 1)
                cols = LB * C if k == NWT + LB else L
                v.tensor_tensor(weight_out(k, 1), weight_in_psum(k, cols), weight_out(k, 0).bitcast(F32),
                                ALU.subtract).then_inc(s_wlo, 1)

            def split(e, n):
                dve.wait_ge(cw_hi, e + 1)
                v.tensor_tensor(w_sp[n][1][:, :, :], w_id[n][:, :, :], w_sp[n][0][:, :, :].bitcast(F32),
                                ALU.subtract).then_inc(cw_lo, 1)

            def merged(e, n):
                for k in range(LB):
                    dve.wait_ge(m_hi, LB * e + k + 1)
                    v.tensor_tensor(mw[1][:, bass.ds(e, 1), k, :].rearrange("p e f -> p (e f)"), acc[k][:, :],
                                    mw[0][:, bass.ds(e, 1), k, :].rearrange("p e f -> p (e f)").bitcast(F32),
                                    ALU.subtract).then_inc(m_lo, 1)
                dve.wait_ge(mc_ps, e + 1)
                v.tensor_copy(mc[:, bass.ds(e, 1), :, :].rearrange("p e k c -> p (e k) c"),
                              wb[n][:, 0:LB * C].rearrange("p (k c) -> p k c", k=LB)).then_inc(mc_ev, 1)

            split(0, 0)
            split(1, 1)
            with dve.Fori(0, IDS // 2 - 1) as t:
                for n in range(2):
                    merged(2 * t + n, n)
                    split(2 * t + n + 2, n)
            merged(IDS - 2, 0)
            merged(IDS - 1, 1)
            dve.wait_ge(s_l1c, 3)
            dve.wait_ge(t_rdy, 4)
            with dve.Fori(0, NTD // TD) as c:
                ch = Chain(dve, s_dn, DOTS * c)
                dve.wait_ge(dm_ps, c * TD + TD)
                dots = acc[0][:, :].rearrange("p (t c) -> p t c", t=TD)

                def per_tile(t):
                    return t.rearrange("p (t o) -> p t o", o=1).broadcast_to([P, TD, C])

                ch.after(v.reduce_max(dmax[:, :], dots, AX))
                v.tensor_tensor(dshift[:, :, :], dots, per_tile(dmax[:, :]), ALU.subtract).then_inc(dt_sh, 1)
                dve.wait_ge(dt_exp, c + 1)
                ch.after(v.reduce_sum(dsum[:, :], dexp[:, :, :], AX))
                ch.after(v.reciprocal(dinv[:, :], dsum[:, :]))
                ch.after(v.tensor_tensor(hits[:, :, :], dexp[:, :, :], per_tile(dinv[:, :]), ALU.mult))
                ch.after(v.tensor_scalar(hits[:, :, :], hits[:, :, :], 0.01, None, ALU.is_gt))
                ch.after(v.tensor_tensor(hits[:, :, :], hits[:, :, :], per_tile(slot_ok[:, bass.ds(c * TD, TD)]),
                                         ALU.mult))
                ch.after(v.reduce_max(query[:, bass.ds(c * TD, TD)], hits[:, :, :], AX))
                ch.after(v.reduce_max(hit8[:, :], hits[:, :, :].rearrange("p t c -> p c t"), AX))
                ch.after(v.tensor_tensor(hitmax[:, :], hitmax[:, :], hit8[:, :], ALU.max))
                assert ch.n == DOTS, ch.n
            dve.wait_ge(s_l1l, 32)
            ch = Chain(dve, s_dn, DOTS * (NTD // TD))
            ch.after(v.tensor_copy(assign_f[:, :], assign_i[:, :]))
            v.tensor_scalar(onehot[:, :], assign_f[:, :], cidx[:, 0:1], None, ALU.is_equal).then_inc(cs_rdy, 1)
            dve.wait_ge(cnt_ps, 1)
            v.tensor_scalar(csel[:, :], acc[1][0:C, 0:P], 0.5, None, ALU.is_gt).then_inc(cs_rdy, 1)
            dve.wait_ge(rs_ps, 1)
            v.tensor_copy(rowsel[:, :], acc[1][:, :]).then_inc(cs_rdy, 1)
            dve.wait_ge(cs_rdy, 3)

            def dense_x(t, n):
                dve.wait_ge(xe_hi, t + 1)
                v.tensor_tensor(xts[n][1][:, :, :], wb[n][:, :].rearrange("p (k b) -> p k b", k=LB),
                                xts[n][0][:, :, :].bitcast(F32), ALU.subtract).then_inc(xe_lo, 1)

            def select(t, n):
                dve.wait_ge(ft_ps, t + 1)
                v.tensor_tensor(dense[n % 2][:, :], acc[n][:, :], b1_bc[:, :], ALU.add).then_inc(ft_ev, 1)
                dve.wait_ge(ft_ev, t + RB + 1)
                dve.wait_ge(o_rdy, t + 1)
                v.scalar_tensor_tensor(dsel[n][:, :], dense[n % 2][:, :], query[:, bass.ds(t, 1)],
                                       rowsel[:, :], ALU.mult, ALU.mult).then_inc(ft_sel, 1)

            dense_x(0, 0)
            with dve.Fori(0, NT // RB) as c:
                for n in range(RB):
                    dense_x(RB * c + n + 1, (n + 1) % 2)
                    select(RB * c + n, n)
            for t in range(NT // RB * RB, NT):
                if t + 1 < NT:
                    dense_x(t + 1, (t + 1) % 2)
                select(t, t % RB)

        @block.tensor
        def _(pe):
            mm = nc.tensor.matmul
            pe.wait_ge(s_id, 1)
            pe.wait_ge(s_stk, 4)
            for q in range(4):
                last = nc.tensor.transpose(bb[0][:, H * q:H * q + H], modes[:, q, :], ident[0:H, 0:H])
            last.then_inc(s_kps_par, 1)

            def weight(k):
                if k >= GH:
                    pe.wait_ge(s_wlo, k - GH + 1)
                bank = acc[k % GH]
                if k < LB:
                    pe.wait_ge(s_rev, 4)
                    src = [(w_rev[:, a, P * k:P * k + P], P * a) for a in range(4)]
                elif k == LB:
                    pe.wait_ge(s_rev, 5)
                    src = [(ar_rev[:, P * a:P * a + P], AR * a) for a in range(LB)]
                elif k < NWT:
                    pe.wait_ge(s_bl, 64)
                    j = k - LB - 1
                    src = [(b_raw[:, a, 2 * j:2 * j + 2, :].rearrange("p e r -> p (e r)"), P * a) for a in range(4)]
                elif k < NWT + LB:
                    a0 = k - NWT
                    pe.wait_ge(s_fwl, 32)
                    src = [(f_raw[:, a, P * a0:P * a0 + P], P * a) for a in range(4)]
                else:
                    src = [(cent_raw[:, P * a:P * a + P], C * a) for a in range(LB)]
                for s, at in src:
                    rows, cols = s.shape[0], s.shape[1]
                    last = nc.tensor.transpose(bank[0:cols, at:at + rows], s, ident[0:rows, 0:rows])
                last.then_inc(s_wps, 1)

            for k in range(GH):
                weight(k)
            pe.wait_ge(s_uv, 2)
            pe.wait_ge(s_parT, 1)
            for h in range(H):
                last = mm(bb[h // 16][0:FA, FB * (h % 16):FB * (h % 16) + FB], a_ph[:, 0, h, :], v_ph[:, h, :],
                          start=True, stop=True)
            last.then_inc(s_kps, 1)
            for k in range(GH, NWT):
                weight(k)

            def u_transpose(h, i, n, g2):
                pe.wait_ge(s_x[n][i], 16 * g2)
                for k in range(LB):
                    last = nc.tensor.transpose(wb[0][:, P * k:P * k + P], xg[n][:, i, P * k:P * k + P], ident[:, :])
                last.then_inc(u_ps, 1)

            def y_conv(h, i, loads):
                pe.wait_ge(u_lo, h + 1)
                pe.wait_ge(s_sk[i % 2], 16 * loads)
                for d in range(LB):
                    cols = slice(L - P * (d + 1), L - P * d)
                    for a, b in ((0, 0), (0, 1), (1, 0)):
                        last = mm(wb[1][:, P * d:L], sk[i % 2][:, a, cols],
                                  uT[i % 2][b][:, 0:LB - d, :].rearrange("p k b -> p (k b)"),
                                  start=(d == 0 and a == 0 and b == 0), stop=(d == LB - 1 and a == 1))
                last.then_inc(y_ps, 1)

            def ar_project(gr):
                pe.wait_ge(y_lo, GH * gr + GH)
                steps = [(a, b, k) for a, b in ((0, 0), (1, 0), (0, 1)) for k in range(LB)]
                for a, b, k in steps:
                    last = mm(wb[0][0:AR, :], arw[a][:, k, :], yT[b][:, k, :, :].rearrange("p i b -> p (i b)"),
                              start=(a, b, k) == steps[0], stop=(a, b, k) == steps[-1])
                last.then_inc(ar_ps, 1)

            def logits(gr):
                for i in range(GH):
                    t = nc.tensor.transpose(bb[0][:, E * i:E * i + E], lgT[:, P * i:P * i + P], ident[0:E, 0:E])
                t.then_inc(lt_ps, 1)

            def base(gr, i, between=None):
                pe.wait_ge(x1_rdy, GH * gr + i + 1)
                for a, b in ((0, 0), (0, 1), (1, 0)):
                    for k in range(LB):
                        last = mm(acc[i][:, :], yT[a][:, k, i, :], w0[b][:, k, :], start=(a == b == k == 0),
                                  stop=False)
                    if between and a == b == 0:
                        between()
                last.then_inc(b_done, 1)

            def gates(gr, j):
                if j >= 2:
                    pe.wait_ge(g_mul, NP * gr + j - 1)
                mm(bb[j % 2][:, :], sel[:, j, :], cTs[:, :], start=True, stop=True).then_inc(bc_ps, 1)

            def experts(gr, j):
                pe.wait_ge(g_lo, NP * gr + j + 1)
                for i in range(GH):
                    for a, b in ((0, 0), (0, 1), (1, 0)):
                        last = mm(acc[i][:, :], gT[j % 2][a][:, P * i:P * i + P], bw[b][:, j, :],
                                  start=False, stop=(j == NP - 1 and a == 1))
                    if j == NP - 1:
                        last.then_inc(a_done, 1)
                if j < NP - 1:
                    last.then_inc(d_done, 1)

            pe.wait_ge(t_mat, 1)
            mm(wb[0][:, 0:IDS], one_s, oh8, start=True, stop=True).then_inc(t_cnt, 1)
            pe.wait_ge(t_mat, 2)
            for q in range(TB):
                mm(wb[1][:, 0:NTD], quad[:, q, :, :].rearrange("p r h -> p (r h)"), match[:, q, :],
                   start=(q == 0), stop=(q == TB - 1))
            mm(wb[0][0:1, 64:64 + NTD], ids_c[:, 0:1], match[:, 0, :], start=True, stop=True)
            mm(wb[0][0:1, 128:128 + TB * NTD], b_col[:, 0:1], match.rearrange("p q t -> p (q t)"),
               start=True, stop=True).then_inc(t_tab, 1)
            pe.wait_ge(t_rdy, 4)
            u_transpose(0, 0, 0, 1)
            for i in range(GH):
                y_wait = i
                if i + 1 < GH:
                    pe.wait_ge(u_lo, i + 1)
                    u_transpose(i + 1, i + 1, 0, 1)
                if i:
                    pe.wait_ge(y_ms, i)
                y_conv(i, i, i // 2 + 1)
            pe.wait_ge(u_lo, GH)
            ar_project(0)

            def group(gr, n, last, half):
                nxt = GH * gr + GH
                g2 = (half + 1) if n == 0 else (half + 2)
                pe.wait_ge(ar_ev, 2 * gr + 2)
                base(gr, 0, between=lambda: logits(gr))
                if not last:
                    u_transpose(nxt, 0, 1 - n, g2)
                base(gr, 1)
                if not last:
                    y_conv(nxt, 0, 2 * gr + 3)
                    u_transpose(nxt + 1, 1, 1 - n, g2)
                base(gr, 2)
                pe.wait_ge(c_rdy, gr + 1)
                for i in range(GH):
                    t = nc.tensor.transpose(bb[1][0:2 * E, P * i:P * i + P], cst[:, i, :], ident[:, :])
                t.then_inc(ct_ps, 1)
                base(gr, 3)
                pe.wait_ge(ct_sb, gr + 1)
                gates(gr, 0)
                gates(gr, 1)
                for i in range(1, GH):
                    if not last:
                        pe.wait_ge(y_ms, nxt + i)
                        y_conv(nxt + i, i, 2 * gr + 3 + i // 2)
                        if i + 1 < GH:
                            u_transpose(nxt + i + 1, i + 1, 1 - n, g2)
                    experts(gr, i - 1)
                    gates(gr, i + 1)
                for j in range(GH - 1, NP):
                    experts(gr, j)
                    if j + 2 < NP:
                        gates(gr, j + 2)
                if not last:
                    ar_project(gr + 1)
            with pe.Fori(0, NG // 2 - 1) as t:
                for n in range(2):
                    group(2 * t + n, n, False, t)
            group(NG - 2, 0, False, NG // 2 - 1)
            group(NG - 1, 1, True, NG // 2 - 1)

            pe.wait_ge(x1_rdy, GH * NG + GH)
            for k in range(NWT, NWT + LB + 1):
                weight(k)
            pe.wait_ge(s_wlo, NWT + LB + 1)

            def merge(e, n, first):
                pe.wait_ge(cw_lo, e + 1)
                steps = [(a, b, o) for a, b in ((0, 0), (0, 1), (1, 0)) for o in range(LB)]
                if not first:
                    pe.wait_ge(mc_ev, e - 1)
                for k in range(LB):
                    if not first or e == 1:
                        pe.wait_ge(m_lo, LB * e + k - 3)
                    for dst, rhs in ((acc[k][:, :], f_w), (wb[n][:, C * k:C * k + C], f_c)):
                        for s in steps:
                            a, b, o = s
                            last = mm(dst, w_sp[n][a][:, o, P * k:P * k + P], rhs[b][:, o, :],
                                      start=s == steps[0], stop=s == steps[-1])
                        if rhs is f_w:
                            last.then_inc(m_ps, 1)
                last.then_inc(mc_ps, 1)

            merge(0, 0, True)
            merge(1, 1, True)
            with pe.Fori(1, IDS // 2) as t:
                for n in range(2):
                    merge(2 * t + n, n, False)
            pe.wait_ge(m_lo, LB * IDS)
            pe.wait_ge(mc_ev, IDS)

            def transpose_rows(n, bank, s, count):
                pe.wait_ge(s[n], TB * 16 * count)
                for k in range(LB):
                    last = nc.tensor.transpose(wb[bank][:, P * k:P * k + P], rows[n][:, P * k:P * k + P], ident[:, :])
                return last

            def dots_step(c, last):
                for w in range(TD):
                    t, nxt = c * TD + w, w + 1
                    if not (last and nxt == TD):
                        pe.wait_ge(xd_ev, t + 2)
                        transpose_rows(nxt % RB, nxt % 2, s_rd, (TD // RB) * c + nxt // RB + 1).then_inc(xd_ps, 1)
                    pe.wait_ge(xd_ev, t + 3)
                    if w == 0:
                        pe.wait_ge(dt_sh, c + 1)
                    e = pe.value_load(tile_id[0:1, bass.ds(t, 1)], min_val=0, max_val=IDS - 1)
                    for k in range(LB):
                        m = mm(acc[0][:, C * w:C * w + C], xtf[w % 2][:, k, :],
                               mc[:, bass.ds(e, 1), k, :].rearrange("p e f -> p (e f)"),
                               start=(k == 0), stop=(k == LB - 1))
                    m.then_inc(dm_ps, 1)

            transpose_rows(0, 0, s_rd, 1).then_inc(xd_ps, 1)
            with pe.Fori(0, NTD // TD - 1) as c:
                dots_step(c, False)
            dots_step(NTD // TD - 1, True)
            pe.wait_ge(s_dn, DOTS * (NTD // TD))
            mm(acc[1][0:C, 0:P], hitmax[:, :], ones[:, :], start=True, stop=True).then_inc(cnt_ps, 1)
            pe.wait_ge(cs_rdy, 2)
            mm(acc[1][:, :], csel[:, :], onehot[:, :], start=True, stop=True).then_inc(rs_ps, 1)
            pe.wait_ge(cs_rdy, 3)

            def dense_tile(t, n, loads):
                if not (isinstance(t, int) and t + 1 == NT):
                    nxt = n + 1
                    pe.wait_ge(xe_lo, t + 2)
                    transpose_rows(nxt % RB, nxt % 2, s_rl, loads + nxt // RB).then_inc(xe_ps, 1)
                pe.wait_ge(xe_lo, t + 3)
                pe.wait_ge(ft_ev, t + 1)
                e = pe.value_load(tile_id[0:1, bass.ds(t, 1)], min_val=0, max_val=IDS - 1)
                steps = [(a, b, k) for a, b in ((0, 0), (0, 1), (1, 0)) for k in range(LB)]
                for s in steps:
                    a, b, k = s
                    m = mm(acc[n][:, :], xts[n % 2][a][:, k, :],
                           mw[b][:, bass.ds(e, 1), k, :].rearrange("p e f -> p (e f)"),
                           start=s == steps[0], stop=s == steps[-1])
                m.then_inc(ft_ps, 1)

            transpose_rows(0, 0, s_rl, 1).then_inc(xe_ps, 1)
            with pe.Fori(0, NT // RB) as c:
                for n in range(RB):
                    dense_tile(RB * c + n, n, c + 1)
            for t in range(NT // RB * RB, NT):
                dense_tile(t, t % RB, t // RB + 1)


_INS = ["x", "itok_B_78_3631", "itok_B_3_7", "L0_cond_log_dt", "L0_cond_C", "L0_cond_log_A_real", "L0_cond_A_imag",
        "L0_cond_D", "L0_ffn_base_w", "L0_ffn_base_b", "L0_ffn_A", "L0_ffn_B", "L0_ffn_router_w",
        "L1_cond_weight", "L1_ffn_weight", "L1_ffn_bias", "L1_ffn_centroids", "L1_ffn_assignments"]
_OUTS = [((B, H, L), "float32")]


def kernel(**inputs):
    import numpy as _np
    import concourse.bacc as _bacc
    from concourse import mybir as _mybir
    from concourse.bass_utils import run_bass_kernel_spmd as _run

    nc = _bacc.Bacc("TRN2", target_bir_lowering=False, num_devices=1)
    arrays, args = {}, []
    for name in _INS:
        a = _np.ascontiguousarray(inputs[name])
        arrays[f"in_{name}_dram"] = a
        args.append(nc.dram_tensor(f"in_{name}_dram", a.shape, _mybir.dt.from_np(a.dtype), kind="ExternalInput").ap())
    for i, (shape, dtype) in enumerate(_OUTS):
        dt = _mybir.dt.from_np(_np.dtype(dtype))
        args.append(nc.dram_tensor(f"out_{i}_dram", shape, dt, kind="ExternalOutput").ap())
    build(nc, *args)
    r = _run(nc, [arrays], core_ids=[0])
    got = tuple(r.results[0][f"out_{i}_dram"] for i in range(len(_OUTS)))
    return got[0]
```

```python
import math
from contextlib import ExitStack

import concourse.bass as bass
from concourse import mybir

P = 128
B, H, L = 128, 32, 512
LB = L // P
NM = 64
E, R = 16, 64
NP = E * R // P
AR = R + E
IDS = 8
C = 64
GH = 4
NG = H // GH
XB = 3
TB = 4
NT = B // TB + IDS - 1
TD = 8
NTD = -(-NT // TD) * TD
RB = 4
FA, FB = 16, 32
KPITCH = L + P
SCALING = 0.5
MAGIC = 1.5 * 2.0 ** 23
TURN = 6.283185
ROUTE = 24
DOTS = 9
NWT = LB + 1 + NP

F32 = mybir.dt.float32
F32R = mybir.dt.float32r
I32 = mybir.dt.int32
U32 = mybir.dt.uint32
ALU = mybir.AluOpType
ACT = mybir.ActivationFunctionType
AX = mybir.AxisListType.X


def build(nc, x, lengths, adapter_ids, log_dt, ssm_c, log_a_real, a_imag, ssm_d, base_w, base_b,
          lora_a, lora_b, router_w, cond_w, ffn_w, ffn_bias, centroids, assignments, out):
    ctx = ExitStack()

    def sem(name):
        return ctx.enter_context(nc.semaphore(name))

    def alloc(stack, name, shape, dt=F32):
        return stack.enter_context(nc.sbuf_tensor(name, shape, dt))

    k_dram = nc.dram_tensor("k_rev", (2, H, KPITCH), F32, kind="Internal").ap()
    x1_dram = nc.dram_tensor("x1_sorted", (B * H, L), F32, kind="Internal").ap()

    with ctx:
        ident = alloc(ctx, "ident", [P, P])
        tile_id = alloc(ctx, "tile_adapter", [1, NTD], I32)
        tile_src = alloc(ctx, "tile_of_part", [1, NTD], I32)
        sort_row = alloc(ctx, "sorted_row", [P, H], U32)
        sort_now = alloc(ctx, "sorted_row_of_group", [P, GH], U32)
        slot_ok = alloc(ctx, "slot_filled", [P, NTD])
        slot_row = alloc(ctx, "slot_out_row", [P, NTD], U32)
        w_id = [alloc(ctx, f"cond_w_{n}", [P, LB, L]) for n in range(2)]
        f_raw = w_id[0]
        cent_raw = alloc(ctx, "centroids_raw", [C, L])

        l0 = ExitStack()
        bw = [alloc(l0, f"lora_b_{n}", [P, NP, L], F32R) for n in ("hi", "lo")]
        w0 = [alloc(l0, f"base_w_{n}", [P, LB, L], F32R) for n in ("hi", "lo")]
        arw = [alloc(l0, f"a_router_{n}", [P, LB, AR], F32R) for n in ("hi", "lo")]
        xg = [alloc(l0, f"x_group_{n}", [P, GH, L]) for n in range(2)]
        sk = [alloc(l0, f"hankel_{n}", [P, 2, L], F32R) for n in range(GH)]
        uT = [[alloc(l0, f"uT_{m}_{n}", [P, LB, B], F32R) for m in ("hi", "lo")] for n in range(2)]
        y32 = [alloc(l0, f"y_masked_{n}", [P, LB, B]) for n in range(2)]
        yT = [alloc(l0, f"yT_{n}", [P, LB, GH, B], F32R) for n in ("hi", "lo")]
        mask = alloc(l0, "length_mask", [P, LB, B])
        b0_bc = alloc(l0, "base_b_bc", [P, L])
        sel = alloc(l0, "expert_selection", [2 * E, NP, P], F32R)
        res = alloc(l0, "res_hidden", [P, GH * B])
        lgT = alloc(l0, "logitsT", [E, GH * B])
        cst = alloc(l0, "combine_split", [P, GH, 2 * E])
        cTs = alloc(l0, "combineT", [2 * E, GH * B], F32R)
        g32 = [alloc(l0, f"gated_{n}", [P, GH * B]) for n in range(2)]
        gT = [[alloc(l0, f"gatedT_{m}_{n}", [P, GH * B], F32R) for m in ("hi", "lo")] for n in range(2)]
        iota_e = alloc(l0, "expert_marks", [P, E])
        rmax = alloc(l0, "r_max", [P, GH])
        rex = alloc(l0, "r_exp", [P, GH, E])
        rsum = alloc(l0, "r_sum", [P, GH])
        rinv = alloc(l0, "r_inv", [P, GH])
        rprob = alloc(l0, "r_prob", [P, GH, E])
        rtop = alloc(l0, "r_top", [P, 2, GH])
        rmark = alloc(l0, "r_mark", [P, GH])
        rden = alloc(l0, "r_den", [P, GH])
        rw = alloc(l0, "r_weight", [P, 2, GH])
        roh = alloc(l0, "r_onehot", [P, GH, 2, E])
        rcomb = alloc(l0, "r_combine", [P, GH, E])
        w_raw = w_id[0]
        w_rev = w_id[1]
        flat = alloc(l0, "setup", [P, 12 * 1024])
        xg.append(flat[:, 0:GH * L].rearrange("p (i l) -> p i l", i=GH))
        spaces, off = [flat[:, :]], [0]

        def carve(cols, parts=P):
            if off[0] + cols > spaces[0].shape[1]:
                spaces.pop(0)
                off[0] = 0
            off[0] += cols
            return spaces[0][0:parts, off[0] - cols:off[0]]

        ar_raw = carve(L, AR)
        ar_rev = carve(L, AR)
        b_raw = carve(4 * E * R).rearrange("p (a e r) -> p a e r", a=4, e=E)
        modes = carve(4 * P, H).rearrange("p (q n) -> p q n", q=4)
        c_raw = carve(2 * NM, H).rearrange("p (n c) -> p n c", c=2)
        par = carve(4 * H).rearrange("p (q h) -> p q h", q=4)
        dt_bc = carve(H)
        small = carve(32 * H).rearrange("p (q h) -> p q h", q=32)
        phase_off = carve(2)
        bval = carve(FB)
        aval = carve(FA)
        v_ph = carve(H * FB).rearrange("p (h b) -> p h b", h=H)
        tmp = carve(H * FB)
        sel32 = tmp[0:2 * E, :].rearrange("p (j q) -> p j q", j=NP)
        a_tmp = tmp.rearrange("p (q h b) -> p q h b", q=2, h=H)
        v_tmp = tmp.rearrange("p (h b) -> p h b", h=H)
        k32 = tmp[0:FA, :].rearrange("p (h b) -> p h b", h=H)
        v_mag = carve(H * FB).rearrange("p (h b) -> p h b", h=H)
        a_ph = carve(2 * H * FA).rearrange("p (q h b) -> p q h b", q=2, h=H)
        a_mag = carve(H * FA).rearrange("p (h b) -> p h b", h=H)
        d_add = carve(H, FA)
        k_zero = carve(P, H)
        len_i = carve(B).bitcast(I32)
        len_f = carve(B)
        pos = carve(LB)
        spaces += [t[:, :] for t in (res, *g32)] + [t[:, :, :].rearrange("p k b -> p (k b)") for t in y32]
        quad = carve(TB * P).rearrange("p (q r h) -> p q r h", q=TB, r=TB)
        ids_ri = carve(B).bitcast(I32)
        ids_ci = carve(1).bitcast(I32)
        ids_r = carve(B)
        ids_c = carve(2)
        low = carve(B)
        one_s = carve(P)
        same = carve(B)
        rank = carve(2)
        iota8 = carve(IDS)
        oh8 = carve(IDS)
        tri8 = carve(IDS * IDS).rearrange("p (e f) -> p e f", e=IDS)
        prod88 = carve(IDS * IDS).rearrange("p (e f) -> p e f", e=IDS)
        count = carve(IDS)
        start = carve(IDS)
        lo_tile = carve(IDS)
        hi_tile = carve(IDS)
        shift_i = carve(IDS).bitcast(I32)
        n_parts = carve(IDS)
        first_part = carve(IDS)
        oh_at = carve(IDS)
        place = carve(8)
        place_i = carve(1).bitcast(I32)
        first_of = carve(2)
        h_iota = carve(H)
        slot_v = carve(TB * NTD).rearrange("p (q t) -> p q t", q=TB)
        match = carve(TB * NTD).rearrange("p (q t) -> p q t", q=TB)
        h_less = carve(1)
        pad_add = carve(1)
        row_f = carve(NTD)
        row_pad = carve(NTD)
        l0.close()

        l1 = ExitStack()
        mw = [alloc(l1, f"merged_w_{n}", [P, IDS, LB, L], F32R) for n in ("hi", "lo")]
        mc = alloc(l1, "merged_c", [P, IDS, LB, C])
        l1b = ExitStack()
        w_sp = [[alloc(l1b, f"cond_w_{m}_{n}", [P, LB, L], F32R) for m in ("hi", "lo")] for n in range(2)]
        f_w = [alloc(l1b, f"ffn_wT_{n}", [P, LB, L], F32R) for n in ("hi", "lo")]
        f_c = [alloc(l1b, f"centroidsT_{n}", [P, LB, C], F32R) for n in ("hi", "lo")]
        l1b.close()
        rows = [w_id[0][:, n, :] for n in range(RB)]
        outt = [w_id[1][:, n, :] for n in range(RB)]
        xtf = [alloc(l1, f"x1T_{n}", [P, LB, P]) for n in range(2)]
        xts = [[alloc(l1, f"x1T_{m}_{n}", [P, LB, P], F32R) for m in ("hi", "lo")] for n in range(2)]
        dshift = alloc(l1, "dots_shifted", [P, TD, C])
        dexp = alloc(l1, "dots_exp", [P, TD, C])
        hits = alloc(l1, "hits", [P, TD, C])
        row_now = [alloc(l1, f"out_row_of_tile_{n}", [P, 1], U32) for n in range(RB)]
        hitmax = alloc(l1, "hit_any", [P, C])
        hit8 = alloc(l1, "hit_any_of_eight", [P, C])
        dmax = alloc(l1, "dots_max", [P, TD])
        dsum = alloc(l1, "dots_sum", [P, TD])
        dinv = alloc(l1, "dots_inv", [P, TD])
        query = alloc(l1, "query_sel", [P, NTD])
        csel = alloc(l1, "cluster_sel", [C, P])
        onehot = alloc(l1, "assign_onehot", [C, L])
        assign_i = alloc(l1, "assign_i", [C, L], I32)
        assign_f = alloc(l1, "assign_f", [C, L])
        cidx = alloc(l1, "cluster_index", [C, 1])
        ones = alloc(l1, "ones", [P, P])
        rowsel = alloc(l1, "row_sel", [P, L])
        b1_bc = alloc(l1, "ffn_bias_bc", [P, L])
        dense = [alloc(l1, f"dense_{n}", [P, L]) for n in range(2)]
        dsel = [alloc(l1, f"dense_sel_{n}", [P, L]) for n in range(RB)]
        l1.close()

        k_split = [yT[n][0:FA, :, :, :].rearrange("a k i b -> a (k i b)")[:, 0:H * FB]
                   .rearrange("a (h b) -> a h b", h=H) for n in range(2)]

        def bank(name):
            return ctx.enter_context(nc.psum_tensor(name, [P, 512], F32))

        acc = [bank(f"acc{i}") for i in range(GH)]
        wb = [bank(f"work{i}") for i in range(2)]
        bb = [bank(f"bcast{i}") for i in range(2)]

        s_par = sem("params_loaded")
        s_ids = sem("ids_loaded")
        s_len = sem("lengths_loaded")
        s_db = sem("d_and_base_b_loaded")
        s_w0l = sem("base_w_loaded")
        s_arl = sem("a_router_loaded")
        s_bl = sem("lora_b_loaded")
        s_cst = sem("pool_constants_ready")
        s_id = sem("ident_ready")
        s_pool = sem("pool_chain")
        s_dve = sem("dve_setup_chain")
        s_rt = sem("dve_routing_chain")
        s_dn = sem("dve_layer1_chain")
        s_stk = sem("mode_stack_ready")
        s_kps_par = sem("params_in_psum")
        s_parT = sem("params_transposed")
        s_sort = sem("sort_inputs_ready")
        t_cnt = sem("adapter_counts_in_psum")
        t_mat = sem("slots_matched")
        t_tab = sem("slot_tables_in_psum")
        t_rdy = sem("slot_tables_ready")
        sn_rdy = sem("sorted_rows_of_group_ready")
        s_dt = sem("dt_and_decay_ready")
        s_t0 = sem("turns_ready")
        s_mag = sem("decay_exponents_ready")
        s_mags = sem("decays_ready")
        s_fr = sem("phases_ready")
        s_sin = sem("sines_ready")
        s_uv = sem("mode_factors_ready")
        s_kps = sem("kernels_in_psum")
        s_khi = sem("kernels_hi")
        s_klo = sem("kernels_lo")
        s_kst = sem("kernels_stored")
        s_rev = sem("weights_reversed")
        s_wps = sem("weights_in_psum")
        s_whi = sem("weights_hi")
        s_wlo = sem("weights_lo")
        s_x = [[sem(f"x_loaded_{n}_{i}") for i in range(GH)] for n in range(XB)]
        s_sk = [sem(f"hankel_loaded_{n}") for n in range(GH)]
        u_ps = sem("u_in_psum")
        u_hi = sem("u_hi")
        u_lo = sem("u_lo")
        y_ps = sem("y_in_psum")
        y_ms = sem("y_masked")
        y_hi = sem("y_hi")
        y_lo = sem("y_lo")
        ar_ps = sem("ar_in_psum")
        ar_ev = sem("ar_evacuated")
        lt_ps = sem("logits_in_psum")
        r_sub = sem("logits_shifted")
        r_exp = sem("logits_exp")
        c_rdy = sem("combine_ready")
        ct_ps = sem("combineT_in_psum")
        ct_sb = sem("combineT_ready")
        bc_ps = sem("gates_in_psum")
        g_mul = sem("gated_ready")
        g_hi = sem("gated_hi")
        g_lo = sem("gated_lo")
        d_done = sem("experts_added")
        b_done = sem("base_added")
        a_done = sem("head_accumulated")
        xb_rdy = sem("x_plus_bias")
        x1_rdy = sem("x1_ready")
        x1_st = [sem(f"x1_stored_{n}") for n in range(XB)]
        s_fwl = sem("ffn_w_loaded")
        s_cwl = [sem(f"cond_w_loaded_{n}") for n in range(2)]
        cw_hi = sem("cond_w_hi")
        cw_lo = sem("cond_w_lo")
        m_ps = sem("merged_in_psum")
        m_hi = sem("merged_hi")
        m_lo = sem("merged_lo")
        mc_ps = sem("merged_c_in_psum")
        mc_ev = sem("merged_c_ready")
        s_l1l = sem("layer1_rows_loaded")
        s_l1c = sem("layer1_consts")
        s_rd = [sem(f"dots_rows_loaded_{n}") for n in range(RB)]
        xd_ps = sem("dots_x1T_in_psum")
        xd_ev = sem("dots_x1T_ready")
        dm_ps = sem("dots_in_psum")
        dt_sh = sem("dots_shifted_ready")
        dt_exp = sem("dots_exp_ready")
        cnt_ps = sem("hit_counts_in_psum")
        cs_rdy = sem("cluster_sel_ready")
        rs_ps = sem("row_sel_in_psum")
        s_rl = [sem(f"rows_loaded_{n}") for n in range(RB)]
        xe_ps = sem("x1T_in_psum")
        xe_hi = sem("x1T_hi")
        xe_lo = sem("x1T_lo")
        ft_ps = sem("dense_in_psum")
        ft_ev = sem("dense_evacuated")
        ft_sel = sem("dense_selected")
        o_rdy = sem("out_tile_ready")
        row_rdy = sem("out_rows_of_tile_ready")
        s_out = [sem(f"out_stored_{n}") for n in range(RB)]

        block = ctx.enter_context(nc.Block())

        def weight_out(k, part):
            if k < NP:
                return bw[part][:, k, :]
            if k < NP + LB:
                return w0[part][:, k - NP, :]
            if k < NWT:
                return arw[part][:, :, :]
            if k < NWT + LB:
                return f_w[part][:, k - NWT, :]
            return f_c[part][:, :, :]

        def weight_in_psum(k, cols):
            src = acc[k % GH][:, 0:cols]
            return src.rearrange("p (k c) -> p k c", k=LB) if k in (NWT - 1, NWT + LB) else src

        class Chain:

            def __init__(self, eng, s, base=0):
                self.eng, self.s, self.base, self.n = eng, s, base, 0
                self.others = {}

            def after(self, ins, other=None):
                if other is not None:
                    self.others[other.name] = self.others.get(other.name, 0) + 1
                    ins.then_inc(other, 1)
                    self.eng.wait_ge(other, self.others[other.name])
                    return
                self.n += 1
                ins.then_inc(self.s, 1)
                self.eng.wait_ge(self.s, self.base + self.n)

        def load_x(sp, n, i, g):
            sp.dma_start(xg[n][:, i, :], x[:, bass.ds(GH * g + i, 1), :].rearrange("b h l -> b (h l)")
                         ).then_inc(s_x[n][i], 16)

        hankel = bass.AP(k_dram.tensor, 0, [[1, P], [H * KPITCH, 2], [KPITCH, H], [1, L]])

        def load_hankel(sp, g, i):
            sp.dma_start(sk[i][:, :, :].bitcast(F32), hankel[:, :, bass.ds(GH * g + i, 1), :].rearrange("p s h l -> p s (h l)")
                         ).then_inc(s_sk[i], 16)

        @block.sync
        def _(sp):
            def twice(t):
                return bass.AP(t.tensor, 0, [[NM, H], [0, 2], [1, NM]])

            sp.dma_start(ids_ri, bass.AP(adapter_ids.tensor, 0, [[0, P], [1, B]])).then_inc(s_ids, 16)
            sp.dma_start(ids_ci, adapter_ids.rearrange("(b a) -> b a", a=1)).then_inc(s_ids, 16)
            sp.dma_start(modes[:, 0, :], twice(log_a_real)).then_inc(s_par, 16)
            sp.dma_start(modes[:, 1, :], twice(a_imag)).then_inc(s_par, 16)
            sp.dma_start(c_raw, ssm_c).then_inc(s_par, 16)
            sp.dma_start(dt_bc, bass.AP(log_dt.tensor, 0, [[0, P], [1, H]])).then_inc(s_par, 16)
            sp.dma_start(len_i, bass.AP(lengths.tensor, 0, [[0, P], [1, B]])).then_inc(s_len, 16)
            for a in range(4):
                sp.dma_start(b_raw[:, a, :, :], lora_b[:, P * a:P * a + P, :].rearrange("e p r -> p e r")
                             ).then_inc(s_bl, 16)
            sp.dma_start(w_raw[:, :, :], base_w.rearrange("(a p) l -> p a l", p=P)).then_inc(s_w0l, 16)
            sp.dma_start(ar_raw[0:R, :], lora_a).then_inc(s_arl, 16)
            sp.dma_start(ar_raw[R:AR, :], router_w).then_inc(s_arl, 16)
            for i in range(GH):
                load_x(sp, 0, i, 0)
            sp.wait_ge(s_cst, 1)
            sp.dma_start(d_add[FA - 1:FA, :], ssm_d.rearrange("(a h) -> a h", a=1)).then_inc(s_db, 16)
            sp.dma_start(b0_bc[:, :], bass.AP(base_b.tensor, 0, [[0, P], [1, L]])).then_inc(s_db, 16)
            for i in range(GH):
                load_x(sp, 1, i, 1)
            sp.wait_ge(s_klo, 1)
            for n in range(2):
                dst = bass.AP(k_dram.tensor, n * H * KPITCH, [[FB, FA], [KPITCH, H], [1, FB]])
                sp.dma_start(dst, k_split[n].bitcast(F32)).then_inc(s_kst, 16)
                dst0 = bass.AP(k_dram.tensor, n * H * KPITCH + L, [[KPITCH, H], [1, P]])
                sp.dma_start(dst0, k_zero).then_inc(s_kst, 16)
            sp.wait_ge(s_kst, 64)
            for i in range(GH):
                load_hankel(sp, 0, i)

            cw = cond_w.rearrange("e (a p) k -> e p a k", p=P)
            sp.wait_ge(s_rev, 4)
            sp.wait_ge(s_wps, NP + LB)
            sp.dma_start(f_raw[:, :, :], ffn_w.rearrange("(a p) o -> p a o", p=P)).then_inc(s_fwl, 16)
            sp.dma_start(cent_raw[:, :], centroids).then_inc(s_fwl, 16)
            sp.dma_start(w_id[1][:, :, :], cw[1, :, :, :]).then_inc(s_cwl[1], 16)

            def hankels(g):
                for i in range(GH):
                    sp.wait_ge(y_ps, GH * g + i - GH + 1)
                    load_hankel(sp, g, i)

            sp.wait_ge(s_wps, NWT)
            with sp.Fori(0, (NG - 2) // XB) as t:
                for n in range(XB):
                    g = XB * t + n
                    hankels(g + 1)
                    sp.wait_ge(sn_rdy, g + 1)
                    for i in range(GH):
                        load_x(sp, (n + 2) % XB, i, g + 2)
            hankels(NG - 1)
            sp.wait_ge(s_wps, NWT + LB)
            sp.dma_start(w_id[0][:, :, :], cw[0, :, :, :]).then_inc(s_cwl[0], 16)
            with sp.Fori(1, IDS // 2) as t:
                for n in range(2):
                    sp.wait_ge(cw_lo, 2 * t + n - 1)
                    sp.dma_start(w_id[n][:, :, :],
                                 cw[bass.ds(2 * t + n, 1), :, :, :].rearrange("e p a k -> p (e a) k")
                                 ).then_inc(s_cwl[n], 16)
            sp.wait_ge(mc_ps, IDS)
            sp.dma_start(b1_bc[:, :], bass.AP(ffn_bias.tensor, 0, [[0, P], [1, L]])).then_inc(s_l1l, 16)
            sp.dma_start(assign_i[:, :], bass.AP(assignments.tensor, 0, [[0, C], [1, L]])).then_inc(s_l1l, 16)
            for n in range(XB):
                sp.wait_ge(x1_st[n], 16 * GH * len(range(n, NG, XB)))
            sp.wait_ge(t_rdy, 5)
            x1_tiles = x1_dram.rearrange("(t p) l -> t p l", p=P)

            def load_rows(t, n, s):
                src = sp.value_load(tile_src[0:1, bass.ds(t, 1)], min_val=0, max_val=B // TB - 1)
                sp.dma_start(rows[n], x1_tiles[bass.ds(src, 1), :, :].rearrange("t p l -> (t p) l")
                             ).then_inc(s[n], 16)

            for n in range(RB):
                load_rows(n, n, s_rd)
            with sp.Fori(1, NTD // RB) as c:
                for n in range(RB):
                    sp.wait_ge(xd_ps, RB * c + n - RB + 1)
                    load_rows(RB * c + n, n, s_rd)
            sp.wait_ge(xd_ps, NTD)
            for n in range(RB):
                load_rows(n, n, s_rl)
            with sp.Fori(1, NT // RB) as c:
                for n in range(RB):
                    sp.wait_ge(o_rdy, RB * c + n + 1)
                    load_rows(RB * c + n, n, s_rl)
            for t in range(NT // RB * RB, NT):
                sp.wait_ge(o_rdy, t + 1)
                load_rows(t, t % RB, s_rl)
            for n in range(RB):
                sp.wait_ge(s_out[n], 16 * len(range(n, NT, RB)))

        @block.gpsimd
        def _(pool):
            g = nc.gpsimd
            pool.sem_inc(o_rdy, RB)
            chain = Chain(pool, s_pool)
            imprecise = dict(allow_small_or_imprecise_dtypes=True)
            chain.after(g.iota(iota8, [[1, IDS]], base=0, channel_multiplier=0, **imprecise), s_sort)
            chain.after(g.memset(low, 1.0))
            chain.after(g.affine_select(out=low, in_=low, compare_op=ALU.is_ge, fill=0.0, base=-1, pattern=[[-1, B]],
                            channel_multiplier=1), s_sort)
            chain.after(g.memset(one_s, 1.0), s_sort)
            chain.after(g.memset(tri8, 1.0))
            chain.after(g.affine_select(out=tri8, in_=tri8, compare_op=ALU.is_ge, fill=0.0, base=-1,
                            pattern=[[1, IDS], [-1, IDS]], channel_multiplier=0), s_sort)
            chain.after(g.memset(ident[:, :], 0.0))
            chain.after(g.affine_select(out=ident[:, :], in_=ident[:, :], compare_op=ALU.not_equal, fill=1.0, base=0,
                            pattern=[[-1, P]], channel_multiplier=1), s_id)
            chain.after(g.iota(slot_v, [[1, TB], [TB, NTD]], base=0, channel_multiplier=0, **imprecise), s_sort)
            chain.after(g.iota(h_iota, [[1, H]], base=0, channel_multiplier=0, **imprecise), s_sort)
            chain.after(g.iota(quad, [[0, TB], [0, TB], [0, H]], base=1, channel_multiplier=1, **imprecise))
            chain.after(g.affine_select(out=quad, in_=quad, compare_op=ALU.is_equal, fill=0.0, base=0,
                            pattern=[[1, TB], [-1, TB], [0, H]], channel_multiplier=0), s_sort)
            for q in range(TB):
                chain.after(g.iota(h_less[H * q:H * q + H, :], [[0, 1]], base=-H, channel_multiplier=1,
                       **imprecise), s_sort)
                chain.after(g.memset(pad_add[H * q:H * q + H, :], float((B + 1 + q) * H)), s_sort)
            chain.after(g.memset(d_add, 0.0))
            chain.after(g.memset(phase_off[0:NM, :], 0.25), s_cst)
            chain.after(g.memset(phase_off[NM:P, :], 0.0), s_cst)
            chain.after(g.iota(bval, [[-1, FB]], base=FB - 1, channel_multiplier=0, **imprecise), s_cst)
            chain.after(g.iota(aval, [[-1, FA]], base=FA - 1, channel_multiplier=0, **imprecise), s_cst)
            chain.after(g.iota(pos, [[P, LB]], base=P - 1, channel_multiplier=-1, **imprecise), s_cst)
            chain.after(g.memset(k_zero, 0.0))
            chain.after(g.iota(iota_e[:, :], [[-1, E]], base=E, channel_multiplier=0, **imprecise), s_cst)
            pool.wait_ge(s_w0l, 16)
            for a in range(4):
                g.tensor_copy(w_rev[:, a, :].rearrange("p (k q) -> p k q", q=P),
                              w_raw[:, a, :].rearrange("p (k q) -> p k q", q=P)[:, :, ::-1]).then_inc(s_rev, 1)
            pool.wait_ge(s_arl, 32)
            g.tensor_copy(ar_rev.rearrange("p (k q) -> p k q", q=P),
                          ar_raw.rearrange("p (k q) -> p k q", q=P)[:, :, ::-1]).then_inc(s_rev, 1)
            pool.wait_ge(s_klo, 1)
            chain.after(g.memset(sel32, 0.0))
            sv = sel32.rearrange("k j (e r) -> k j e r", e=2)
            for part in range(2):
                chain.after(g.affine_select(out=sv, in_=sv, compare_op=ALU.not_equal, fill=1.0, base=-E * part,
                                            pattern=[[-2, NP], [-1, 2], [0, R]], channel_multiplier=1))
            chain.after(g.tensor_copy(sel[:, :, :], sel32), s_cst)

            def y_low(h, i):
                pool.wait_ge(y_hi, h + 1)
                g.tensor_tensor(yT[1][:, :, i, :], y32[i % 2][:, :, :], yT[0][:, :, i, :].bitcast(F32),
                                ALU.subtract).then_inc(y_lo, 1)

            def x_bias(h, n, i):
                pool.wait_ge(u_ps, h + 1)
                g.tensor_tensor(xg[n][:, i, :], xg[n][:, i, :], b0_bc[:, :], ALU.add).then_inc(xb_rdy, 1)

            def g_low(gr, j):
                pool.wait_ge(g_hi, NP * gr + j + 1)
                g.tensor_tensor(gT[j % 2][1][:, :], g32[j % 2][:, :], gT[j % 2][0][:, :].bitcast(F32),
                                ALU.subtract).then_inc(g_lo, 1)

            pool.wait_ge(t_rdy, 5)
            pool.wait_ge(s_db, 32)
            last_row = pool.to_reg(B * H - 1)
            for i in range(GH):
                y_low(i, i)
                x_bias(i, 0, i)

            def sorted_rows(gr):
                g.tensor_copy(sort_now[:, :], sort_row[:, bass.ds(GH * gr, GH)]).then_inc(sn_rdy, 1)

            def scatter(gr, n, last):
                pool.wait_ge(x1_rdy, GH * gr + GH + GH)
                pool.wait_ge(sn_rdy, gr + 1)
                if not last:
                    x_bias(GH * gr + 2 * GH - 1, (n + 1) % XB, GH - 1)
                for i in range(GH):
                    g.indirect_dma_start(x1_dram, bass.IndirectOffsetOnAxis(ap=sort_now[:, i:i + 1], axis=0),
                                         xg[n][:, i, :], None, bounds_check=last_row, oob_is_err=False
                                         ).then_inc(x1_st[n], 16)

            def group(gr, n, stores):
                first, last = isinstance(gr, int) and gr == 0, isinstance(gr, int) and gr == NG - 1
                nxt = GH * gr + GH
                if not first:
                    scatter(gr - 1, (n - 1) % XB, False)
                if not last:
                    y_low(nxt, 0)
                g_low(gr, 0)
                g_low(gr, 1)
                for i in range(1, GH):
                    if not last:
                        y_low(nxt + i, i)
                    g_low(gr, i + 1)
                    if i == 1 and not first:
                        pool.wait_ge(x1_st[(n - 1) % XB], 16 * GH * stores)
                        sorted_rows(gr)
                for i in range(GH - 1):
                    if not last:
                        x_bias(nxt + i, (n + 1) % XB, i)
                    g_low(gr, i + 5)

            sorted_rows(0)
            group(0, 0, 0)
            with pool.Fori(0, (NG - 2) // XB) as t:
                for n in range(XB):
                    group(XB * t + n + 1, (n + 1) % XB, t + 1)
            group(NG - 1, (NG - 1) % XB, (NG - 2) // XB + 1)
            scatter(NG - 1, (NG - 1) % XB, True)
            pool.wait_ge(mc_ps, IDS)
            g.memset(ones[:, :], 1.0).then_inc(s_l1c, 1)
            g.memset(hitmax[:, :], 0.0).then_inc(s_l1c, 1)
            g.iota(cidx[:, :], [[0, 1]], base=0, channel_multiplier=1, **imprecise).then_inc(s_l1c, 1)
            out_rows = out.rearrange("b h l -> (b h) l")

            def next_row(t, n, stores):
                if not (isinstance(stores, int) and stores == 0):
                    pool.wait_ge(s_out[n], 16 * stores)
                g.tensor_copy(row_now[n][:, :], slot_row[:, bass.ds(t, 1)]).then_inc(row_rdy, 1)

            def finish(t, n, loads):
                pool.wait_ge(ft_sel, t + 1)
                pool.wait_ge(s_rl[n], 16 * loads)
                pool.wait_ge(row_rdy, t + 1)
                g.tensor_tensor(outt[n], dsel[n][:, :], rows[n], ALU.add).then_inc(o_rdy, 1)
                pool.wait_ge(o_rdy, t + RB + 1)
                next_row(t + 1, (n + 1) % RB, loads - 1 + (n + 1) // RB)
                g.indirect_dma_start(out_rows, bass.IndirectOffsetOnAxis(ap=row_now[n][:, 0:1], axis=0),
                                     outt[n], None, bounds_check=last_row, oob_is_err=False
                                     ).then_inc(s_out[n], 16)

            next_row(0, 0, 0)
            for t in range(RB):
                finish(t, t, 1)
            with pool.Fori(1, NT // RB) as c:
                for n in range(RB):
                    finish(RB * c + n, n, c + 1)
            for t in range(NT // RB * RB, NT):
                finish(t, t % RB, t // RB + 1)

        S = {name: small[:, k, :] for k, name in enumerate(
            "dt ear th nal tu tr t0 ea tnh sn sh em1 t1 t2 t3 er1 ei den rden gr gi cr ci k1 k2 u32 r32 t32".split())}

        @block.scalar
        def _(act):
            a = nc.scalar
            act.sem_inc(xd_ev, 2)
            act.wait_ge(s_par, 64)
            a.activation(S["dt"], dt_bc, ACT.Exp).then_inc(s_dt, 1)
            act.wait_ge(s_parT, 1)
            a.activation(S["ear"], par[:, 0, :], ACT.Exp).then_inc(s_dt, 1)
            act.wait_ge(s_t0, 1)
            a.activation(S["ea"], S["nal"], ACT.Exp, scale=-1.0).then_inc(s_mags, 1)
            a.activation(S["tnh"], S["nal"], ACT.Tanh, scale=-0.5).then_inc(s_mags, 1)
            act.wait_ge(s_mag, 2)
            a.activation(v_mag, v_mag, ACT.Exp, scale=-1.0).then_inc(s_mags, 1)
            a.activation(a_mag, a_mag, ACT.Exp, scale=-float(FB)).then_inc(s_mags, 1)
            act.wait_ge(s_t0, 2)
            a.activation(S["sn"], S["t0"], ACT.Sin, scale=TURN).then_inc(s_sin, 1)
            a.activation(S["sh"], S["t0"], ACT.Sin, scale=TURN / 2).then_inc(s_sin, 1)
            act.wait_ge(s_fr, 1)
            a.activation(a_ph, a_ph, ACT.Sin, scale=TURN).then_inc(s_sin, 1)
            act.wait_ge(s_fr, 2)
            a.activation(v_ph, v_ph, ACT.Sin, scale=TURN).then_inc(s_sin, 1)

            for k in range(NWT):
                act.wait_ge(s_wps, k + 1)
                cols = LB * AR if k == NWT - 1 else L
                a.activation(weight_out(k, 0), weight_in_psum(k, cols), ACT.Copy).then_inc(s_whi, 1)

            def u_high(h, i, first=False):
                act.wait_ge(u_ps, h + 1)
                if not (first and i < 2):
                    act.wait_ge(y_ps, h - 1)
                a.activation(uT[i % 2][0][:, :, :], wb[0][:, :], ACT.Copy).then_inc(u_hi, 1)

            def y_high(h, i, first=False):
                act.wait_ge(y_ms, h + 1)
                if not first:
                    act.wait_ge(b_done, h - GH + 1)
                a.activation(yT[0][:, :, i, :], y32[i % 2][:, :, :], ACT.Copy).then_inc(y_hi, 1)

            def ar_evac(gr):
                act.wait_ge(ar_ps, gr + 1)
                a.activation(lgT[:, :], wb[0][R:AR, :], ACT.Copy).then_inc(ar_ev, 1)
                a.activation(res[0:R, :], wb[0][0:R, :], ACT.Copy).then_inc(ar_ev, 1)

            def g_high(gr, j):
                act.wait_ge(g_mul, NP * gr + j + 1)
                if j >= 2:
                    act.wait_ge(d_done, (NP - 1) * gr + j - 1)
                a.activation(gT[j % 2][0][:, :], g32[j % 2][:, :], ACT.Copy).then_inc(g_hi, 1)

            u_high(0, 0, True)
            for i in range(GH):
                if i + 1 < GH:
                    u_high(i + 1, i + 1, True)
                y_high(i, i, True)
            ar_evac(0)

            def group(gr, last):
                nxt = GH * gr + GH
                act.wait_ge(r_sub, gr + 1)
                a.activation(rex[:, :, :], rex[:, :, :], ACT.Exp).then_inc(r_exp, 1)
                if not last:
                    u_high(nxt, 0)
                    y_high(nxt, 0)
                    u_high(nxt + 1, 1)
                act.wait_ge(ct_ps, gr + 1)
                a.activation(cTs[:, :], bb[1][0:2 * E, :], ACT.Copy).then_inc(ct_sb, 1)
                g_high(gr, 0)
                g_high(gr, 1)
                for i in range(1, GH):
                    if not last:
                        y_high(nxt + i, i)
                        if i + 1 < GH:
                            u_high(nxt + i + 1, i + 1)
                    g_high(gr, i + 1)
                for j in range(GH + 1, NP):
                    g_high(gr, j)
                if not last:
                    ar_evac(gr + 1)
            with act.Fori(0, NG - 1) as gr:
                group(gr, False)
            group(NG - 1, True)
            for n in range(XB):
                act.wait_ge(x1_st[n], 16 * GH * len(range(n, NG, XB)))
            for k in range(NWT, NWT + LB + 1):
                act.wait_ge(s_wps, k + 1)
                cols = LB * C if k == NWT + LB else L
                a.activation(weight_out(k, 0), weight_in_psum(k, cols), ACT.Copy).then_inc(s_whi, 1)

            def split(e, n, first):
                act.wait_ge(s_cwl[n], 16 if first else (e - n) * 8 + 16)
                if not first:
                    act.wait_ge(mc_ps, e - 1)
                a.activation(w_sp[n][0][:, :, :], w_id[n][:, :, :], ACT.Copy).then_inc(cw_hi, 1)

            def merged(e):
                for k in range(LB):
                    act.wait_ge(m_ps, LB * e + k + 1)
                    a.activation(mw[0][:, bass.ds(e, 1), k, :].rearrange("p e f -> p (e f)"), acc[k][:, :],
                                 ACT.Copy).then_inc(m_hi, 1)

            split(0, 0, True)
            split(1, 1, True)
            with act.Fori(0, IDS // 2 - 1) as t:
                for n in range(2):
                    merged(2 * t + n)
                    split(2 * t + n + 2, n, False)
            merged(IDS - 2)
            merged(IDS - 1)

            def dots_x(t, n):
                act.wait_ge(xd_ps, t + 1)
                a.activation(xtf[n][:, :, :], wb[n][:, :], ACT.Copy).then_inc(xd_ev, 1)

            def dots_step(c, last):
                for w in range(TD - 1 if last else TD):
                    dots_x(c * TD + w + 1, (w + 1) % 2)
                act.wait_ge(dt_sh, c + 2)
                a.activation(dexp[:, :, :], dshift[:, :, :], ACT.Exp, scale=10.0).then_inc(dt_exp, 1)

            act.wait_ge(mc_ps, IDS)
            dots_x(0, 0)
            with act.Fori(0, NTD // TD - 1) as c:
                dots_step(c, False)
            dots_step(NTD // TD - 1, True)

            def dense_x(t, n):
                act.wait_ge(xe_ps, t + 1)
                a.activation(xts[n][0][:, :, :], wb[n][:, :], ACT.Copy).then_inc(xe_hi, 1)

            dense_x(0, 0)
            with act.Fori(0, NT // RB) as c:
                for n in range(RB):
                    dense_x(RB * c + n + 1, (n + 1) % 2)
            for t in range(NT // RB * RB + 1, NT):
                dense_x(t, t % 2)

        @block.vector
        def _(dve):
            v = nc.vector
            dve.sem_inc(x1_rdy, GH)
            dve.sem_inc(dt_sh, 1)
            dve.sem_inc(xe_lo, 2)
            dve.sem_inc(ft_ev, RB)
            chain = Chain(dve, s_dve)
            dve.wait_ge(s_ids, 32)
            dve.wait_ge(s_sort, 4)
            chain.after(v.tensor_copy(ids_r, ids_ri))
            chain.after(v.tensor_copy(ids_c[:, 0:1], ids_ci))
            chain.after(v.tensor_scalar(same, ids_r, ids_c[:, 0:1], None, ALU.is_equal))
            chain.after(v.tensor_tensor(same, same, low, ALU.mult))
            chain.after(v.reduce_sum(rank[:, 0:1], same, AX))
            v.tensor_scalar(oh8, iota8, ids_c[:, 0:1], None, ALU.is_equal).then_inc(t_mat, 1)
            dve.wait_ge(t_cnt, 1)
            chain.after(v.tensor_copy(count, wb[0][:, 0:IDS]))

            def before(t, of):
                chain.after(v.tensor_tensor(prod88, tri8, of.rearrange("p (o e) -> p o e", o=1)
                                            .broadcast_to([P, IDS, IDS]), ALU.mult))
                chain.after(v.reduce_sum(t, prod88, AX))

            def tile_of(t, of, of_i, extra):
                chain.after(v.tensor_scalar(of_i, of, float(extra), None, ALU.add))
                chain.after(v.tensor_scalar(of_i, of_i, 2, None, ALU.arith_shift_right))
                chain.after(v.tensor_copy(t, of_i))

            def mine(t, of):
                chain.after(v.tensor_tensor(oh_at, of, oh8, ALU.mult))
                chain.after(v.reduce_sum(t, oh_at, AX))

            before(start, count)
            tile_of(lo_tile, start, shift_i, 0)
            chain.after(v.tensor_tensor(hi_tile, start, count, ALU.add))
            tile_of(hi_tile, hi_tile, shift_i, TB - 1)
            chain.after(v.tensor_tensor(hi_tile, hi_tile, lo_tile, ALU.subtract))
            chain.after(v.scalar_tensor_tensor(n_parts, count, 1.0, hi_tile, ALU.min, ALU.mult))
            dve.wait_ge(s_par, 64)
            for q in range(2):
                for half in range(2):
                    v.tensor_copy(modes[:, 2 + q, NM * half:NM * half + NM], c_raw[:, :, q]).then_inc(s_stk, 1)
            before(first_part, n_parts)
            dve.wait_ge(t_mat, 1)
            mine(place[:, 3:4], start)
            chain.after(v.tensor_tensor(place[:, 0:1], place[:, 3:4], rank[:, 0:1], ALU.add))
            tile_of(place[:, 1:2], place[:, 0:1], place_i, 0)
            chain.after(v.tensor_tensor(first_part, first_part, lo_tile, ALU.subtract))
            mine(place[:, 4:5], first_part)
            chain.after(v.scalar_tensor_tensor(place[:, 2:3], place[:, 4:5], float(TB), place[:, 0:1],
                                               ALU.mult, ALU.add))
            chain.after(v.tensor_scalar(place[:, 5:6], place[:, 0:1], float(H), None, ALU.mult))
            dve.wait_ge(s_sort, 7 + 2 * TB)
            v.tensor_scalar(sort_row[:, :], h_iota, place[:, 5:6], None, ALU.add).then_inc(t_rdy, 1)
            chain.after(v.scalar_tensor_tensor(place[:, 6:7], place[:, 1:2], -float(TB), place[:, 0:1],
                                               ALU.mult, ALU.add))
            chain.after(v.tensor_tensor(place[:, 6:7], place[:, 6:7], rank[:, 0:1], ALU.min))
            chain.after(v.tensor_scalar(place[:, 6:7], place[:, 6:7], 0.0, None, ALU.is_equal))
            chain.after(v.tensor_tensor(first_of[:, 0:1], place[:, 6:7], ids_c[:, 0:1], ALU.mult))
            chain.after(v.tensor_tensor(first_of[:, 1:2], place[:, 6:7], place[:, 1:2], ALU.mult))
            v.tensor_scalar(match, slot_v, place[:, 2:3], None, ALU.is_equal).then_inc(t_mat, 1)
            dve.wait_ge(t_tab, 1)
            slot1 = wb[1][:, 0:NTD]
            v.tensor_scalar(slot_ok[:, :], slot1, 0.5, None, ALU.is_gt).then_inc(t_rdy, 1)
            chain.after(v.tensor_scalar(row_f, slot1, float(H), h_less, ALU.mult, ALU.add))
            chain.after(v.tensor_scalar(row_pad, slot1, 0.5, pad_add, ALU.is_lt, ALU.mult))
            v.tensor_tensor(slot_row[:, :], row_f, row_pad, ALU.add).then_inc(t_rdy, 1)
            v.tensor_copy(tile_id[:, :], wb[0][0:1, 64:64 + NTD]).then_inc(t_rdy, 1)
            v.tensor_copy(tile_src[:, :], wb[0][0:1, 128:128 + NTD]).then_inc(t_rdy, 1)

            dve.wait_ge(s_len, 16)
            chain.after(v.tensor_copy(len_f, len_i))
            dve.wait_ge(s_cst, 6)
            for k in range(LB):
                chain.after(v.tensor_scalar(mask[:, k, :], len_f, pos[:, k:k + 1], None, ALU.is_gt))
            dve.wait_ge(s_kps_par, 1)
            v.tensor_copy(par, bb[0][:, 0:4 * H].rearrange("p (q h) -> p q h", q=4)).then_inc(s_parT, 1)
            dve.wait_ge(s_parT, 1)
            dve.wait_ge(s_dt, 2)

            def tt(o, x0, x1, op):
                chain.after(v.tensor_tensor(S.get(o, o) if isinstance(o, str) else o,
                                            S[x0] if isinstance(x0, str) else x0,
                                            S[x1] if isinstance(x1, str) else x1, op))

            def ts(o, x0, s0, s1, op0, op1):
                chain.after(v.tensor_scalar(S[o] if isinstance(o, str) else o,
                                            S[x0] if isinstance(x0, str) else x0, s0, s1, op0, op1))

            aim = par[:, 1, :]
            v.tensor_tensor(S["nal"], S["ear"], S["dt"], ALU.mult).then_inc(s_t0, 1)
            dve.wait_ge(s_t0, 1)
            tt("th", aim, "dt", ALU.mult)
            ts("tu", "th", 1.0 / (2.0 * math.pi), None, ALU.mult, ALU.bypass)
            ts("tr", "tu", MAGIC, MAGIC, ALU.add, ALU.subtract)
            v.tensor_tensor(S["t0"], S["tu"], S["tr"], ALU.subtract).then_inc(s_t0, 1)
            dve.wait_ge(s_t0, 2)

            def bc(t, n):
                return t.rearrange("p (h o) -> p h o", o=1).broadcast_to([P, H, n])

            def row(t, n):
                return t.rearrange("p (o b) -> p o b", o=1).broadcast_to([P, H, n])

            v.tensor_tensor(v_mag, bc(S["nal"], FB), row(bval, FB), ALU.mult).then_inc(s_mag, 1)
            v.tensor_tensor(a_mag, bc(S["nal"], FA), row(aval, FA), ALU.mult).then_inc(s_mag, 1)
            ts("u32", "t0", float(FB), None, ALU.mult, ALU.bypass)
            ts("r32", "u32", MAGIC, MAGIC, ALU.add, ALU.subtract)
            tt("t32", "u32", "r32", ALU.subtract)
            chain.after(v.tensor_tensor(a_ph[:, 1, :, :], bc(S["t32"], FA), row(aval, FA), ALU.mult))
            chain.after(v.tensor_scalar(a_ph[:, 0, :, :], a_ph[:, 1, :, :], 0.25, None, ALU.add))
            chain.after(v.tensor_scalar(a_tmp, a_ph, MAGIC, MAGIC, ALU.add, ALU.subtract))
            v.tensor_tensor(a_ph, a_ph, a_tmp, ALU.subtract).then_inc(s_fr, 1)
            chain.after(v.tensor_tensor(v_ph, bc(S["t0"], FB), row(bval, FB), ALU.mult))
            chain.after(v.tensor_scalar(v_ph, v_ph, phase_off[:, 0:1], None, ALU.add))
            dve.wait_ge(s_fr, 1)
            chain.after(v.tensor_scalar(v_tmp, v_ph, MAGIC, MAGIC, ALU.add, ALU.subtract))
            v.tensor_tensor(v_ph, v_ph, v_tmp, ALU.subtract).then_inc(s_fr, 1)
            dve.wait_ge(s_mags, 2)
            chain.after(v.scalar_tensor_tensor(S["em1"], S["ea"], 1.0, S["tnh"], ALU.add, ALU.mult))
            dve.wait_ge(s_sin, 2)
            tt("t1", "sh", "sh", ALU.mult)
            tt("t2", "t1", "ea", ALU.mult)
            chain.after(v.scalar_tensor_tensor(S["er1"], S["t2"], -2.0, S["em1"], ALU.mult, ALU.add))
            tt("ei", "ea", "sn", ALU.mult)
            tt("t1", "ear", "ear", ALU.mult)
            tt("t2", aim, aim, ALU.mult)
            tt("den", "t1", "t2", ALU.add)
            chain.after(v.reciprocal(S["rden"], S["den"]))
            tt("t1", "ei", aim, ALU.mult)
            tt("t2", "er1", "ear", ALU.mult)
            tt("t3", "t1", "t2", ALU.subtract)
            tt("gr", "t3", "rden", ALU.mult)
            tt("t1", "ei", "ear", ALU.mult)
            tt("t2", "er1", aim, ALU.mult)
            tt("t3", "t1", "t2", ALU.add)
            chain.after(v.scalar_tensor_tensor(S["gi"], S["t3"], -1.0, S["rden"], ALU.mult, ALU.mult))
            tt("t1", par[:, 2, :], "gr", ALU.mult)
            tt("t2", par[:, 3, :], "gi", ALU.mult)
            tt("cr", "t1", "t2", ALU.subtract)
            tt("t1", par[:, 2, :], "gi", ALU.mult)
            tt("t2", par[:, 3, :], "gr", ALU.mult)
            tt("ci", "t1", "t2", ALU.add)
            for half, (f1, s1, f2, s2) in enumerate((("cr", 2.0, "ci", -2.0), ("ci", -2.0, "cr", -2.0))):
                rows = slice(NM * half, NM * half + NM)
                ts(S["k1"][rows, :], S[f1][rows, :], s1, None, ALU.mult, ALU.bypass)
                ts(S["k2"][rows, :], S[f2][rows, :], s2, None, ALU.mult, ALU.bypass)
            dve.wait_ge(s_mags, 4)
            dve.wait_ge(s_sin, 3)
            for q in range(2):
                chain.after(v.tensor_tensor(a_ph[:, q, :, :], a_ph[:, q, :, :], a_mag, ALU.mult))
                chain.after(v.tensor_tensor(a_ph[:, q, :, :], a_ph[:, q, :, :], bc(S["k1" if q == 0 else "k2"], FA),
                                            ALU.mult))
            v.tensor_tensor(a_ph[:, 0, :, :], a_ph[:, 0, :, :], a_ph[:, 1, :, :], ALU.add).then_inc(s_uv, 1)
            dve.wait_ge(s_sin, 4)
            v.tensor_tensor(v_ph, v_ph, v_mag, ALU.mult).then_inc(s_uv, 1)
            def weight_low(k, cols):
                dve.wait_ge(s_whi, k + 1)
                v.tensor_tensor(weight_out(k, 1), weight_in_psum(k, cols), weight_out(k, 0).bitcast(F32),
                                ALU.subtract).then_inc(s_wlo, 1)

            for k in range(GH):
                weight_low(k, L)
            dve.wait_ge(s_db, 32)
            dve.wait_ge(s_kps, 1)
            for n in range(2):
                hs = slice(H // 2 * n, H // 2 * n + H // 2)
                chain.after(v.tensor_copy(k32[:, hs, :], bb[n][0:FA, :].rearrange("a (h b) -> a h b", b=FB)))
            chain.after(v.tensor_tensor(k32[:, :, FB - 1], k32[:, :, FB - 1], d_add, ALU.add))
            chain.after(v.tensor_copy(k_split[0], k32))
            v.tensor_tensor(k_split[1], k32, k_split[0].bitcast(F32), ALU.subtract).then_inc(s_klo, 1)
            for k in range(GH, NWT):
                weight_low(k, LB * AR if k == NWT - 1 else L)

            def u_low(h, i):
                dve.wait_ge(u_hi, h + 1)
                v.tensor_tensor(uT[i % 2][1][:, :, :], wb[0][:, :].rearrange("p (k b) -> p k b", k=LB),
                                uT[i % 2][0][:, :, :].bitcast(F32), ALU.subtract).then_inc(u_lo, 1)

            def y_mask(h, i, first=False):
                dve.wait_ge(y_ps, h + 1)
                if not (first and i < 2):
                    dve.wait_ge(y_lo, h - 1)
                v.tensor_tensor(y32[i % 2][:, :, :], wb[1][:, :].rearrange("p (k b) -> p k b", k=LB),
                                mask[:, :, :], ALU.mult).then_inc(y_ms, 1)

            def gated(gr, j):
                dve.wait_ge(bc_ps, NP * gr + j + 1)
                if j >= 2:
                    dve.wait_ge(g_lo, NP * gr + j - 1)
                v.tensor_tensor(g32[j % 2][:, :], bb[j % 2][:, :], res[:, :], ALU.mult).then_inc(g_mul, 1)

            def routing(gr):
                ch = Chain(dve, s_rt, ROUTE * gr)
                dve.wait_ge(ar_ev, 2 * gr + 2)
                ch.after(v.tensor_copy(res[R:P, :], res[0:R, :]))
                dve.wait_ge(lt_ps, gr + 1)
                lg = bb[0][:, 0:GH * E].rearrange("p (i e) -> p i e", i=GH)

                def over(t, n=E):
                    return t.rearrange("p (i o) -> p i o", o=1).broadcast_to([P, GH, n])

                ch.after(v.reduce_max(rmax[:, :], lg, AX))
                v.tensor_tensor(rex[:, :, :], lg, over(rmax[:, :]), ALU.subtract).then_inc(r_sub, 1)
                dve.wait_ge(r_exp, gr + 1)
                ch.after(v.reduce_sum(rsum[:, :], rex[:, :, :], AX))
                ch.after(v.reciprocal(rinv[:, :], rsum[:, :]))
                ch.after(v.tensor_tensor(rprob[:, :, :], rex[:, :, :], over(rinv[:, :]), ALU.mult))
                marks = iota_e[:, :].rearrange("p (o e) -> p o e", o=1).broadcast_to([P, GH, E])
                for q in range(2):
                    ch.after(v.reduce_max(rtop[:, q, :], rprob[:, :, :], AX))
                    ch.after(v.tensor_tensor(roh[:, :, q, :], rprob[:, :, :], over(rtop[:, q, :]), ALU.is_equal))
                    ch.after(v.tensor_tensor(roh[:, :, q, :], roh[:, :, q, :], marks, ALU.mult))
                    ch.after(v.reduce_max(rmark[:, :], roh[:, :, q, :], AX))
                    ch.after(v.tensor_tensor(roh[:, :, q, :], marks, over(rmark[:, :]), ALU.is_equal))
                    if q == 0:
                        ch.after(v.scalar_tensor_tensor(rprob[:, :, :], roh[:, :, q, :], -2.0, rprob[:, :, :],
                                                        ALU.mult, ALU.add))
                ch.after(v.scalar_tensor_tensor(rden[:, :], rtop[:, 0, :], 1e-6, rtop[:, 1, :], ALU.add, ALU.add))
                ch.after(v.reciprocal(rinv[:, :], rden[:, :]))
                for q in range(2):
                    ch.after(v.scalar_tensor_tensor(rw[:, q, :], rtop[:, q, :], SCALING, rinv[:, :],
                                                    ALU.mult, ALU.mult))
                for q in range(2):
                    ch.after(v.tensor_tensor(roh[:, :, q, :], roh[:, :, q, :], over(rw[:, q, :]), ALU.mult))
                ch.after(v.tensor_tensor(rcomb[:, :, :], roh[:, :, 0, :], roh[:, :, 1, :], ALU.add))
                ch.after(v.tensor_copy(cst[:, :, 0:E].bitcast(F32R), rcomb[:, :, :]))
                v.tensor_tensor(cst[:, :, E:2 * E], rcomb[:, :, :], cst[:, :, 0:E], ALU.subtract).then_inc(c_rdy, 1)
                assert ch.n == ROUTE, ch.n

            u_low(0, 0)
            for i in range(GH):
                if i + 1 < GH:
                    u_low(i + 1, i + 1)
                y_mask(i, i, True)

            def group(gr, n, last):
                nxt = GH * gr + GH
                routing(gr)
                if not last:
                    u_low(nxt, 0)
                    y_mask(nxt, 0)
                    u_low(nxt + 1, 1)
                gated(gr, 0)
                gated(gr, 1)
                for i in range(1, GH):
                    if not last:
                        y_mask(nxt + i, i)
                        if i + 1 < GH:
                            u_low(nxt + i + 1, i + 1)
                    gated(gr, i + 1)
                for j in range(GH + 1, NP):
                    gated(gr, j)
                for i in range(GH):
                    dve.wait_ge(a_done, GH * gr + i + 1)
                    dve.wait_ge(xb_rdy, GH * gr + i + 1)
                    v.tensor_tensor(xg[n][:, i, :], acc[i][:, :], xg[n][:, i, :], ALU.add).then_inc(x1_rdy, 1)

            group(0, 0, False)
            with dve.Fori(0, (NG - 2) // XB) as t:
                for n in range(XB):
                    group(XB * t + n + 1, (n + 1) % XB, False)
            group(NG - 1, (NG - 1) % XB, True)
            for k in range(NWT, NWT + LB + 1):
                weight_low(k, LB * C if k == NWT + LB else L)

            def split(e, n):
                dve.wait_ge(cw_hi, e + 1)
                v.tensor_tensor(w_sp[n][1][:, :, :], w_id[n][:, :, :], w_sp[n][0][:, :, :].bitcast(F32),
                                ALU.subtract).then_inc(cw_lo, 1)

            def merged(e, n):
                for k in range(LB):
                    dve.wait_ge(m_hi, LB * e + k + 1)
                    v.tensor_tensor(mw[1][:, bass.ds(e, 1), k, :].rearrange("p e f -> p (e f)"), acc[k][:, :],
                                    mw[0][:, bass.ds(e, 1), k, :].rearrange("p e f -> p (e f)").bitcast(F32),
                                    ALU.subtract).then_inc(m_lo, 1)
                dve.wait_ge(mc_ps, e + 1)
                v.tensor_copy(mc[:, bass.ds(e, 1), :, :].rearrange("p e k c -> p (e k) c"),
                              wb[n][:, 0:LB * C].rearrange("p (k c) -> p k c", k=LB)).then_inc(mc_ev, 1)

            split(0, 0)
            split(1, 1)
            with dve.Fori(0, IDS // 2 - 1) as t:
                for n in range(2):
                    merged(2 * t + n, n)
                    split(2 * t + n + 2, n)
            merged(IDS - 2, 0)
            merged(IDS - 1, 1)
            dve.wait_ge(s_l1c, 3)
            dve.wait_ge(t_rdy, 5)
            with dve.Fori(0, NTD // TD) as c:
                ch = Chain(dve, s_dn, DOTS * c)
                dve.wait_ge(dm_ps, c * TD + TD)
                dots = acc[0][:, :].rearrange("p (t c) -> p t c", t=TD)

                def per_tile(t):
                    return t.rearrange("p (t o) -> p t o", o=1).broadcast_to([P, TD, C])

                ch.after(v.reduce_max(dmax[:, :], dots, AX))
                v.tensor_tensor(dshift[:, :, :], dots, per_tile(dmax[:, :]), ALU.subtract).then_inc(dt_sh, 1)
                dve.wait_ge(dt_exp, c + 1)
                ch.after(v.reduce_sum(dsum[:, :], dexp[:, :, :], AX))
                ch.after(v.reciprocal(dinv[:, :], dsum[:, :]))
                ch.after(v.tensor_tensor(hits[:, :, :], dexp[:, :, :], per_tile(dinv[:, :]), ALU.mult))
                ch.after(v.tensor_scalar(hits[:, :, :], hits[:, :, :], 0.01, None, ALU.is_gt))
                ch.after(v.tensor_tensor(hits[:, :, :], hits[:, :, :], per_tile(slot_ok[:, bass.ds(c * TD, TD)]),
                                         ALU.mult))
                ch.after(v.reduce_max(query[:, bass.ds(c * TD, TD)], hits[:, :, :], AX))
                ch.after(v.reduce_max(hit8[:, :], hits[:, :, :].rearrange("p t c -> p c t"), AX))
                ch.after(v.tensor_tensor(hitmax[:, :], hitmax[:, :], hit8[:, :], ALU.max))
                assert ch.n == DOTS, ch.n
            dve.wait_ge(s_l1l, 32)
            ch = Chain(dve, s_dn, DOTS * (NTD // TD))
            ch.after(v.tensor_copy(assign_f[:, :], assign_i[:, :]))
            v.tensor_scalar(onehot[:, :], assign_f[:, :], cidx[:, 0:1], None, ALU.is_equal).then_inc(cs_rdy, 1)
            dve.wait_ge(cnt_ps, 1)
            v.tensor_scalar(csel[:, :], acc[1][0:C, 0:P], 0.5, None, ALU.is_gt).then_inc(cs_rdy, 1)
            dve.wait_ge(rs_ps, 1)
            v.tensor_copy(rowsel[:, :], acc[1][:, :]).then_inc(cs_rdy, 1)
            dve.wait_ge(cs_rdy, 3)

            def dense_x(t, n):
                dve.wait_ge(xe_hi, t + 1)
                v.tensor_tensor(xts[n][1][:, :, :], wb[n][:, :].rearrange("p (k b) -> p k b", k=LB),
                                xts[n][0][:, :, :].bitcast(F32), ALU.subtract).then_inc(xe_lo, 1)

            def select(t, n):
                dve.wait_ge(ft_ps, t + 1)
                v.tensor_tensor(dense[n % 2][:, :], acc[n][:, :], b1_bc[:, :], ALU.add).then_inc(ft_ev, 1)
                dve.wait_ge(ft_ev, t + RB + 1)
                dve.wait_ge(o_rdy, t + 1)
                v.scalar_tensor_tensor(dsel[n][:, :], dense[n % 2][:, :], query[:, bass.ds(t, 1)],
                                       rowsel[:, :], ALU.mult, ALU.mult).then_inc(ft_sel, 1)

            dense_x(0, 0)
            with dve.Fori(0, NT // RB) as c:
                for n in range(RB):
                    dense_x(RB * c + n + 1, (n + 1) % 2)
                    select(RB * c + n, n)
            for t in range(NT // RB * RB, NT):
                if t + 1 < NT:
                    dense_x(t + 1, (t + 1) % 2)
                select(t, t % RB)

        @block.tensor
        def _(pe):
            mm = nc.tensor.matmul
            pe.wait_ge(s_sort, 3)
            pe.wait_ge(t_mat, 1)
            mm(wb[0][:, 0:IDS], one_s, oh8, start=True, stop=True).then_inc(t_cnt, 1)
            pe.wait_ge(s_id, 1)
            pe.wait_ge(s_stk, 4)
            for q in range(4):
                last = nc.tensor.transpose(bb[0][:, H * q:H * q + H], modes[:, q, :], ident[0:H, 0:H])
            last.then_inc(s_kps_par, 1)
            pe.wait_ge(t_mat, 2)
            for q in range(TB):
                mm(wb[1][:, 0:NTD], quad[:, q, :, :].rearrange("p r h -> p (r h)"), match[:, q, :],
                   start=(q == 0), stop=(q == TB - 1))
            for k, at in ((0, 64), (1, 128)):
                for q in range(TB):
                    last = mm(wb[0][0:1, at:at + NTD], first_of[:, k:k + 1], match[:, q, :],
                              start=(q == 0), stop=(q == TB - 1))
            last.then_inc(t_tab, 1)

            def weight(k):
                if k >= GH:
                    pe.wait_ge(s_wlo, k - GH + 1)
                bank = acc[k % GH]
                if k < NP:
                    pe.wait_ge(s_bl, 64)
                    src = [(b_raw[:, a, 2 * k:2 * k + 2, :].rearrange("p e r -> p (e r)"), P * a) for a in range(4)]
                elif k < NP + LB:
                    k0 = k - NP
                    pe.wait_ge(s_rev, 4)
                    src = [(w_rev[:, a, P * k0:P * k0 + P], P * a) for a in range(4)]
                elif k < NWT:
                    pe.wait_ge(s_rev, 5)
                    src = [(ar_rev[:, P * a:P * a + P], AR * a) for a in range(LB)]
                elif k < NWT + LB:
                    a0 = k - NWT
                    pe.wait_ge(s_fwl, 32)
                    src = [(f_raw[:, a, P * a0:P * a0 + P], P * a) for a in range(4)]
                else:
                    src = [(cent_raw[:, P * a:P * a + P], C * a) for a in range(LB)]
                for s, at in src:
                    rows, cols = s.shape[0], s.shape[1]
                    last = nc.tensor.transpose(bank[0:cols, at:at + rows], s, ident[0:rows, 0:rows])
                last.then_inc(s_wps, 1)

            for k in range(GH):
                weight(k)
            pe.wait_ge(s_uv, 2)
            pe.wait_ge(s_parT, 1)
            for h in range(H):
                last = mm(bb[h // 16][0:FA, FB * (h % 16):FB * (h % 16) + FB], a_ph[:, 0, h, :], v_ph[:, h, :],
                          start=True, stop=True)
            last.then_inc(s_kps, 1)
            for k in range(GH, NWT):
                weight(k)

            def u_transpose(h, i, n, g2):
                pe.wait_ge(s_x[n][i], 16 * g2)
                for k in range(LB):
                    last = nc.tensor.transpose(wb[0][:, P * k:P * k + P], xg[n][:, i, P * k:P * k + P], ident[:, :])
                last.then_inc(u_ps, 1)

            def y_conv(h, i, loads):
                pe.wait_ge(u_lo, h + 1)
                pe.wait_ge(s_sk[i], 16 * loads)
                for d in range(LB):
                    cols = slice(L - P * (d + 1), L - P * d)
                    for a, b in ((0, 0), (0, 1), (1, 0)):
                        last = mm(wb[1][:, P * d:L], sk[i][:, a, cols],
                                  uT[i % 2][b][:, 0:LB - d, :].rearrange("p k b -> p (k b)"),
                                  start=(d == 0 and a == 0 and b == 0), stop=(d == LB - 1 and a == 1))
                last.then_inc(y_ps, 1)

            def ar_project(gr):
                pe.wait_ge(y_lo, GH * gr + GH)
                steps = [(a, b, k) for a, b in ((0, 0), (1, 0), (0, 1)) for k in range(LB)]
                for a, b, k in steps:
                    last = mm(wb[0][0:AR, :], arw[a][:, k, :], yT[b][:, k, :, :].rearrange("p i b -> p (i b)"),
                              start=(a, b, k) == steps[0], stop=(a, b, k) == steps[-1])
                last.then_inc(ar_ps, 1)

            def logits(gr):
                for i in range(GH):
                    t = nc.tensor.transpose(bb[0][:, E * i:E * i + E], lgT[:, P * i:P * i + P], ident[0:E, 0:E])
                t.then_inc(lt_ps, 1)

            def base(gr, i, with_logits=False):
                pe.wait_ge(x1_rdy, GH * gr + i + 1)
                for a, b in ((0, 0), (0, 1), (1, 0)):
                    for k in range(LB):
                        if with_logits and a == b == 0 and k == LB - 1:
                            pe.wait_ge(ar_ev, 2 * gr + 2)
                        last = mm(acc[i][:, :], yT[a][:, k, i, :], w0[b][:, k, :], start=(a == b == k == 0),
                                  stop=False)
                    if with_logits and a == b == 0:
                        logits(gr)
                last.then_inc(b_done, 1)

            def gates(gr, j):
                if j >= 2:
                    pe.wait_ge(g_mul, NP * gr + j - 1)
                mm(bb[j % 2][:, :], sel[:, j, :], cTs[:, :], start=True, stop=True).then_inc(bc_ps, 1)

            def experts(gr, j):
                pe.wait_ge(g_lo, NP * gr + j + 1)
                for i in range(GH):
                    for a, b in ((0, 0), (0, 1), (1, 0)):
                        last = mm(acc[i][:, :], gT[j % 2][a][:, P * i:P * i + P], bw[b][:, j, :],
                                  start=False, stop=(j == NP - 1 and a == 1))
                    if j == NP - 1:
                        last.then_inc(a_done, 1)
                if j < NP - 1:
                    last.then_inc(d_done, 1)

            pe.wait_ge(t_rdy, 5)
            u_transpose(0, 0, 0, 1)
            for i in range(GH):
                y_wait = i
                if i + 1 < GH:
                    pe.wait_ge(u_lo, i + 1)
                    u_transpose(i + 1, i + 1, 0, 1)
                if i:
                    pe.wait_ge(y_ms, i)
                y_conv(i, i, 1)
            pe.wait_ge(u_lo, GH)
            ar_project(0)

            def group(gr, n, last, loads):
                nxt, n2 = GH * gr + GH, (n + 1) % XB
                base(gr, 0, with_logits=True)
                base(gr, 1)
                if not last:
                    u_transpose(nxt, 0, n2, loads)
                base(gr, 2)
                if not last:
                    y_conv(nxt, 0, gr + 2)
                    u_transpose(nxt + 1, 1, n2, loads)
                pe.wait_ge(c_rdy, gr + 1)
                for i in range(GH):
                    t = nc.tensor.transpose(bb[1][0:2 * E, P * i:P * i + P], cst[:, i, :], ident[:, :])
                t.then_inc(ct_ps, 1)
                base(gr, 3)
                pe.wait_ge(ct_sb, gr + 1)
                gates(gr, 0)
                gates(gr, 1)
                for i in range(1, GH):
                    if not last:
                        pe.wait_ge(y_ms, nxt + i)
                        y_conv(nxt + i, i, gr + 2)
                        if i + 1 < GH:
                            u_transpose(nxt + i + 1, i + 1, n2, loads)
                    experts(gr, i - 1)
                    gates(gr, i + 1)
                for j in range(GH - 1, NP):
                    experts(gr, j)
                    if j + 2 < NP:
                        gates(gr, j + 2)
                if not last:
                    ar_project(gr + 1)

            group(0, 0, False, 1)
            with pe.Fori(0, (NG - 2) // XB) as t:
                for n in range(XB):
                    group(XB * t + n + 1, (n + 1) % XB, False, t + 1 + (n + 2) // XB)
            group(NG - 1, (NG - 1) % XB, True, 0)

            pe.wait_ge(x1_rdy, GH * NG + GH)
            for k in range(NWT, NWT + LB + 1):
                weight(k)
            pe.wait_ge(s_wlo, NWT + LB + 1)

            def merge(e, n, first):
                pe.wait_ge(cw_lo, e + 1)
                steps = [(a, b, o) for a, b in ((0, 0), (0, 1), (1, 0)) for o in range(LB)]
                if not first:
                    pe.wait_ge(mc_ev, e - 1)
                for k in range(LB):
                    if not first or e == 1:
                        pe.wait_ge(m_lo, LB * e + k - 3)
                    for dst, rhs in ((acc[k][:, :], f_w), (wb[n][:, C * k:C * k + C], f_c)):
                        for s in steps:
                            a, b, o = s
                            last = mm(dst, w_sp[n][a][:, o, P * k:P * k + P], rhs[b][:, o, :],
                                      start=s == steps[0], stop=s == steps[-1])
                        if rhs is f_w:
                            last.then_inc(m_ps, 1)
                last.then_inc(mc_ps, 1)

            merge(0, 0, True)
            merge(1, 1, True)
            with pe.Fori(1, IDS // 2) as t:
                for n in range(2):
                    merge(2 * t + n, n, False)
            pe.wait_ge(m_lo, LB * IDS)
            pe.wait_ge(mc_ev, IDS)

            def transpose_rows(n, bank, s, count):
                pe.wait_ge(s[n], 16 * count)
                for k in range(LB):
                    last = nc.tensor.transpose(wb[bank][:, P * k:P * k + P], rows[n][:, P * k:P * k + P], ident[:, :])
                return last

            def dots_step(c, last):
                for w in range(TD):
                    t, nxt = c * TD + w, w + 1
                    if not (last and nxt == TD):
                        pe.wait_ge(xd_ev, t + 2)
                        transpose_rows(nxt % RB, nxt % 2, s_rd, (TD // RB) * c + nxt // RB + 1).then_inc(xd_ps, 1)
                    pe.wait_ge(xd_ev, t + 3)
                    if w == 0:
                        pe.wait_ge(dt_sh, c + 1)
                    e = pe.value_load(tile_id[0:1, bass.ds(t, 1)], min_val=0, max_val=IDS - 1)
                    for k in range(LB):
                        m = mm(acc[0][:, C * w:C * w + C], xtf[w % 2][:, k, :],
                               mc[:, bass.ds(e, 1), k, :].rearrange("p e f -> p (e f)"),
                               start=(k == 0), stop=(k == LB - 1))
                    m.then_inc(dm_ps, 1)

            transpose_rows(0, 0, s_rd, 1).then_inc(xd_ps, 1)
            with pe.Fori(0, NTD // TD - 1) as c:
                dots_step(c, False)
            dots_step(NTD // TD - 1, True)
            pe.wait_ge(s_dn, DOTS * (NTD // TD))
            mm(acc[1][0:C, 0:P], hitmax[:, :], ones[:, :], start=True, stop=True).then_inc(cnt_ps, 1)
            pe.wait_ge(cs_rdy, 2)
            mm(acc[1][:, :], csel[:, :], onehot[:, :], start=True, stop=True).then_inc(rs_ps, 1)
            pe.wait_ge(cs_rdy, 3)

            def dense_tile(t, n, loads):
                if not (isinstance(t, int) and t + 1 == NT):
                    nxt = n + 1
                    pe.wait_ge(xe_lo, t + 2)
                    transpose_rows(nxt % RB, nxt % 2, s_rl, loads + nxt // RB).then_inc(xe_ps, 1)
                pe.wait_ge(xe_lo, t + 3)
                pe.wait_ge(ft_ev, t + 1)
                e = pe.value_load(tile_id[0:1, bass.ds(t, 1)], min_val=0, max_val=IDS - 1)
                steps = [(a, b, k) for a, b in ((0, 0), (0, 1), (1, 0)) for k in range(LB)]
                for s in steps:
                    a, b, k = s
                    m = mm(acc[n][:, :], xts[n % 2][a][:, k, :],
                           mw[b][:, bass.ds(e, 1), k, :].rearrange("p e f -> p (e f)"),
                           start=s == steps[0], stop=s == steps[-1])
                m.then_inc(ft_ps, 1)

            transpose_rows(0, 0, s_rl, 1).then_inc(xe_ps, 1)
            with pe.Fori(0, NT // RB) as c:
                for n in range(RB):
                    dense_tile(RB * c + n, n, c + 1)
            for t in range(NT // RB * RB, NT):
                dense_tile(t, t % RB, t // RB + 1)


_INS = ["x", "itok_B_78_3631", "itok_B_3_7", "L0_cond_log_dt", "L0_cond_C", "L0_cond_log_A_real", "L0_cond_A_imag",
        "L0_cond_D", "L0_ffn_base_w", "L0_ffn_base_b", "L0_ffn_A", "L0_ffn_B", "L0_ffn_router_w",
        "L1_cond_weight", "L1_ffn_weight", "L1_ffn_bias", "L1_ffn_centroids", "L1_ffn_assignments"]
_OUTS = [((B, H, L), "float32")]


def kernel(**inputs):
    import numpy as _np
    import concourse.bacc as _bacc
    from concourse import mybir as _mybir
    from concourse.bass_utils import run_bass_kernel_spmd as _run

    nc = _bacc.Bacc("TRN2", target_bir_lowering=False, num_devices=1)
    arrays, args = {}, []
    for name in _INS:
        a = _np.ascontiguousarray(inputs[name])
        arrays[f"in_{name}_dram"] = a
        args.append(nc.dram_tensor(f"in_{name}_dram", a.shape, _mybir.dt.from_np(a.dtype), kind="ExternalInput").ap())
    for i, (shape, dtype) in enumerate(_OUTS):
        dt = _mybir.dt.from_np(_np.dtype(dtype))
        args.append(nc.dram_tensor(f"out_{i}_dram", shape, dt, kind="ExternalOutput").ap())
    build(nc, *args)
    r = _run(nc, [arrays], core_ids=[0])
    got = tuple(r.results[0][f"out_{i}_dram"] for i in range(len(_OUTS)))
    return got[0]
```

```python
import math
from contextlib import ExitStack

import concourse.bass as bass
from concourse import mybir

P = 128
B, H, L = 128, 32, 512
LB = L // P
NM = 64
E, R = 16, 64
NP = E * R // P
AR = R + E
IDS = 8
C = 64
GH = 4
NG = H // GH
XB = 3
TB = 4
NT = B // TB + IDS - 1
TD = 5
TK = 3
NTD = TD * IDS
RB = 6
FA, FB = 16, 32
KPITCH = L + P
SCALING = 0.5
MAGIC = 1.5 * 2.0 ** 23
TURN = 6.283185
ROUTE = 24
DOTS = 6
NWT = LB + 1 + NP

F32 = mybir.dt.float32
F32R = mybir.dt.float32r
I32 = mybir.dt.int32
U32 = mybir.dt.uint32
ALU = mybir.AluOpType
ACT = mybir.ActivationFunctionType
AX = mybir.AxisListType.X


def build(nc, x, lengths, adapter_ids, log_dt, ssm_c, log_a_real, a_imag, ssm_d, base_w, base_b,
          lora_a, lora_b, router_w, cond_w, ffn_w, ffn_bias, centroids, assignments, out):
    ctx = ExitStack()

    def sem(name):
        return ctx.enter_context(nc.semaphore(name))

    def alloc(stack, name, shape, dt=F32):
        return stack.enter_context(nc.sbuf_tensor(name, shape, dt))

    k_dram = nc.dram_tensor("k_rev", (2, H, KPITCH), F32, kind="Internal").ap()
    x1_dram = nc.dram_tensor("x1_sorted", (B * H, L), F32, kind="Internal").ap()

    with ctx:
        ident = alloc(ctx, "ident", [P, P])
        tile_id = alloc(ctx, "tile_adapter", [1, NTD], I32)
        tile_src = alloc(ctx, "tile_of_part", [1, NTD], I32)
        sort_row = alloc(ctx, "sorted_row", [P, NG], U32)
        sort_now = alloc(ctx, "sorted_row_of_group", [P, 1], U32)
        slot_off = alloc(ctx, "slot_threshold_added", [P, NTD])
        slot_row = alloc(ctx, "slot_out_row", [P, NTD], U32)
        w_id = alloc(ctx, "cond_w", [P, LB, L])
        ctb0 = alloc(ctx, "merged_cT_0", [C, L])

        l0 = ExitStack()
        bw = [alloc(l0, f"lora_b_{n}", [P, NP, L], F32R) for n in ("hi", "lo")]
        w0 = [alloc(l0, f"base_w_{n}", [P, LB, L], F32R) for n in ("hi", "lo")]
        xg = [alloc(l0, f"x_group_{n}", [P, GH, L]) for n in range(2)]
        arw = [alloc(l0, f"a_router_{n}", [P, LB, AR], F32R) for n in ("hi", "lo")]
        sk = [alloc(l0, f"hankel_{n}", [P, 2, L], F32R) for n in range(GH)]
        before_u = ExitStack()
        w_rev = alloc(before_u, "base_w_reversed", [P, LB, L])
        before_u.close()
        uT = [[alloc(l0, f"uT_{m}_{n}", [P, LB, B], F32R) for m in ("hi", "lo")] for n in range(2)]
        y32 = [alloc(l0, f"y_masked_{n}", [P, LB, B]) for n in range(2)]
        yT = [alloc(l0, f"yT_{n}", [P, LB, GH, B], F32R) for n in ("hi", "lo")]
        mask = alloc(l0, "length_mask", [P, LB, B])
        b0_bc = alloc(l0, "base_b_bc", [P, L])
        sel = alloc(l0, "expert_selection", [2 * E, NP, P], F32R)
        res = alloc(l0, "res_hidden", [P, GH * B])
        lgT = alloc(l0, "logitsT", [E, GH * B])
        cst = alloc(l0, "combine_split", [P, GH, 2 * E])
        cTs = alloc(l0, "combineT", [2 * E, GH * B], F32R)
        g32 = [alloc(l0, f"gated_{n}", [P, GH * B]) for n in range(2)]
        gT = [[alloc(l0, f"gatedT_{m}_{n}", [P, GH * B], F32R) for m in ("hi", "lo")] for n in range(2)]
        iota_e = alloc(l0, "expert_marks", [P, E])
        rmax = alloc(l0, "r_max", [P, GH])
        rex = alloc(l0, "r_exp", [P, GH, E])
        rsum = alloc(l0, "r_sum", [P, GH])
        rinv = alloc(l0, "r_inv", [P, GH])
        rprob = alloc(l0, "r_prob", [P, GH, E])
        rtop = alloc(l0, "r_top", [P, 2, GH])
        rmark = alloc(l0, "r_mark", [P, GH])
        rden = alloc(l0, "r_den", [P, GH])
        rw = alloc(l0, "r_weight", [P, 2, GH])
        roh = alloc(l0, "r_onehot", [P, GH, 2, E])
        rcomb = alloc(l0, "r_combine", [P, GH, E])
        flat = alloc(l0, "setup", [P, 12 * 1024])
        sorting = alloc(l0, "sorting", [P, 1800])
        xg.append(flat[:, 0:GH * L].rearrange("p (i l) -> p i l", i=GH))
        spaces, off = [flat[:, :]], [0]

        def carve(cols, parts=P):
            if off[0] + cols > spaces[0].shape[1]:
                spaces.pop(0)
                off[0] = 0
            off[0] += cols
            return spaces[0][0:parts, off[0] - cols:off[0]]

        ar_raw = carve(L, AR)
        ar_rev = carve(L, AR)
        b_raw = carve(4 * E * R).rearrange("p (a e r) -> p a e r", a=4, e=E)
        modes = carve(4 * P, H).rearrange("p (q n) -> p q n", q=4)
        c_raw = carve(2 * NM, H).rearrange("p (n c) -> p n c", c=2)
        par = carve(4 * H).rearrange("p (q h) -> p q h", q=4)
        dt_bc = carve(H)
        small = carve(32 * H).rearrange("p (q h) -> p q h", q=32)
        phase_off = carve(2)
        bval = carve(FB)
        aval = carve(FA)
        v_ph = carve(H * FB).rearrange("p (h b) -> p h b", h=H)
        tmp = carve(H * FB)
        sel32 = tmp[0:2 * E, :].rearrange("p (j q) -> p j q", j=NP)
        a_tmp = tmp.rearrange("p (q h b) -> p q h b", q=2, h=H)
        v_tmp = tmp.rearrange("p (h b) -> p h b", h=H)
        k32 = tmp[0:FA, :].rearrange("p (h b) -> p h b", h=H)
        v_mag = carve(H * FB).rearrange("p (h b) -> p h b", h=H)
        a_ph = carve(2 * H * FA).rearrange("p (q h b) -> p q h b", q=2, h=H)
        a_mag = carve(H * FA).rearrange("p (h b) -> p h b", h=H)
        d_add = carve(H, FA)
        k_zero = carve(P, H)
        len_i = carve(B).bitcast(I32)
        len_f = carve(B)
        pos = carve(LB)
        same8 = flat[:, GH * L:GH * L + IDS * B].rearrange("p (e b) -> p e b", e=IDS)
        spaces, off = [sorting[:, :]], [0]
        quad = carve(TB * P).rearrange("p (q r h) -> p q r h", q=TB, r=TB)
        ids_ri = carve(B).bitcast(I32)
        ids_ci = carve(1).bitcast(I32)
        ids_r = carve(B)
        ids_c = carve(2)
        low = carve(B)
        same = carve(B)
        rank = carve(2)
        iota8 = carve(IDS)
        oh8 = carve(IDS)
        tri8 = carve(IDS * IDS).rearrange("p (e f) -> p e f", e=IDS)
        prod88 = carve(IDS * IDS).rearrange("p (e f) -> p e f", e=IDS)
        count = carve(IDS)
        start = carve(IDS)
        lo_tile = carve(IDS)
        hi_tile = carve(IDS)
        shift_i = carve(IDS).bitcast(I32)
        n_parts = carve(IDS)
        first_part = carve(IDS)
        oh_at = carve(IDS)
        place = carve(8)
        place_i = carve(1).bitcast(I32)
        first_of = carve(2)
        g_iota = carve(NG)
        slot_v = carve(TB * NTD).rearrange("p (q t) -> p q t", q=TB)
        match = carve(TB * NTD).rearrange("p (q t) -> p q t", q=TB)
        h_less = carve(1)
        pad_add = carve(1)
        row_f = carve(NTD)
        row_pad = carve(NTD)
        l0.close()

        l1 = ExitStack()
        mw = [alloc(l1, f"merged_w_{n}", [P, IDS, LB, L], F32R) for n in ("hi", "lo")]
        mc = alloc(l1, "merged_c", [P, IDS, LB, 2 * C], F32R)
        raws = ExitStack()
        raw_late = alloc(raws, "cond_w_raw_3", [P, LB, L])
        raw_a = alloc(raws, "cond_w_raw_1", [P, LB, L])
        alloc(raws, "ffn_w_and_centroids_here", [P, 2 * LB * L + LB * C])
        raw_b = alloc(raws, "cond_w_raw_2", [P, LB, L])
        alloc(raws, "two_rows_here", [P, 2 * L])
        ctb = [ctb0, alloc(raws, "merged_cT_1", [C, L])]
        cent_raw = ctb[0][:, :]
        raws.close()
        raw = [w_id, raw_a, raw_b, raw_late]
        fold = ExitStack()
        w_sp = [alloc(fold, f"cond_w_{m}", [P, LB, L], F32R) for m in ("hi", "lo")]
        f_w = [alloc(fold, f"ffn_wT_{n}", [P, LB, L], F32R) for n in ("hi", "lo")]
        f_c = alloc(fold, "centroidsT", [P, LB, C])
        xts = [[alloc(fold, f"x1T_{m}_{n}", [P, LB, P], F32R) for m in ("hi", "lo")] for n in range(2)]
        rows2 = [alloc(fold, f"dots_rows_{n}", [P, L]) for n in range(2)]
        dots = alloc(fold, "dots", [P, TD, C])
        dexp = alloc(fold, "dots_exp", [P, TD, C])
        hits = alloc(fold, "hits", [P, TD, C])
        hitmax = alloc(fold, "hit_any_of_step", [P, TD, C])
        hitany = alloc(fold, "hit_any", [P, C])
        dmax = alloc(fold, "dots_max", [P, TD])
        dsum = alloc(fold, "dots_sum", [P, TD])
        dthr = alloc(fold, "dots_threshold", [P, TD])
        query = alloc(fold, "query_sel", [P, NTD])
        ones = alloc(fold, "ones", [P, P])
        csel = alloc(fold, "cluster_sel", [C, P])
        cidx = alloc(fold, "cluster_index", [C, 1])
        onehot = ctb[0][:, :]
        fold.close()
        rows = [w_id[:, n, :] for n in range(LB)] + [t[:, :] for t in rows2]
        outt = [alloc(l1, f"out_tile_{n}", [P, L])[:, :] for n in range(RB)]
        dense = [alloc(l1, f"dense_{n}", [P, L]) for n in range(2)]
        dsel = [alloc(l1, f"dense_sel_{n}", [P, L]) for n in range(RB)]
        rowsel = alloc(l1, "row_sel", [P, L])
        b1_bc = alloc(l1, "ffn_bias_bc", [P, L])
        row_now = [alloc(l1, f"out_row_of_tile_{n}", [P, 1], U32) for n in range(RB)]
        assert (2 * RB + 2 + 2) * L + RB <= 4 * LB * L + LB * C
        l1.close()

        k_split = [yT[n][0:FA, :, :, :].rearrange("a k i b -> a (k i b)")[:, 0:H * FB]
                   .rearrange("a (h b) -> a h b", h=H) for n in range(2)]

        def bank(name):
            return ctx.enter_context(nc.psum_tensor(name, [P, 512], F32))

        acc = [bank(f"acc{i}") for i in range(GH)]
        wb = [bank(f"work{i}") for i in range(2)]
        bb = [bank(f"bcast{i}") for i in range(2)]
        db = acc + bb

        s_par = sem("params_loaded")
        s_ids = sem("ids_loaded")
        s_len = sem("lengths_loaded")
        s_db = sem("d_and_base_b_loaded")
        s_w0l = sem("base_w_loaded")
        s_arl = sem("a_router_loaded")
        s_bl = sem("lora_b_loaded")
        s_cst = sem("pool_constants_ready")
        s_id = sem("ident_ready")
        s_pool = sem("pool_chain")
        s_dve = sem("dve_setup_chain")
        s_rt = sem("dve_routing_chain")
        s_dn = sem("dve_layer1_chain")
        s_stk = sem("mode_stack_ready")
        s_parP = sem("params_in_psum")
        s_parT = sem("params_transposed")
        s_sort = sem("sort_inputs_ready")
        t_mat = sem("slots_matched")
        t_tab = sem("slot_tables_in_psum")
        t_rdy = sem("slot_tables_ready")
        sn_rdy = sem("sorted_rows_of_group_ready")
        s_dt = sem("dt_and_decay_ready")
        s_t0 = sem("turns_ready")
        s_mag = sem("decay_exponents_ready")
        s_mags = sem("decays_ready")
        s_fr = sem("phases_ready")
        s_sin = sem("sines_ready")
        s_uv = sem("mode_factors_u_ready")
        s_v = sem("mode_factors_v_ready")
        s_kps = sem("kernels_in_psum")
        s_klo = sem("kernels_lo")
        s_kst = sem("kernels_stored")
        s_rev = sem("weights_reversed")
        s_wps = sem("weights_in_psum")
        s_whi = sem("weights_hi")
        s_wlo = sem("weights_lo")
        s_x = [[sem(f"x_loaded_{n}_{i}") for i in range(GH)] for n in range(XB)]
        s_sk = [sem(f"hankel_loaded_{n}") for n in range(GH)]
        u_ps = sem("u_in_psum")
        u_hi = sem("u_hi")
        u_lo = sem("u_lo")
        y_ps = sem("y_in_psum")
        y_ms = sem("y_masked")
        y_hi = sem("y_hi")
        y_lo = sem("y_lo")
        ar_ps = sem("ar_in_psum")
        ar_ev = sem("ar_evacuated")
        lt_ps = sem("logits_in_psum")
        r_sub = sem("logits_shifted")
        r_exp = sem("logits_exp")
        c_rdy = sem("combine_ready")
        ct_ps = sem("combineT_in_psum")
        ct_sb = sem("combineT_ready")
        bc_ps = sem("gates_in_psum")
        g_mul = sem("gated_ready")
        g_hi = sem("gated_hi")
        g_lo = sem("gated_lo")
        d_done = sem("experts_added")
        b_done = sem("base_added")
        a_done = sem("head_accumulated")
        xb_rdy = sem("x_plus_bias")
        x1_rdy = sem("x1_ready")
        x1_st = [sem(f"x1_stored_{n}") for n in range(XB)]
        s_fwl = sem("ffn_w_loaded")
        s_cwl = [sem(f"cond_w_columns_loaded_{k}") for k in range(LB)]
        s_raw = [sem(f"cond_w_raw_loaded_{n}") for n in range(4)]
        cw_hi = sem("cond_w_hi")
        cw_lo = sem("cond_w_lo")
        m_ps = sem("merged_in_psum")
        m_hi = sem("merged_hi")
        m_lo = sem("merged_lo")
        ct_mm = sem("merged_cT_in_psum")
        ct_ev = sem("merged_cT_evacuated")
        mc_ps = sem("merged_c_in_psum")
        mc_hi = sem("merged_c_hi")
        mc_ev = sem("merged_c_ready")
        s_l1l = sem("ffn_bias_loaded")
        s_asg = sem("assignments_loaded")
        s_l1c = sem("layer1_consts")
        s_rd = [sem(f"dots_rows_loaded_{n}") for n in range(2)]
        xd_ps = sem("dots_x1T_in_psum")
        xd_hi = sem("dots_x1T_hi")
        xd_lo = sem("dots_x1T_lo")
        dm_ps = sem("dots_in_psum")
        dt_half = sem("dots_halves_copied")
        dt_ev = sem("dots_evacuated")
        dt_sh = sem("dots_shifted_ready")
        dt_exp = sem("dots_exp_ready")
        cnt_ps = sem("hit_counts_in_psum")
        cs_rdy = sem("cluster_sel_ready")
        rs_ps = sem("row_sel_in_psum")
        s_rl = [sem(f"rows_loaded_{n}") for n in range(RB)]
        xe_ps = sem("x1T_in_psum")
        xe_hi = sem("x1T_hi")
        xe_lo = sem("x1T_lo")
        ft_ps = sem("dense_in_psum")
        ft_ev = sem("dense_evacuated")
        ft_sel = sem("dense_selected")
        o_rdy = sem("out_tile_ready")
        row_rdy = sem("out_rows_of_tile_ready")
        s_out = [sem(f"out_stored_{n}") for n in range(RB)]

        block = ctx.enter_context(nc.Block())

        def weight_out(k, part):
            if k < NP:
                return bw[part][:, k, :]
            if k < NP + LB:
                return w0[part][:, k - NP, :]
            if k < NWT:
                return arw[part][:, :, :]
            if k < NWT + LB:
                return f_w[part][:, k - NWT, :]
            return f_c[:, :, :]

        def weight_in_psum(k, cols):
            src = acc[k % GH][:, 0:cols]
            return src.rearrange("p (k c) -> p k c", k=LB) if k in (NWT - 1, NWT + LB) else src

        class Chain:

            def __init__(self, eng, s, base=0):
                self.eng, self.s, self.base, self.n = eng, s, base, 0
                self.others = {}

            def after(self, ins, other=None):
                if other is not None:
                    self.others[other.name] = self.others.get(other.name, 0) + 1
                    ins.then_inc(other, 1)
                    self.eng.wait_ge(other, self.others[other.name])
                    return
                self.n += 1
                ins.then_inc(self.s, 1)
                self.eng.wait_ge(self.s, self.base + self.n)

        def load_x(sp, n, i, g):
            sp.dma_start(xg[n][:, i, :], x[:, bass.ds(GH * g + i, 1), :].rearrange("b h l -> b (h l)")
                         ).then_inc(s_x[n][i], 16)

        hankel = bass.AP(k_dram.tensor, 0, [[1, P], [H * KPITCH, 2], [KPITCH, H], [1, L]])

        def load_hankel(sp, g, i):
            src = hankel[:, :, bass.ds(GH * g + i, 1), :].rearrange("p s h l -> p s (h l)")
            sp.dma_start(sk[i][:, :, :].bitcast(F32), src).then_inc(s_sk[i], 16)

        @block.sync
        def _(sp):
            def twice(t):
                return bass.AP(t.tensor, 0, [[NM, H], [0, 2], [1, NM]])

            sp.dma_start(modes[:, 0, :], twice(log_a_real)).then_inc(s_par, 16)
            sp.dma_start(modes[:, 1, :], twice(a_imag)).then_inc(s_par, 16)
            sp.dma_start(c_raw, ssm_c).then_inc(s_par, 16)
            sp.dma_start(dt_bc, bass.AP(log_dt.tensor, 0, [[0, P], [1, H]])).then_inc(s_par, 16)
            sp.dma_start(len_i, bass.AP(lengths.tensor, 0, [[0, P], [1, B]])).then_inc(s_len, 16)
            for a in range(4):
                sp.dma_start(b_raw[:, a, :, :], lora_b[:, P * a:P * a + P, :].rearrange("e p r -> p e r")
                             ).then_inc(s_bl, 16)
            sp.dma_start(w_id[:, :, :], base_w.rearrange("(a p) l -> p a l", p=P)).then_inc(s_w0l, 16)
            sp.dma_start(ar_raw[0:R, :], lora_a).then_inc(s_arl, 16)
            sp.dma_start(ar_raw[R:AR, :], router_w).then_inc(s_arl, 16)
            for i in range(GH):
                load_x(sp, 0, i, 0)
            sp.wait_ge(s_cst, 1)
            sp.dma_start(d_add[FA - 1:FA, :], ssm_d.rearrange("(a h) -> a h", a=1)).then_inc(s_db, 16)
            sp.dma_start(b0_bc[:, :], bass.AP(base_b.tensor, 0, [[0, P], [1, L]])).then_inc(s_db, 16)
            sp.dma_start(ids_ri, bass.AP(adapter_ids.tensor, 0, [[0, P], [1, B]])).then_inc(s_ids, 16)
            sp.dma_start(ids_ci, adapter_ids.rearrange("(b a) -> b a", a=1)).then_inc(s_ids, 16)
            for i in range(GH):
                load_x(sp, 1, i, 1)
            cw = cond_w.rearrange("e (a p) k -> e p a k", p=P)
            sp.wait_ge(s_rev, 4)
            sp.dma_start(w_id[:, :, :], ffn_w.rearrange("(a p) o -> p a o", p=P)).then_inc(s_fwl, 16)
            sp.dma_start(cent_raw, centroids).then_inc(s_fwl, 16)
            sp.wait_ge(s_klo, 1)
            for n in range(2):
                dst = bass.AP(k_dram.tensor, n * H * KPITCH, [[FB, FA], [KPITCH, H], [1, FB]])
                sp.dma_start(dst, k_split[n].bitcast(F32)).then_inc(s_kst, 16)
                dst0 = bass.AP(k_dram.tensor, n * H * KPITCH + L, [[KPITCH, H], [1, P]])
                sp.dma_start(dst0, k_zero).then_inc(s_kst, 16)
            sp.wait_ge(s_kst, 64)
            for i in range(GH):
                load_hankel(sp, 0, i)

            sp.wait_ge(s_wps, NWT + LB)
            for e in range(3):
                sp.dma_start(raw[e][:, :, :], cw[e, :, :, :]).then_inc(s_raw[e], 16)

            def hankels(g):
                for i in range(GH):
                    sp.wait_ge(y_ps, GH * g + i - GH + 1)
                    load_hankel(sp, g, i)

            with sp.Fori(0, (NG - 2) // XB) as t:
                for n in range(XB):
                    g = XB * t + n
                    hankels(g + 1)
                    sp.wait_ge(sn_rdy, g + 1)
                    for i in range(GH):
                        load_x(sp, (n + 2) % XB, i, g + 2)
            hankels(NG - 1)
            sp.wait_ge(x1_st[XB - 1], 16 * len(range(XB - 1, NG, XB)))
            sp.wait_ge(a_done, GH * NG)
            sp.dma_start(raw[3][:, :, :], cw[3, :, :, :]).then_inc(s_raw[3], 16)
            for e in range(4, IDS):
                sp.wait_ge(ct_mm, e - 3)
                sp.dma_start(raw[e % 4][:, :, :], cw[e, :, :, :]).then_inc(s_raw[e % 4], 16)
            def load_block(e, k):
                cols = slice(P * k, P * k + P)
                src = cw[bass.ds(e, 1), :, :, cols].rearrange("e p a k -> p (e a) k")
                sp.dma_start(w_id[:, :, cols], src).then_inc(s_cwl[k], 16)

            sp.wait_ge(ct_mm, 5)
            for k in range(LB):
                load_block(0, k)
            for n in range(XB):
                sp.wait_ge(x1_st[n], 16 * len(range(n, NG, XB)))
            sp.wait_ge(t_rdy, 5)
            x1_tiles = x1_dram.rearrange("(t p) l -> t p l", p=P)

            def load_rows(t, dst, s):
                src = sp.value_load(tile_src[0:1, bass.ds(t, 1)], min_val=0, max_val=B // TB - 1)
                sp.dma_start(dst, x1_tiles[bass.ds(src, 1), :, :].rearrange("t p l -> (t p) l")
                             ).then_inc(s, 16)

            def dots_rows(t, n):
                sp.wait_ge(xd_ps, t - 1)
                load_rows(t, rows2[n][:, :], s_rd[n])

            def fold_step(e, n, tiles, weights):
                for w in range(3, 3 + tiles):
                    dots_rows(TD * e + w, (n + w) % 2)
                    if weights and w > 3:
                        sp.wait_ge(cw_lo, LB * (e + 1) + w - 3)
                        load_block(e + 2, w - 4)

            for t in range(2):
                load_rows(t, rows2[t][:, :], s_rd[t])
            sp.wait_ge(mc_ps, IDS)
            sp.dma_start(onehot.bitcast(I32), bass.AP(assignments.tensor, 0, [[0, C], [1, L]])).then_inc(s_asg, 16)
            dots_rows(2, 0)
            for k in range(LB):
                sp.wait_ge(cw_lo, k + 1)
                load_block(1, k)
            with sp.Fori(0, IDS // 2 - 1) as t:
                for n in range(2):
                    fold_step(2 * t + n, n, TD, True)
            fold_step(IDS - 2, 0, TD, False)
            fold_step(IDS - 1, 1, TD - 3, False)
            sp.wait_ge(cw_lo, LB * IDS)
            sp.wait_ge(xd_ps, NTD)
            for n in range(RB):
                load_rows(n, rows[n], s_rl[n])
            sp.wait_ge(m_ps, LB * IDS)
            sp.dma_start(b1_bc[:, :], bass.AP(ffn_bias.tensor, 0, [[0, P], [1, L]])).then_inc(s_l1l, 16)
            with sp.Fori(1, NT // RB) as c:
                for n in range(RB):
                    sp.wait_ge(o_rdy, RB * c + n + 1)
                    load_rows(RB * c + n, rows[n], s_rl[n])
            for t in range(NT // RB * RB, NT):
                sp.wait_ge(o_rdy, t + 1)
                load_rows(t, rows[t % RB], s_rl[t % RB])
            for n in range(RB):
                sp.wait_ge(s_out[n], 16 * len(range(n, NT, RB)))

        S = {name: small[:, k, :] for k, name in enumerate(
            "dt ear th nal tu tr t0 ea tnh sn sh em1 t1 t2 t3 er1 ei den rden gr gi cr ci k1 k2 u32 r32 t32".split())}

        def bc(t, n):
            return t.rearrange("p (h o) -> p h o", o=1).broadcast_to([P, H, n])

        def row(t, n):
            return t.rearrange("p (o b) -> p o b", o=1).broadcast_to([P, H, n])

        @block.gpsimd
        def _(pool):
            g = nc.gpsimd
            pool.sem_inc(o_rdy, RB)
            chain = Chain(pool, s_pool)
            imprecise = dict(allow_small_or_imprecise_dtypes=True)
            chain.after(g.memset(ident[:, :], 0.0))
            chain.after(g.affine_select(out=ident[:, :], in_=ident[:, :], compare_op=ALU.not_equal, fill=1.0, base=0,
                            pattern=[[-1, P]], channel_multiplier=1), s_id)
            chain.after(g.memset(d_add, 0.0))
            chain.after(g.memset(phase_off[0:NM, :], 0.25), s_cst)
            chain.after(g.memset(phase_off[NM:P, :], 0.0), s_cst)
            chain.after(g.iota(bval, [[-1, FB]], base=FB - 1, channel_multiplier=0, **imprecise), s_cst)
            chain.after(g.iota(aval, [[-1, FA]], base=FA - 1, channel_multiplier=0, **imprecise), s_cst)
            chain.after(g.iota(pos, [[P, LB]], base=P - 1, channel_multiplier=-1, **imprecise), s_cst)
            chain.after(g.memset(k_zero, 0.0))
            chain.after(g.iota(iota_e[:, :], [[-1, E]], base=E, channel_multiplier=0, **imprecise), s_cst)
            chain.after(g.iota(iota8, [[1, IDS]], base=0, channel_multiplier=0, **imprecise), s_sort)
            chain.after(g.memset(low, 1.0))
            chain.after(g.affine_select(out=low, in_=low, compare_op=ALU.is_ge, fill=0.0, base=-1, pattern=[[-1, B]],
                            channel_multiplier=1), s_sort)
            chain.after(g.memset(tri8, 1.0))
            chain.after(g.affine_select(out=tri8, in_=tri8, compare_op=ALU.is_ge, fill=0.0, base=-1,
                            pattern=[[1, IDS], [-1, IDS]], channel_multiplier=0), s_sort)
            chain.after(g.iota(slot_v, [[1, TB], [TB, NTD]], base=0, channel_multiplier=0, **imprecise), s_sort)
            chain.after(g.iota(g_iota, [[1, NG]], base=0, channel_multiplier=0, **imprecise), s_sort)
            chain.after(g.iota(quad, [[0, TB], [0, TB], [0, H]], base=1, channel_multiplier=1, **imprecise))
            chain.after(g.affine_select(out=quad, in_=quad, compare_op=ALU.is_equal, fill=0.0, base=0,
                            pattern=[[1, TB], [-1, TB], [0, H]], channel_multiplier=0), s_sort)
            for q in range(TB):
                chain.after(g.iota(h_less[H * q:H * q + H, :], [[0, 1]], base=-H, channel_multiplier=1,
                       **imprecise), s_sort)
                chain.after(g.memset(pad_add[H * q:H * q + H, :], float((B + 1 + q) * H)), s_sort)
            pool.wait_ge(s_t0, 1)
            g.tensor_tensor(v_mag, bc(S["nal"], FB), row(bval, FB), ALU.mult).then_inc(s_mag, 1)
            g.tensor_tensor(a_mag, bc(S["nal"], FA), row(aval, FA), ALU.mult).then_inc(s_mag, 1)
            pool.wait_ge(s_mags, 4)
            pool.wait_ge(s_sin, 4)
            g.tensor_tensor(v_ph, v_ph, v_mag, ALU.mult).then_inc(s_v, 1)
            pool.wait_ge(s_w0l, 16)
            for a in range(4):
                g.tensor_copy(w_rev[:, a, :].rearrange("p (k q) -> p k q", q=P),
                              w_id[:, a, :].rearrange("p (k q) -> p k q", q=P)[:, :, ::-1]).then_inc(s_rev, 1)
            pool.wait_ge(s_arl, 32)
            g.tensor_copy(ar_rev.rearrange("p (k q) -> p k q", q=P),
                          ar_raw.rearrange("p (k q) -> p k q", q=P)[:, :, ::-1]).then_inc(s_rev, 1)
            pool.wait_ge(s_klo, 1)
            chain.after(g.memset(sel32, 0.0))
            sv = sel32.rearrange("k j (e r) -> k j e r", e=2)
            for part in range(2):
                chain.after(g.affine_select(out=sv, in_=sv, compare_op=ALU.not_equal, fill=1.0, base=-E * part,
                                            pattern=[[-2, NP], [-1, 2], [0, R]], channel_multiplier=1))
            chain.after(g.tensor_copy(sel[:, :, :], sel32), s_cst)

            def y_low(h, i):
                pool.wait_ge(y_hi, h + 1)
                g.tensor_tensor(yT[1][:, :, i, :], y32[i % 2][:, :, :], yT[0][:, :, i, :].bitcast(F32),
                                ALU.subtract).then_inc(y_lo, 1)

            def x_bias(h, n, i):
                pool.wait_ge(u_ps, h + 1)
                g.tensor_tensor(xg[n][:, i, :], xg[n][:, i, :], b0_bc[:, :], ALU.add).then_inc(xb_rdy, 1)

            def g_low(gr, j):
                pool.wait_ge(g_hi, NP * gr + j + 1)
                g.tensor_tensor(gT[j % 2][1][:, :], g32[j % 2][:, :], gT[j % 2][0][:, :].bitcast(F32),
                                ALU.subtract).then_inc(g_lo, 1)

            pool.wait_ge(s_db, 32)
            last_row = pool.to_reg(B * H - 1)
            last_group = pool.to_reg(B * NG - 1)
            x1_groups = x1_dram.rearrange("(b i) l -> b (i l)", i=GH)
            for i in range(GH):
                y_low(i, i)
                x_bias(i, 0, i)

            def sorted_rows(gr):
                g.tensor_copy(sort_now[:, :], sort_row[:, bass.ds(gr, 1)]).then_inc(sn_rdy, 1)

            def scatter(gr, n, last):
                pool.wait_ge(x1_rdy, GH * gr + GH + GH)
                pool.wait_ge(sn_rdy, gr + 1)
                if not last:
                    x_bias(GH * gr + 2 * GH - 1, (n + 1) % XB, GH - 1)
                g.indirect_dma_start(x1_groups, bass.IndirectOffsetOnAxis(ap=sort_now[:, 0:1], axis=0),
                                     xg[n][:, :, :].rearrange("p i l -> p (i l)"), None, bounds_check=last_group,
                                     oob_is_err=False).then_inc(x1_st[n], 16)

            def group(gr, n, stores):
                first, last = isinstance(gr, int) and gr == 0, isinstance(gr, int) and gr == NG - 1
                nxt = GH * gr + GH
                if not first:
                    scatter(gr - 1, (n - 1) % XB, False)
                if not last:
                    y_low(nxt, 0)
                g_low(gr, 0)
                g_low(gr, 1)
                for i in range(1, GH):
                    if not last:
                        y_low(nxt + i, i)
                    g_low(gr, i + 1)
                    if i == 1 and not first:
                        pool.wait_ge(x1_st[(n - 1) % XB], 16 * stores)
                        sorted_rows(gr)
                for i in range(GH - 1):
                    if not last:
                        x_bias(nxt + i, (n + 1) % XB, i)
                    g_low(gr, i + 5)
                if first:
                    pool.wait_ge(t_rdy, 1)
                    sorted_rows(gr)

            group(0, 0, 0)
            with pool.Fori(0, (NG - 2) // XB) as t:
                for n in range(XB):
                    group(XB * t + n + 1, (n + 1) % XB, t + 1)
            group(NG - 1, (NG - 1) % XB, (NG - 2) // XB + 1)
            scatter(NG - 1, (NG - 1) % XB, True)
            pool.wait_ge(t_rdy, 5)
            pool.wait_ge(mc_ps, IDS)
            g.memset(hitmax[:, :, :], 0.0).then_inc(s_l1c, 1)
            g.memset(ones[:, :], 1.0).then_inc(s_l1c, 1)
            g.iota(cidx[:, :], [[0, 1]], base=0, channel_multiplier=1, **imprecise).then_inc(s_l1c, 1)
            out_rows = out.rearrange("b h l -> (b h) l")

            def next_row(t, n, stores):
                if not (isinstance(stores, int) and stores == 0):
                    pool.wait_ge(s_out[n], 16 * stores)
                g.tensor_copy(row_now[n][:, :], slot_row[:, bass.ds(t, 1)]).then_inc(row_rdy, 1)

            def finish(t, n, loads):
                pool.wait_ge(ft_sel, t + 1)
                pool.wait_ge(s_rl[n], 16 * loads)
                pool.wait_ge(row_rdy, t + 1)
                g.tensor_tensor(outt[n], dsel[n][:, :], rows[n], ALU.add).then_inc(o_rdy, 1)
                pool.wait_ge(o_rdy, t + RB + 1)
                next_row(t + 1, (n + 1) % RB, loads - 1 + (n + 1) // RB)
                g.indirect_dma_start(out_rows, bass.IndirectOffsetOnAxis(ap=row_now[n][:, 0:1], axis=0),
                                     outt[n], None, bounds_check=last_row, oob_is_err=False
                                     ).then_inc(s_out[n], 16)

            pool.wait_ge(m_ps, LB * IDS)
            next_row(0, 0, 0)
            for t in range(RB):
                finish(t, t, 1)
            with pool.Fori(1, NT // RB) as c:
                for n in range(RB):
                    finish(RB * c + n, n, c + 1)
            for t in range(NT // RB * RB, NT):
                finish(t, t % RB, t // RB + 1)

        @block.scalar
        def _(act):
            a = nc.scalar
            act.wait_ge(s_par, 64)
            a.activation(S["dt"], dt_bc, ACT.Exp).then_inc(s_dt, 1)
            act.wait_ge(s_parT, 1)
            a.activation(S["ear"], par[:, 0, :], ACT.Exp).then_inc(s_dt, 1)
            act.wait_ge(s_t0, 1)
            a.activation(S["ea"], S["nal"], ACT.Exp, scale=-1.0).then_inc(s_mags, 1)
            a.activation(S["tnh"], S["nal"], ACT.Tanh, scale=-0.5).then_inc(s_mags, 1)
            act.wait_ge(s_mag, 2)
            a.activation(v_mag, v_mag, ACT.Exp, scale=-1.0).then_inc(s_mags, 1)
            a.activation(a_mag, a_mag, ACT.Exp, scale=-float(FB)).then_inc(s_mags, 1)
            act.wait_ge(s_t0, 2)
            a.activation(S["sn"], S["t0"], ACT.Sin, scale=TURN).then_inc(s_sin, 1)
            a.activation(S["sh"], S["t0"], ACT.Sin, scale=TURN / 2).then_inc(s_sin, 1)
            act.wait_ge(s_fr, 1)
            a.activation(a_ph, a_ph, ACT.Sin, scale=TURN).then_inc(s_sin, 1)
            act.wait_ge(s_fr, 2)
            a.activation(v_ph, v_ph, ACT.Sin, scale=TURN).then_inc(s_sin, 1)

            for k in range(NWT):
                act.wait_ge(s_wps, k + 1)
                cols = LB * AR if k == NWT - 1 else L
                a.activation(weight_out(k, 0), weight_in_psum(k, cols), ACT.Copy).then_inc(s_whi, 1)

            def layer1_weight_high(k):
                act.wait_ge(s_wps, NWT + k + 1)
                if k == 0:
                    act.wait_ge(s_cst, 7)
                a.activation(weight_out(NWT + k, 0), weight_in_psum(NWT + k, L if k < LB else LB * C), ACT.Copy
                             ).then_inc(s_whi, 1)

            def u_high(h, i, first=False):
                act.wait_ge(u_ps, h + 1)
                if not (first and i < 2):
                    act.wait_ge(y_ps, h - 1)
                a.activation(uT[i % 2][0][:, :, :], wb[0][:, :], ACT.Copy).then_inc(u_hi, 1)

            def y_high(h, i, first=False):
                act.wait_ge(y_ms, h + 1)
                if not first:
                    act.wait_ge(b_done, h - GH + 1)
                a.activation(yT[0][:, :, i, :], y32[i % 2][:, :, :], ACT.Copy).then_inc(y_hi, 1)

            def ar_evac(gr):
                act.wait_ge(ar_ps, gr + 1)
                a.activation(lgT[:, :], wb[0][R:AR, :], ACT.Copy).then_inc(ar_ev, 1)
                a.activation(res[0:R, :], wb[0][0:R, :], ACT.Copy).then_inc(ar_ev, 1)

            def g_high(gr, j):
                act.wait_ge(g_mul, NP * gr + j + 1)
                if j >= 2:
                    act.wait_ge(d_done, (NP - 1) * gr + j - 1)
                a.activation(gT[j % 2][0][:, :], g32[j % 2][:, :], ACT.Copy).then_inc(g_hi, 1)

            u_high(0, 0, True)
            for i in range(GH):
                if i + 1 < GH:
                    u_high(i + 1, i + 1, True)
                y_high(i, i, True)
                layer1_weight_high(i)
            layer1_weight_high(LB)
            ar_evac(0)

            def group(gr, last):
                nxt = GH * gr + GH
                act.wait_ge(r_sub, gr + 1)
                a.activation(rex[:, :, :], rex[:, :, :], ACT.Exp).then_inc(r_exp, 1)
                if not last:
                    u_high(nxt, 0)
                    y_high(nxt, 0)
                    u_high(nxt + 1, 1)
                act.wait_ge(ct_ps, gr + 1)
                a.activation(cTs[:, :], bb[1][0:2 * E, :], ACT.Copy).then_inc(ct_sb, 1)
                g_high(gr, 0)
                g_high(gr, 1)
                for i in range(1, GH):
                    if not last:
                        y_high(nxt + i, i)
                        if i + 1 < GH:
                            u_high(nxt + i + 1, i + 1)
                    g_high(gr, i + 1)
                for j in range(GH + 1, NP):
                    g_high(gr, j)
                if not last:
                    ar_evac(gr + 1)
            with act.Fori(0, NG - 1) as gr:
                group(gr, False)
            group(NG - 1, True)
            def centroids_pair(j):
                for n in range(2):
                    act.wait_ge(ct_mm, 2 * j + n + 1)
                    a.activation(ctb[n][:, :], wb[n][0:C, :], ACT.Copy).then_inc(ct_ev, 1)
                for n in range(2):
                    act.wait_ge(mc_ps, 2 * j + n + 1)
                    a.activation(mc[:, bass.ds(2 * j + n, 1), :, 0:C].rearrange("p e k c -> p (e k) c"),
                                 bb[n][:, 0:LB * C].rearrange("p (k c) -> p k c", k=LB), ACT.Copy).then_inc(mc_hi, 1)

            act.sem_inc(ct_ev, 2)
            act.wait_ge(x1_st[XB - 1], 16 * len(range(XB - 1, NG, XB)))
            act.wait_ge(a_done, GH * NG)
            with act.Fori(0, IDS // 2) as j:
                centroids_pair(j)
            for n in range(XB - 1):
                act.wait_ge(x1_st[n], 16 * len(range(n, NG, XB)))

            def split_high(e, k):
                act.wait_ge(s_cwl[k], 16 * e + 16)
                if isinstance(e, int) and e == 0:
                    act.wait_ge(ct_mm, IDS)
                else:
                    act.wait_ge(m_ps, LB * e + k - 3)
                a.activation(w_sp[0][:, :, P * k:P * k + P], w_id[:, :, P * k:P * k + P], ACT.Copy).then_inc(cw_hi, 1)

            def x_high(t, n, ps, hi):
                act.wait_ge(ps, t + 1)
                a.activation(xts[n][0][:, :, :], wb[n][:, :], ACT.Copy).then_inc(hi, 1)

            def dots_exp(st):
                act.wait_ge(dt_sh, st + 1)
                a.activation(dexp[:, :, :], dots[:, :, :], ACT.Exp, scale=10.0).then_inc(dt_exp, 1)

            def merged_high(e, k):
                act.wait_ge(m_ps, LB * e + k + 1)
                a.activation(mw[0][:, bass.ds(e, 1), k, :].rearrange("p e f -> p (e f)"), acc[k][:, :],
                             ACT.Copy).then_inc(m_hi, 1)

            def fold_step(e, n, first):
                for k in range(LB):
                    x_high(TD * e + k + 1, (n + k + 1) % 2, xd_ps, xd_hi)
                    if k == 0 and not first:
                        dots_exp(e - 1)
                    merged_high(e, k)
                    split_high(e + 1, k)
                x_high(TD * e + TD, (n + 1) % 2, xd_ps, xd_hi)

            for k in range(LB):
                split_high(0, k)
                if k == 0:
                    x_high(0, 0, xd_ps, xd_hi)
            fold_step(0, 0, True)
            with act.Fori(0, IDS // 2 - 1) as t:
                for n in range(2):
                    fold_step(2 * t + n + 1, 1 - n, False)
            e = IDS - 1
            x_high(TD * e + 1, 0, xd_ps, xd_hi)
            dots_exp(e - 1)
            merged_high(e, 0)
            for w in range(2, TD):
                x_high(TD * e + w, (w + 1) % 2, xd_ps, xd_hi)
            dots_exp(e)
            for k in range(1, LB):
                merged_high(e, k)
            x_high(0, 0, xe_ps, xe_hi)
            with act.Fori(0, NT // RB) as c:
                for n in range(RB):
                    x_high(RB * c + n + 1, (n + 1) % 2, xe_ps, xe_hi)
            for t in range(NT // RB * RB + 1, NT):
                x_high(t, t % 2, xe_ps, xe_hi)

        @block.vector
        def _(dve):
            v = nc.vector
            dve.sem_inc(x1_rdy, GH)
            dve.sem_inc(dt_ev, 2)
            dve.sem_inc(mc_ev, 2)
            dve.sem_inc(xd_lo, 2)
            dve.sem_inc(xe_lo, 2)
            dve.sem_inc(ft_ev, RB)
            chain = Chain(dve, s_dve)
            dve.wait_ge(s_par, 64)
            for q in range(2):
                for half in range(2):
                    v.tensor_copy(modes[:, 2 + q, NM * half:NM * half + NM], c_raw[:, :, q]).then_inc(s_stk, 1)
            dve.wait_ge(s_len, 16)
            chain.after(v.tensor_copy(len_f, len_i))
            dve.wait_ge(s_cst, 6)
            for k in range(LB):
                chain.after(v.tensor_scalar(mask[:, k, :], len_f, pos[:, k:k + 1], None, ALU.is_gt))
            dve.wait_ge(s_parP, 1)
            v.tensor_copy(par, bb[0][:, 0:4 * H].rearrange("p (q h) -> p q h", q=4)).then_inc(s_parT, 1)
            dve.wait_ge(s_parT, 1)
            dve.wait_ge(s_dt, 2)

            def tt(o, x0, x1, op):
                chain.after(v.tensor_tensor(S.get(o, o) if isinstance(o, str) else o,
                                            S[x0] if isinstance(x0, str) else x0,
                                            S[x1] if isinstance(x1, str) else x1, op))

            def ts(o, x0, s0, s1, op0, op1):
                chain.after(v.tensor_scalar(S[o] if isinstance(o, str) else o,
                                            S[x0] if isinstance(x0, str) else x0, s0, s1, op0, op1))

            aim = par[:, 1, :]
            v.tensor_tensor(S["nal"], S["ear"], S["dt"], ALU.mult).then_inc(s_t0, 1)
            dve.wait_ge(s_t0, 1)
            tt("th", aim, "dt", ALU.mult)
            ts("tu", "th", 1.0 / (2.0 * math.pi), None, ALU.mult, ALU.bypass)
            ts("tr", "tu", MAGIC, MAGIC, ALU.add, ALU.subtract)
            v.tensor_tensor(S["t0"], S["tu"], S["tr"], ALU.subtract).then_inc(s_t0, 1)
            dve.wait_ge(s_t0, 2)

            ts("u32", "t0", float(FB), None, ALU.mult, ALU.bypass)
            ts("r32", "u32", MAGIC, MAGIC, ALU.add, ALU.subtract)
            tt("t32", "u32", "r32", ALU.subtract)
            chain.after(v.tensor_tensor(a_ph[:, 1, :, :], bc(S["t32"], FA), row(aval, FA), ALU.mult))
            chain.after(v.tensor_scalar(a_ph[:, 0, :, :], a_ph[:, 1, :, :], 0.25, None, ALU.add))
            chain.after(v.tensor_scalar(a_tmp, a_ph, MAGIC, MAGIC, ALU.add, ALU.subtract))
            v.tensor_tensor(a_ph, a_ph, a_tmp, ALU.subtract).then_inc(s_fr, 1)
            chain.after(v.tensor_tensor(v_ph, bc(S["t0"], FB), row(bval, FB), ALU.mult))
            chain.after(v.tensor_scalar(v_ph, v_ph, phase_off[:, 0:1], None, ALU.add))
            dve.wait_ge(s_fr, 1)
            chain.after(v.tensor_scalar(v_tmp, v_ph, MAGIC, MAGIC, ALU.add, ALU.subtract))
            v.tensor_tensor(v_ph, v_ph, v_tmp, ALU.subtract).then_inc(s_fr, 1)
            dve.wait_ge(s_mags, 2)
            chain.after(v.scalar_tensor_tensor(S["em1"], S["ea"], 1.0, S["tnh"], ALU.add, ALU.mult))
            dve.wait_ge(s_sin, 2)
            tt("t1", "sh", "sh", ALU.mult)
            tt("t2", "t1", "ea", ALU.mult)
            chain.after(v.scalar_tensor_tensor(S["er1"], S["t2"], -2.0, S["em1"], ALU.mult, ALU.add))
            tt("ei", "ea", "sn", ALU.mult)
            tt("t1", "ear", "ear", ALU.mult)
            tt("t2", aim, aim, ALU.mult)
            tt("den", "t1", "t2", ALU.add)
            chain.after(v.reciprocal(S["rden"], S["den"]))
            tt("t1", "ei", aim, ALU.mult)
            tt("t2", "er1", "ear", ALU.mult)
            tt("t3", "t1", "t2", ALU.subtract)
            tt("gr", "t3", "rden", ALU.mult)
            tt("t1", "ei", "ear", ALU.mult)
            tt("t2", "er1", aim, ALU.mult)
            tt("t3", "t1", "t2", ALU.add)
            chain.after(v.scalar_tensor_tensor(S["gi"], S["t3"], -1.0, S["rden"], ALU.mult, ALU.mult))
            tt("t1", par[:, 2, :], "gr", ALU.mult)
            tt("t2", par[:, 3, :], "gi", ALU.mult)
            tt("cr", "t1", "t2", ALU.subtract)
            tt("t1", par[:, 2, :], "gi", ALU.mult)
            tt("t2", par[:, 3, :], "gr", ALU.mult)
            tt("ci", "t1", "t2", ALU.add)
            for half, (f1, s1, f2, s2) in enumerate((("cr", 2.0, "ci", -2.0), ("ci", -2.0, "cr", -2.0))):
                rows = slice(NM * half, NM * half + NM)
                ts(S["k1"][rows, :], S[f1][rows, :], s1, None, ALU.mult, ALU.bypass)
                ts(S["k2"][rows, :], S[f2][rows, :], s2, None, ALU.mult, ALU.bypass)
            dve.wait_ge(s_mags, 4)
            dve.wait_ge(s_sin, 3)
            for q in range(2):
                chain.after(v.tensor_tensor(a_ph[:, q, :, :], a_ph[:, q, :, :], a_mag, ALU.mult))
                chain.after(v.tensor_tensor(a_ph[:, q, :, :], a_ph[:, q, :, :], bc(S["k1" if q == 0 else "k2"], FA),
                                            ALU.mult))
            v.tensor_tensor(a_ph[:, 0, :, :], a_ph[:, 0, :, :], a_ph[:, 1, :, :], ALU.add).then_inc(s_uv, 1)
            def weight_low(k, cols):
                dve.wait_ge(s_whi, k + 1)
                v.tensor_tensor(weight_out(k, 1), weight_in_psum(k, cols), weight_out(k, 0).bitcast(F32),
                                ALU.subtract).then_inc(s_wlo, 1)

            for k in range(GH):
                weight_low(k, L)
            dve.wait_ge(s_db, 32)
            dve.wait_ge(s_kps, 1)
            for n in range(2):
                hs = slice(H // 2 * n, H // 2 * n + H // 2)
                chain.after(v.tensor_copy(k32[:, hs, :], bb[n][0:FA, :].rearrange("a (h b) -> a h b", b=FB)))
            chain.after(v.tensor_tensor(k32[:, :, FB - 1], k32[:, :, FB - 1], d_add, ALU.add))
            chain.after(v.tensor_copy(k_split[0], k32))
            v.tensor_tensor(k_split[1], k32, k_split[0].bitcast(F32), ALU.subtract).then_inc(s_klo, 1)
            for k in range(GH, NWT):
                weight_low(k, LB * AR if k == NWT - 1 else L)

            def before(t, of):
                chain.after(v.tensor_tensor(prod88, tri8, of.rearrange("p (o e) -> p o e", o=1)
                                            .broadcast_to([P, IDS, IDS]), ALU.mult))
                chain.after(v.reduce_sum(t, prod88, AX))

            def tile_of(t, of, of_i, extra):
                chain.after(v.tensor_scalar(of_i, of, float(extra), None, ALU.add))
                chain.after(v.tensor_scalar(of_i, of_i, 2, None, ALU.arith_shift_right))
                chain.after(v.tensor_copy(t, of_i))

            def mine(t, of):
                chain.after(v.tensor_tensor(oh_at, of, oh8, ALU.mult))
                chain.after(v.reduce_sum(t, oh_at, AX))

            def sort_ranks():
                dve.wait_ge(s_ids, 32)
                dve.wait_ge(s_sort, 6 + 2 * TB)
                chain.after(v.tensor_copy(ids_r, ids_ri))
                chain.after(v.tensor_copy(ids_c[:, 0:1], ids_ci))
                chain.after(v.tensor_scalar(same, ids_r, ids_c[:, 0:1], None, ALU.is_equal))
                chain.after(v.tensor_tensor(same, same, low, ALU.mult))
                chain.after(v.reduce_sum(rank[:, 0:1], same, AX))

            def sort_one_hot():
                chain.after(v.tensor_scalar(oh8, iota8, ids_c[:, 0:1], None, ALU.is_equal))
                chain.after(v.tensor_tensor(same8, ids_r.rearrange("p (o b) -> p o b", o=1).broadcast_to([P, IDS, B]),
                                            iota8.rearrange("p (e o) -> p e o", o=1).broadcast_to([P, IDS, B]),
                                            ALU.is_equal))

            def sort_starts():
                chain.after(v.reduce_sum(count, same8, AX))
                before(start, count)

            def sort_parts():
                tile_of(lo_tile, start, shift_i, 0)
                chain.after(v.tensor_tensor(hi_tile, start, count, ALU.add))
                tile_of(hi_tile, hi_tile, shift_i, TB - 1)
                chain.after(v.tensor_tensor(hi_tile, hi_tile, lo_tile, ALU.subtract))
                chain.after(v.scalar_tensor_tensor(n_parts, count, 1.0, hi_tile, ALU.min, ALU.mult))
                before(first_part, n_parts)

            def sort_places():
                mine(place[:, 3:4], start)
                chain.after(v.tensor_tensor(place[:, 0:1], place[:, 3:4], rank[:, 0:1], ALU.add))
                tile_of(place[:, 1:2], place[:, 0:1], place_i, 0)
                chain.after(v.tensor_tensor(first_part, first_part, lo_tile, ALU.subtract))
                mine(place[:, 4:5], first_part)
                chain.after(v.scalar_tensor_tensor(place[:, 2:3], place[:, 4:5], float(TB), place[:, 0:1],
                                                   ALU.mult, ALU.add))
                chain.after(v.tensor_scalar(place[:, 5:6], place[:, 0:1], float(NG), None, ALU.mult))
                v.tensor_scalar(sort_row[:, :], g_iota, place[:, 5:6], None, ALU.add).then_inc(t_rdy, 1)

            def sort_slots():
                chain.after(v.scalar_tensor_tensor(place[:, 6:7], place[:, 1:2], -float(TB), place[:, 0:1],
                                                   ALU.mult, ALU.add))
                chain.after(v.tensor_tensor(place[:, 6:7], place[:, 6:7], rank[:, 0:1], ALU.min))
                chain.after(v.tensor_scalar(place[:, 6:7], place[:, 6:7], 0.0, None, ALU.is_equal))
                chain.after(v.tensor_tensor(first_of[:, 0:1], place[:, 6:7], ids_c[:, 0:1], ALU.mult))
                chain.after(v.tensor_tensor(first_of[:, 1:2], place[:, 6:7], place[:, 1:2], ALU.mult))
                v.tensor_scalar(match, slot_v, place[:, 2:3], None, ALU.is_equal).then_inc(t_mat, 1)

            def sort_tables():
                dve.wait_ge(t_tab, 1)
                slot1 = wb[1][:, 0:NTD]
                v.tensor_scalar(slot_off[:, :], slot1, 0.5, 1e30, ALU.is_lt, ALU.mult).then_inc(t_rdy, 1)
                chain.after(v.tensor_scalar(row_f, slot1, float(H), h_less, ALU.mult, ALU.add))
                chain.after(v.tensor_scalar(row_pad, slot1, 0.5, pad_add, ALU.is_lt, ALU.mult))
                v.tensor_tensor(slot_row[:, :], row_f, row_pad, ALU.add).then_inc(t_rdy, 1)
                v.tensor_copy(tile_id[:, :], wb[1][0:1, 64:64 + NTD]).then_inc(t_rdy, 1)
                v.tensor_copy(tile_src[:, :], wb[1][0:1, 128:128 + NTD]).then_inc(t_rdy, 1)

            def u_low(h, i):
                dve.wait_ge(u_hi, h + 1)
                v.tensor_tensor(uT[i % 2][1][:, :, :], wb[0][:, :].rearrange("p (k b) -> p k b", k=LB),
                                uT[i % 2][0][:, :, :].bitcast(F32), ALU.subtract).then_inc(u_lo, 1)

            def y_mask(h, i, first=False):
                dve.wait_ge(y_ps, h + 1)
                if not (first and i < 2):
                    dve.wait_ge(y_lo, h - 1)
                v.tensor_tensor(y32[i % 2][:, :, :], wb[1][:, :].rearrange("p (k b) -> p k b", k=LB),
                                mask[:, :, :], ALU.mult).then_inc(y_ms, 1)

            def gated(gr, j):
                dve.wait_ge(bc_ps, NP * gr + j + 1)
                if j >= 2:
                    dve.wait_ge(g_lo, NP * gr + j - 1)
                v.tensor_tensor(g32[j % 2][:, :], bb[j % 2][:, :], res[:, :], ALU.mult).then_inc(g_mul, 1)

            def routing(gr):
                ch = Chain(dve, s_rt, ROUTE * gr)
                dve.wait_ge(ar_ev, 2 * gr + 2)
                ch.after(v.tensor_copy(res[R:P, :], res[0:R, :]))
                dve.wait_ge(lt_ps, gr + 1)
                lg = bb[0][:, 0:GH * E].rearrange("p (i e) -> p i e", i=GH)

                def over(t, n=E):
                    return t.rearrange("p (i o) -> p i o", o=1).broadcast_to([P, GH, n])

                ch.after(v.reduce_max(rmax[:, :], lg, AX))
                v.tensor_tensor(rex[:, :, :], lg, over(rmax[:, :]), ALU.subtract).then_inc(r_sub, 1)
                dve.wait_ge(r_exp, gr + 1)
                ch.after(v.reduce_sum(rsum[:, :], rex[:, :, :], AX))
                ch.after(v.reciprocal(rinv[:, :], rsum[:, :]))
                ch.after(v.tensor_tensor(rprob[:, :, :], rex[:, :, :], over(rinv[:, :]), ALU.mult))
                marks = iota_e[:, :].rearrange("p (o e) -> p o e", o=1).broadcast_to([P, GH, E])
                for q in range(2):
                    ch.after(v.reduce_max(rtop[:, q, :], rprob[:, :, :], AX))
                    ch.after(v.tensor_tensor(roh[:, :, q, :], rprob[:, :, :], over(rtop[:, q, :]), ALU.is_equal))
                    ch.after(v.tensor_tensor(roh[:, :, q, :], roh[:, :, q, :], marks, ALU.mult))
                    ch.after(v.reduce_max(rmark[:, :], roh[:, :, q, :], AX))
                    ch.after(v.tensor_tensor(roh[:, :, q, :], marks, over(rmark[:, :]), ALU.is_equal))
                    if q == 0:
                        ch.after(v.scalar_tensor_tensor(rprob[:, :, :], roh[:, :, q, :], -2.0, rprob[:, :, :],
                                                        ALU.mult, ALU.add))
                ch.after(v.scalar_tensor_tensor(rden[:, :], rtop[:, 0, :], 1e-6, rtop[:, 1, :], ALU.add, ALU.add))
                ch.after(v.reciprocal(rinv[:, :], rden[:, :]))
                for q in range(2):
                    ch.after(v.scalar_tensor_tensor(rw[:, q, :], rtop[:, q, :], SCALING, rinv[:, :],
                                                    ALU.mult, ALU.mult))
                for q in range(2):
                    ch.after(v.tensor_tensor(roh[:, :, q, :], roh[:, :, q, :], over(rw[:, q, :]), ALU.mult))
                ch.after(v.tensor_tensor(rcomb[:, :, :], roh[:, :, 0, :], roh[:, :, 1, :], ALU.add))
                ch.after(v.tensor_copy(cst[:, :, 0:E].bitcast(F32R), rcomb[:, :, :]))
                v.tensor_tensor(cst[:, :, E:2 * E], rcomb[:, :, :], cst[:, :, 0:E], ALU.subtract).then_inc(c_rdy, 1)
                assert ch.n == ROUTE, ch.n

            u_low(0, 0)
            for i in range(GH):
                if i + 1 < GH:
                    u_low(i + 1, i + 1)
                y_mask(i, i, True)
                weight_low(NWT + i, L)

            def group(gr, n, last, first=False):
                nxt = GH * gr + GH
                routing(gr)
                if not last:
                    u_low(nxt, 0)
                    y_mask(nxt, 0)
                    u_low(nxt + 1, 1)
                gated(gr, 0)
                gated(gr, 1)
                if first:
                    sort_ranks()
                for i in range(1, GH):
                    if not last:
                        y_mask(nxt + i, i)
                        if i + 1 < GH:
                            u_low(nxt + i + 1, i + 1)
                    gated(gr, i + 1)
                    if first:
                        (sort_one_hot, sort_starts, sort_parts)[i - 1]()
                for j in range(GH + 1, NP):
                    gated(gr, j)
                    if first and j > GH + 1:
                        (sort_places, sort_slots)[j - GH - 2]()
                for i in range(GH):
                    dve.wait_ge(a_done, GH * gr + i + 1)
                    dve.wait_ge(xb_rdy, GH * gr + i + 1)
                    v.tensor_tensor(xg[n][:, i, :], acc[i][:, :], xg[n][:, i, :], ALU.add).then_inc(x1_rdy, 1)
                if first:
                    sort_tables()

            group(0, 0, False, True)
            with dve.Fori(0, (NG - 2) // XB) as t:
                for n in range(XB):
                    group(XB * t + n + 1, (n + 1) % XB, False)
            group(NG - 1, (NG - 1) % XB, True)
            with dve.Fori(0, IDS // 2) as j:
                for n in range(2):
                    dve.wait_ge(mc_hi, 2 * j + n + 1)
                    both = mc[:, bass.ds(2 * j + n, 1), :, :].rearrange("p e k c -> p (e k) c")
                    v.tensor_tensor(both[:, :, C:2 * C], bb[n][:, 0:LB * C].rearrange("p (k c) -> p k c", k=LB),
                                    both[:, :, 0:C].bitcast(F32), ALU.subtract).then_inc(mc_ev, 1)

            def split_low(e, k):
                dve.wait_ge(cw_hi, LB * e + k + 1)
                cols = slice(P * k, P * k + P)
                v.tensor_tensor(w_sp[1][:, :, cols], w_id[:, :, cols], w_sp[0][:, :, cols].bitcast(F32),
                                ALU.subtract).then_inc(cw_lo, 1)

            def x_low(t, n, hi, lo):
                dve.wait_ge(hi, t + 1)
                v.tensor_tensor(xts[n][1][:, :, :], wb[n][:, :].rearrange("p (k b) -> p k b", k=LB),
                                xts[n][0][:, :, :].bitcast(F32), ALU.subtract).then_inc(lo, 1)

            def per_tile(t):
                return t.rearrange("p (t o) -> p t o", o=1).broadcast_to([P, TD, C])

            def dots_part(st, part):
                ch = Chain(dve, s_dn, DOTS * st + (0, 0, 1, 3, 5)[part])
                if part == 0:
                    dve.wait_ge(dm_ps, TD * st + TD)
                    halves = [(slice(0, TK), bb[0][:, 0:2 * C * TK].rearrange("p (t m c) -> p t m c", t=TK, m=2)),
                              (slice(TK, TD), bb[1][:, 0:2 * C * (TD - TK)]
                               .rearrange("p (t m c) -> p t m c", t=TD - TK, m=2))]
                    for ts_, h in halves:
                        v.tensor_copy(dots[:, ts_, :], h[:, :, 1, :]).then_inc(dt_half, 1)
                    dve.wait_ge(dt_half, 2 * st + 2)
                    for ts_, h in halves:
                        v.tensor_tensor(dots[:, ts_, :], dots[:, ts_, :], h[:, :, 0, :], ALU.add).then_inc(dt_ev, 1)
                elif part == 1:
                    dve.wait_ge(dt_ev, 2 * st + 4)
                    ch.after(v.reduce_max(dmax[:, :], dots[:, :, :], AX))
                    v.tensor_tensor(dots[:, :, :], dots[:, :, :], per_tile(dmax[:, :]), ALU.subtract
                                    ).then_inc(dt_sh, 1)
                elif part == 2:
                    dve.wait_ge(dt_exp, st + 1)
                    ch.after(v.reduce_sum(dsum[:, :], dexp[:, :, :], AX))
                    ch.after(v.scalar_tensor_tensor(dthr[:, :], dsum[:, :], 0.01, slot_off[:, bass.ds(TD * st, TD)],
                                                    ALU.mult, ALU.add))
                elif part == 3:
                    ch.after(v.tensor_tensor(hits[:, :, :], dexp[:, :, :], per_tile(dthr[:, :]), ALU.is_gt))
                    ch.after(v.reduce_max(query[:, bass.ds(TD * st, TD)], hits[:, :, :], AX))
                else:
                    ch.after(v.tensor_tensor(hitmax[:, :, :], hitmax[:, :, :], hits[:, :, :], ALU.max))

            def merged_low(e, k):
                dve.wait_ge(m_hi, LB * e + k + 1)
                v.tensor_tensor(mw[1][:, bass.ds(e, 1), k, :].rearrange("p e f -> p (e f)"), acc[k][:, :],
                                mw[0][:, bass.ds(e, 1), k, :].rearrange("p e f -> p (e f)").bitcast(F32),
                                ALU.subtract).then_inc(m_lo, 1)

            def fold_step(e, n, first):
                if not first:
                    dots_part(e - 1, 0)
                for k in range(LB):
                    x_low(TD * e + k + 1, (n + k + 1) % 2, xd_hi, xd_lo)
                    if not first:
                        dots_part(e - 1, k + 1)
                    merged_low(e, k)
                    split_low(e + 1, k)
                x_low(TD * e + TD, (n + 1) % 2, xd_hi, xd_lo)

            for k in range(LB):
                split_low(0, k)
                if k == 0:
                    x_low(0, 0, xd_hi, xd_lo)
            dve.wait_ge(s_l1c, 3)
            dve.wait_ge(t_rdy, 5)
            dve.wait_ge(s_asg, 16)
            v.tensor_copy(onehot, onehot.bitcast(I32)).then_inc(cs_rdy, 1)
            dve.wait_ge(cs_rdy, 1)
            v.tensor_scalar(onehot, onehot, cidx[:, 0:1], None, ALU.is_equal).then_inc(cs_rdy, 1)
            fold_step(0, 0, True)
            with dve.Fori(0, IDS // 2 - 1) as t:
                for n in range(2):
                    fold_step(2 * t + n + 1, 1 - n, False)
            e = IDS - 1
            dots_part(e - 1, 0)
            x_low(TD * e + 1, 0, xd_hi, xd_lo)
            dots_part(e - 1, 1)
            merged_low(e, 0)
            for w in range(2, TD):
                x_low(TD * e + w, (w + 1) % 2, xd_hi, xd_lo)
                dots_part(e - 1, w)
            for part in range(3):
                dots_part(e, part)
            merged_low(e, 1)
            dots_part(e, 3)
            dots_part(e, 4)
            ch = Chain(dve, s_dn, DOTS * IDS)
            ch.after(v.reduce_max(hitany[:, :], hitmax[:, :, :].rearrange("p t c -> p c t"), AX))
            merged_low(e, 2)
            merged_low(e, 3)
            dve.wait_ge(cnt_ps, 1)
            v.tensor_scalar(csel[:, :], bb[0][0:C, 0:P], 0.5, None, ALU.is_gt).then_inc(cs_rdy, 1)
            x_low(0, 0, xe_hi, xe_lo)
            dve.wait_ge(rs_ps, 1)
            v.tensor_copy(rowsel[:, :], bb[1][:, :]).then_inc(cs_rdy, 1)
            dve.wait_ge(cs_rdy, 4)
            dve.wait_ge(s_l1l, 16)

            def select(t, n):
                dve.wait_ge(ft_ps, t + 1)
                v.tensor_tensor(dense[n % 2][:, :], db[n][:, :], b1_bc[:, :], ALU.add).then_inc(ft_ev, 1)
                dve.wait_ge(ft_ev, t + RB + 1)
                dve.wait_ge(o_rdy, t + 1)
                v.scalar_tensor_tensor(dsel[n][:, :], dense[n % 2][:, :], query[:, bass.ds(t, 1)],
                                       rowsel[:, :], ALU.mult, ALU.mult).then_inc(ft_sel, 1)

            with dve.Fori(0, NT // RB) as c:
                for n in range(RB):
                    x_low(RB * c + n + 1, (n + 1) % 2, xe_hi, xe_lo)
                    select(RB * c + n, n)
            for t in range(NT // RB * RB, NT):
                if t + 1 < NT:
                    x_low(t + 1, (t + 1) % 2, xe_hi, xe_lo)
                select(t, t % RB)

        @block.tensor
        def _(pe):
            mm = nc.tensor.matmul
            pe.wait_ge(s_id, 1)
            pe.wait_ge(s_stk, 4)
            for q in range(4):
                last = nc.tensor.transpose(bb[0][:, H * q:H * q + H], modes[:, q, :], ident[0:H, 0:H])
            last.then_inc(s_parP, 1)
            def weight(k):
                if k >= GH:
                    pe.wait_ge(s_wlo, k - GH + 1)
                bank = acc[k % GH]
                if k < NP:
                    pe.wait_ge(s_bl, 64)
                    src = [(b_raw[:, a, 2 * k:2 * k + 2, :].rearrange("p e r -> p (e r)"), P * a) for a in range(4)]
                elif k < NP + LB:
                    k0 = k - NP
                    pe.wait_ge(s_rev, 4)
                    src = [(w_rev[:, a, P * k0:P * k0 + P], P * a) for a in range(4)]
                elif k < NWT:
                    pe.wait_ge(s_rev, 5)
                    src = [(ar_rev[:, P * a:P * a + P], AR * a) for a in range(LB)]
                elif k < NWT + LB:
                    a0 = k - NWT
                    pe.wait_ge(s_fwl, 32)
                    src = [(w_id[:, a, P * a0:P * a0 + P], P * a) for a in range(4)]
                else:
                    src = [(cent_raw[:, P * a:P * a + P], C * a) for a in range(LB)]
                for s, at in src:
                    rows, cols = s.shape[0], s.shape[1]
                    last = nc.tensor.transpose(bank[0:cols, at:at + rows], s, ident[0:rows, 0:rows])
                last.then_inc(s_wps, 1)

            for k in range(GH):
                weight(k)
            pe.wait_ge(s_uv, 1)
            pe.wait_ge(s_v, 1)
            pe.wait_ge(s_parT, 1)
            for h in range(H):
                last = mm(bb[h // 16][0:FA, FB * (h % 16):FB * (h % 16) + FB], a_ph[:, 0, h, :], v_ph[:, h, :],
                          start=True, stop=True)
            last.then_inc(s_kps, 1)
            for k in range(GH, NWT):
                weight(k)

            def u_transpose(h, i, n, g2):
                pe.wait_ge(s_x[n][i], 16 * g2)
                for k in range(LB):
                    last = nc.tensor.transpose(wb[0][:, P * k:P * k + P], xg[n][:, i, P * k:P * k + P], ident[:, :])
                last.then_inc(u_ps, 1)

            def y_conv(h, i, loads):
                pe.wait_ge(u_lo, h + 1)
                pe.wait_ge(s_sk[i], 16 * loads)
                for d in range(LB):
                    cols = slice(L - P * (d + 1), L - P * d)
                    for a, b in ((0, 0), (0, 1), (1, 0)):
                        last = mm(wb[1][:, P * d:L], sk[i][:, a, cols],
                                  uT[i % 2][b][:, 0:LB - d, :].rearrange("p k b -> p (k b)"),
                                  start=(d == 0 and a == 0 and b == 0), stop=(d == LB - 1 and a == 1))
                last.then_inc(y_ps, 1)

            def ar_project(gr):
                pe.wait_ge(y_lo, GH * gr + GH)
                steps = [(a, b, k) for a, b in ((0, 0), (1, 0), (0, 1)) for k in range(LB)]
                for a, b, k in steps:
                    last = mm(wb[0][0:AR, :], arw[a][:, k, :], yT[b][:, k, :, :].rearrange("p i b -> p (i b)"),
                              start=(a, b, k) == steps[0], stop=(a, b, k) == steps[-1])
                last.then_inc(ar_ps, 1)

            def logits(gr):
                for i in range(GH):
                    t = nc.tensor.transpose(bb[0][:, E * i:E * i + E], lgT[:, P * i:P * i + P], ident[0:E, 0:E])
                t.then_inc(lt_ps, 1)

            def base(gr, i, with_logits=False):
                pe.wait_ge(x1_rdy, GH * gr + i + 1)
                for a, b in ((0, 0), (0, 1), (1, 0)):
                    for k in range(LB):
                        if with_logits and a == b == 0 and k == LB - 1:
                            pe.wait_ge(ar_ev, 2 * gr + 2)
                        last = mm(acc[i][:, :], yT[a][:, k, i, :], w0[b][:, k, :], start=(a == b == k == 0),
                                  stop=False)
                    if with_logits and a == b == 0:
                        logits(gr)
                last.then_inc(b_done, 1)

            def gates(gr, j):
                if j >= 2:
                    pe.wait_ge(g_mul, NP * gr + j - 1)
                mm(bb[j % 2][:, :], sel[:, j, :], cTs[:, :], start=True, stop=True).then_inc(bc_ps, 1)

            def experts(gr, j):
                pe.wait_ge(g_lo, NP * gr + j + 1)
                for i in range(GH):
                    for a, b in ((0, 0), (0, 1), (1, 0)):
                        last = mm(acc[i][:, :], gT[j % 2][a][:, P * i:P * i + P], bw[b][:, j, :],
                                  start=False, stop=(j == NP - 1 and a == 1))
                    if j == NP - 1:
                        last.then_inc(a_done, 1)
                if j < NP - 1:
                    last.then_inc(d_done, 1)

            u_transpose(0, 0, 0, 1)
            for i in range(GH):
                y_wait = i
                if i + 1 < GH:
                    pe.wait_ge(u_lo, i + 1)
                    u_transpose(i + 1, i + 1, 0, 1)
                if i:
                    pe.wait_ge(y_ms, i)
                y_conv(i, i, 1)
                weight(NWT + i)
            weight(NWT + LB)
            pe.wait_ge(u_lo, GH)
            ar_project(0)
            pe.wait_ge(s_wlo, NWT + LB)
            pe.wait_ge(s_whi, NWT + LB + 1)

            def sort_tables():
                pe.wait_ge(t_mat, 1)
                pe.wait_ge(y_ms, 2 * GH)
                for q in range(TB):
                    mm(wb[1][:, 0:NTD], quad[:, q, :, :].rearrange("p r h -> p (r h)"), match[:, q, :],
                       start=(q == 0), stop=(q == TB - 1))
                for k, at in ((0, 64), (1, 128)):
                    for q in range(TB):
                        last = mm(wb[1][0:1, at:at + NTD], first_of[:, k:k + 1], match[:, q, :],
                                  start=(q == 0), stop=(q == TB - 1))
                last.then_inc(t_tab, 1)

            def group(gr, n, last, loads, first=False):
                nxt, n2 = GH * gr + GH, (n + 1) % XB
                base(gr, 0, with_logits=True)
                base(gr, 1)
                if not last:
                    u_transpose(nxt, 0, n2, loads)
                base(gr, 2)
                if not last:
                    y_conv(nxt, 0, gr + 2)
                    u_transpose(nxt + 1, 1, n2, loads)
                pe.wait_ge(c_rdy, gr + 1)
                for i in range(GH):
                    t = nc.tensor.transpose(bb[1][0:2 * E, P * i:P * i + P], cst[:, i, :], ident[:, :])
                t.then_inc(ct_ps, 1)
                base(gr, 3)
                pe.wait_ge(ct_sb, gr + 1)
                gates(gr, 0)
                gates(gr, 1)
                for i in range(1, GH):
                    if not last:
                        pe.wait_ge(y_ms, nxt + i)
                        y_conv(nxt + i, i, gr + 2)
                        if i + 1 < GH:
                            u_transpose(nxt + i + 1, i + 1, n2, loads)
                    experts(gr, i - 1)
                    gates(gr, i + 1)
                for j in range(GH - 1, NP):
                    experts(gr, j)
                    if j + 2 < NP:
                        gates(gr, j + 2)
                if first:
                    sort_tables()
                if not last:
                    ar_project(gr + 1)

            group(0, 0, False, 1, True)
            pe.wait_ge(t_rdy, 5)
            with pe.Fori(0, (NG - 2) // XB) as t:
                for n in range(XB):
                    group(XB * t + n + 1, (n + 1) % XB, False, t + 1 + (n + 2) // XB)
            group(NG - 1, (NG - 1) % XB, True, 0)

            def centroids_pair(j2, u):
                e = 4 * j2 + 2 * u
                for n in range(2):
                    pe.wait_ge(s_raw[2 * u + n], 16 * j2 + 16)
                    pe.wait_ge(ct_ev, e + n + 1)
                    for o in range(LB):
                        last = mm(wb[n][0:C, :], f_c[:, o, :], raw[2 * u + n][:, o, :], start=(o == 0),
                                  stop=(o == LB - 1))
                    last.then_inc(ct_mm, 1)
                for n in range(2):
                    pe.wait_ge(ct_ev, e + n + 3)
                    pe.wait_ge(mc_ev, e + n + 1)
                    for k in range(LB):
                        last = mm(bb[n][:, C * k:C * k + C], ctb[n][:, P * k:P * k + P], ident[0:C, 0:C],
                                  start=True, stop=True)
                    last.then_inc(mc_ps, 1)

            with pe.Fori(0, IDS // 4) as j2:
                for u in range(2):
                    centroids_pair(j2, u)

            def transpose_rows(src, bank):
                for k in range(LB):
                    last = nc.tensor.transpose(wb[bank][:, P * k:P * k + P], src[:, P * k:P * k + P], ident[:, :])
                return last

            def transpose_next(t, turn, tiles2):
                pe.wait_ge(xd_lo, t + 2)
                pe.wait_ge(s_rd[turn % 2], 16 * (tiles2 + turn // 2 + 1))
                transpose_rows(rows2[turn % 2], turn % 2).then_inc(xd_ps, 1)

            def merge(e, k):
                pe.wait_ge(cw_lo, LB * e + k + 1)
                if isinstance(e, int) and e == 0:
                    pe.wait_ge(x1_rdy, GH * NG + k + 1)
                else:
                    pe.wait_ge(m_lo, LB * e + k - 3)
                steps = [(a, b, o) for a, b in ((0, 0), (0, 1), (1, 0)) for o in range(LB)]
                for s in steps:
                    a, b, o = s
                    m = mm(acc[k][:, :], w_sp[a][:, o, P * k:P * k + P], f_w[b][:, o, :],
                           start=s == steps[0], stop=s == steps[-1])
                m.then_inc(m_ps, 1)

            def dots_tile(e, w, n):
                t = TD * e + w
                pe.wait_ge(xd_lo, t + 3)
                if w == 0:
                    pe.wait_ge(dt_ev, 2 * e + 2)
                ad = pe.value_load(tile_id[0:1, bass.ds(t, 1)], min_val=0, max_val=IDS - 1)
                bank, at = (bb[0], 2 * C * w) if w < TK else (bb[1], 2 * C * (w - TK))
                for a in range(2):
                    cols = 2 * C if a == 0 else C
                    for k in range(LB):
                        m = mm(bank[:, at:at + cols], xts[(TD * n + w) % 2][a][:, k, :],
                               mc[:, bass.ds(ad, 1), k, 0:cols].rearrange("p e f -> p (e f)"),
                               start=(a == k == 0), stop=(a == 1 and k == LB - 1))
                m.then_inc(dm_ps, 1)

            def fold_step(e, n, tiles2):
                for w in range(TD):
                    transpose_next(TD * e + w, TD * n + w + 1, tiles2)
                    if w < LB:
                        merge(e, w)
                    dots_tile(e, w, n)

            pe.wait_ge(s_rd[0], 16)
            transpose_rows(rows2[0], 0).then_inc(xd_ps, 1)
            pe.wait_ge(mc_ev, IDS + 2)
            fold_step(0, 0, 0)
            with pe.Fori(0, IDS // 2 - 1) as t:
                fold_step(2 * t + 1, 1, TD * t)
                fold_step(2 * t + 2, 0, TD * t + TD)
            e = IDS - 1
            for w in range(TD):
                if w < TD - 1:
                    transpose_next(TD * e + w, TD + w + 1, TD * (IDS // 2 - 1))
                if w == 0:
                    merge(e, 0)
                dots_tile(e, w, 1)
            for k in range(1, LB):
                merge(e, k)
            pe.wait_ge(s_dn, DOTS * IDS + 1)
            pe.wait_ge(s_l1c, 3)
            mm(bb[0][0:C, 0:P], hitany[:, :], ones[:, :], start=True, stop=True).then_inc(cnt_ps, 1)
            pe.wait_ge(s_rl[0], 16)
            transpose_rows(rows[0], 0).then_inc(xe_ps, 1)
            pe.wait_ge(cs_rdy, 3)
            mm(bb[1][:, :], csel[:, :], onehot, start=True, stop=True).then_inc(rs_ps, 1)
            pe.wait_ge(m_lo, LB * IDS)
            pe.wait_ge(cs_rdy, 4)
            def dense_tile(t, n, loads):
                if not (isinstance(t, int) and t + 1 == NT):
                    nxt = n + 1
                    pe.wait_ge(xe_lo, t + 2)
                    pe.wait_ge(s_rl[nxt % RB], 16 * (loads + nxt // RB))
                    transpose_rows(rows[nxt % RB], nxt % 2).then_inc(xe_ps, 1)
                pe.wait_ge(xe_lo, t + 3)
                pe.wait_ge(ft_ev, t + 1)
                e = pe.value_load(tile_id[0:1, bass.ds(t, 1)], min_val=0, max_val=IDS - 1)
                steps = [(a, b, k) for a, b in ((0, 0), (0, 1), (1, 0)) for k in range(LB)]
                for s in steps:
                    a, b, k = s
                    m = mm(db[n][:, :], xts[n % 2][a][:, k, :],
                           mw[b][:, bass.ds(e, 1), k, :].rearrange("p e f -> p (e f)"),
                           start=s == steps[0], stop=s == steps[-1])
                m.then_inc(ft_ps, 1)

            with pe.Fori(0, NT // RB) as c:
                for n in range(RB):
                    dense_tile(RB * c + n, n, c + 1)
            for t in range(NT // RB * RB, NT):
                dense_tile(t, t % RB, t // RB + 1)


_INS = ["x", "itok_B_78_3631", "itok_B_3_7", "L0_cond_log_dt", "L0_cond_C", "L0_cond_log_A_real", "L0_cond_A_imag",
        "L0_cond_D", "L0_ffn_base_w", "L0_ffn_base_b", "L0_ffn_A", "L0_ffn_B", "L0_ffn_router_w",
        "L1_cond_weight", "L1_ffn_weight", "L1_ffn_bias", "L1_ffn_centroids", "L1_ffn_assignments"]
_OUTS = [((B, H, L), "float32")]


def kernel(**inputs):
    import numpy as _np
    import concourse.bacc as _bacc
    from concourse import mybir as _mybir
    from concourse.bass_utils import run_bass_kernel_spmd as _run

    nc = _bacc.Bacc("TRN2", target_bir_lowering=False, num_devices=1)
    arrays, args = {}, []
    for name in _INS:
        a = _np.ascontiguousarray(inputs[name])
        arrays[f"in_{name}_dram"] = a
        args.append(nc.dram_tensor(f"in_{name}_dram", a.shape, _mybir.dt.from_np(a.dtype), kind="ExternalInput").ap())
    for i, (shape, dtype) in enumerate(_OUTS):
        dt = _mybir.dt.from_np(_np.dtype(dtype))
        args.append(nc.dram_tensor(f"out_{i}_dram", shape, dt, kind="ExternalOutput").ap())
    build(nc, *args)
    r = _run(nc, [arrays], core_ids=[0])
    got = tuple(r.results[0][f"out_{i}_dram"] for i in range(len(_OUTS)))
    return got[0]
```
